# Optimizing a Trainium2 kernel written in Bass

```python
import numpy as np
import jax
import jax.numpy as jnp

def _softmax(x, axis=-1):
    return jax.nn.softmax(x, axis=axis)

def _gelu(x):
    return jax.nn.gelu(x, approximate=True)

def _silu(x):
    return jax.nn.silu(x)

def _sigmoid(x):
    return jax.nn.sigmoid(x)

def _layernorm(x, axis=-1, eps=1e-05):
    m = jnp.mean(x, axis=axis, keepdims=True)
    v = jnp.var(x, axis=axis, keepdims=True)
    return (x - m) / jnp.sqrt(v + eps)

def _scatter_add(tgt, idx, src, axis=0):
    return tgt.at[idx].add(src)

def _segment_sum(src, seg, n):
    return jax.ops.segment_sum(src, seg, n)
kernel_name = 'mk_flamingo_gated_d1_seqx_r4_fdf62e'

def setup_inputs(seed: int=0):
    np.random.seed(seed)
    _w = jnp.asarray

    def _rec_inputs():
        import jax
        import jax.numpy as jnp
        _rk = jax.random.key(seed)
        x = 7.22e-05 + 1 * jax.random.normal(jax.random.fold_in(_rk, 1), (16, 128, 256), jnp.float32)
        _lenS = 128 - jax.random.randint(jax.random.fold_in(_rk, 7), (16,), 0, max(1, 128 // 4) + 1, jnp.int32)
        _lenS2 = 128 - jax.random.randint(jax.random.fold_in(_rk, 8), (16,), 0, max(1, 128 // 4) + 1, jnp.int32)
        _ctx_1024P = jax.random.normal(jax.random.fold_in(_rk, 11), (16, 16, 256), jnp.float32)
        _ctx_1024c = jax.random.dirichlet(jax.random.fold_in(_rk, 511), 0.3 * jnp.ones((16,), jnp.float32), (16, 128))
        _ctx_1024t = jnp.einsum('bsk,bkd->bsd', _ctx_1024c, _ctx_1024P)
        _ctx_1024t = _ctx_1024t * jax.lax.rsqrt(jnp.mean(jnp.square(_ctx_1024t)) + 1e-12) * 0.953939
        ctx_1024 = 4.13588e-05 + 0.999923 * (_ctx_1024t + 0.3 * jax.random.normal(jax.random.fold_in(_rk, 611), (16, 128, 256), jnp.float32))
        _g = jax.random.normal(jax.random.fold_in(_rk, 9001), (2, 1), jnp.float32)
        _g = jnp.sign(_g) * jnp.maximum(jnp.abs(_g), 1.0) + (_g == 0) * 1.0
        g_xattn = _g[0]
        g_ffn = _g[1]
        return (x, ctx_1024, g_xattn, g_ffn)
    x, ctx_1024, g_xattn, g_ffn = _rec_inputs()

    def _L0_xattn_setup():
        import jax, jax.numpy as jnp
        import numpy as np
        EMBED = 256
        HEADS = 16
        HEAD_DIM = EMBED // HEADS
        WINDOW = 256
        HALF = WINDOW // 2
        SCALE = HEAD_DIM ** (-0.5)
        B, T = (2, 1024)

        def _sliding_window_attn(q, k, v):
            Bq, H, Tq, D = q.shape
            Bk = HALF
            nb = Tq // Bk
            qb = q.reshape(Bq, H, nb, Bk, D)

            def ctx(x):
                xb = x.reshape(Bq, H, nb, Bk, D)
                prev = jnp.concatenate([jnp.zeros_like(xb[:, :, :1]), xb[:, :, :-1]], axis=2)
                return jnp.concatenate([prev, xb], axis=3)
            kc, vc = (ctx(k), ctx(v))
            scores = jnp.einsum('bhnrd,bhncd->bhnrc', qb, kc)
            r = jnp.arange(Bk)[:, None]
            c = jnp.arange(2 * Bk)[None, :]
            band = (c >= r) & (c <= r + Bk)
            b_idx = jnp.arange(nb)[:, None, None]
            valid = band[None] & ((b_idx > 0) | (c[None] >= Bk))
            neg_inf = jnp.finfo(jnp.float32).min
            scores = jnp.where(valid[None, None], scores.astype(jnp.float32), neg_inf)
            attn = jax.nn.softmax(scores, axis=-1).astype(q.dtype)
            out = jnp.einsum('bhnrc,bhncd->bhnrd', attn, vc)
            return out.reshape(Bq, H, Tq, D)
        key = jax.random.key(seed)
        ks = jax.random.split(key, 11)
        f = jnp.float32
        return {'query': jax.random.normal(ks[0], (B, T, EMBED), f), 'key': jax.random.normal(ks[1], (B, T, EMBED), f), 'value': jax.random.normal(ks[2], (B, T, EMBED), f), 'wq': jax.random.normal(ks[3], (EMBED, EMBED), f) * 0.02, 'bq': jax.random.normal(ks[4], (EMBED,), f) * 0.02, 'wk': jax.random.normal(ks[5], (EMBED, EMBED), f) * 0.02, 'bk': jax.random.normal(ks[6], (EMBED,), f) * 0.02, 'wv': jax.random.normal(ks[7], (EMBED, EMBED), f) * 0.02, 'bv': jax.random.normal(ks[8], (EMBED,), f) * 0.02, 'wo': jax.random.normal(ks[9], (EMBED, EMBED), f) * 0.02, 'bo': jax.random.normal(ks[10], (EMBED,), f) * 0.02}
    _L0_xattn_all = _L0_xattn_setup()
    _L0_xattn_in = {k: v for k, v in _L0_xattn_all.items() if k in ('wq', 'bq', 'wk', 'bk', 'wv', 'bv', 'wo', 'bo')}
    del _L0_xattn_all

    def _L0_ffn_setup():
        import math
        import jax, jax.numpy as jnp
        import numpy as np
        D_MODEL = 256
        D_FF = 1024
        E = 8
        K = 2
        CF = 1.25
        CLAMP = 10000.0
        key = jax.random.key(seed)
        k0, k1, k2, k3 = jax.random.split(key, 4)
        B, S = (4, 512)
        x = jax.random.normal(k0, (B, S, D_MODEL), dtype=jnp.float32)
        ln_gamma = jnp.ones((D_MODEL,), jnp.float32)
        ln_beta = jnp.zeros((D_MODEL,), jnp.float32)
        rb = 0.02 * math.sqrt(3.0)
        Wr = jax.random.uniform(k1, (E, D_MODEL), jnp.float32, -rb, rb)
        b12 = math.sqrt(6.0 / (D_MODEL + 2 * D_FF))
        W12 = jax.random.uniform(k2, (E, 2 * D_FF, D_MODEL), jnp.float32, -b12, b12)
        b3 = math.sqrt(6.0 / (D_FF + D_MODEL))
        W3 = jax.random.uniform(k3, (E, D_MODEL, D_FF), jnp.float32, -b3, b3)
        return {'x': x, 'ln_gamma': ln_gamma, 'ln_beta': ln_beta, 'Wr': Wr, 'W12': W12, 'W3': W3}
    _L0_ffn_all = _L0_ffn_setup()
    _L0_ffn_in = {k: v for k, v in _L0_ffn_all.items() if k in ('ln_gamma', 'ln_beta', 'Wr', 'W12', 'W3')}
    del _L0_ffn_all
    return {'x': x, 'ctx_1024': ctx_1024, 'g_xattn': g_xattn, 'g_ffn': g_ffn, 'L0_xattn_wq': _L0_xattn_in['wq'], 'L0_xattn_bq': _L0_xattn_in['bq'], 'L0_xattn_wk': _L0_xattn_in['wk'], 'L0_xattn_bk': _L0_xattn_in['bk'], 'L0_xattn_wv': _L0_xattn_in['wv'], 'L0_xattn_bv': _L0_xattn_in['bv'], 'L0_xattn_wo': _L0_xattn_in['wo'], 'L0_xattn_bo': _L0_xattn_in['bo'], 'L0_ffn_ln_gamma': _L0_ffn_in['ln_gamma'], 'L0_ffn_ln_beta': _L0_ffn_in['ln_beta'], 'L0_ffn_Wr': _L0_ffn_in['Wr'], 'L0_ffn_W12': _L0_ffn_in['W12'], 'L0_ffn_W3': _L0_ffn_in['W3']}

def reference(x, ctx_1024, g_xattn, g_ffn, L0_xattn_wq, L0_xattn_bq, L0_xattn_wk, L0_xattn_bk, L0_xattn_wv, L0_xattn_bv, L0_xattn_wo, L0_xattn_bo, L0_ffn_ln_gamma, L0_ffn_ln_beta, L0_ffn_Wr, L0_ffn_W12, L0_ffn_W3):
    import jax
    import jax.numpy as jnp

    def _L0_xattn_ref(query, key, value, wq, bq, wk, bk, wv, bv, wo, bo):
        import jax, jax.numpy as jnp
        import numpy as np
        EMBED = 256
        HEADS = 16
        HEAD_DIM = EMBED // HEADS
        WINDOW = 256
        HALF = WINDOW // 2
        SCALE = HEAD_DIM ** (-0.5)
        B, T = (2, 1024)

        def _sliding_window_attn(q, k, v):
            Bq, H, Tq, D = q.shape
            Bk = HALF
            nb = Tq // Bk
            qb = q.reshape(Bq, H, nb, Bk, D)

            def ctx(x):
                xb = x.reshape(Bq, H, nb, Bk, D)
                prev = jnp.concatenate([jnp.zeros_like(xb[:, :, :1]), xb[:, :, :-1]], axis=2)
                return jnp.concatenate([prev, xb], axis=3)
            kc, vc = (ctx(k), ctx(v))
            scores = jnp.einsum('bhnrd,bhncd->bhnrc', qb, kc)
            r = jnp.arange(Bk)[:, None]
            c = jnp.arange(2 * Bk)[None, :]
            band = (c >= r) & (c <= r + Bk)
            b_idx = jnp.arange(nb)[:, None, None]
            valid = band[None] & ((b_idx > 0) | (c[None] >= Bk))
            neg_inf = jnp.finfo(jnp.float32).min
            scores = jnp.where(valid[None, None], scores.astype(jnp.float32), neg_inf)
            attn = jax.nn.softmax(scores, axis=-1).astype(q.dtype)
            out = jnp.einsum('bhnrc,bhncd->bhnrd', attn, vc)
            return out.reshape(Bq, H, Tq, D)
        Bq, Tq, C = query.shape
        split = lambda x: x.reshape(Bq, Tq, HEADS, HEAD_DIM).transpose(0, 2, 1, 3)
        q = split(jnp.einsum('btc,oc->bto', query, wq) + bq) * SCALE
        k = split(jnp.einsum('btc,oc->bto', key, wk) + bk)
        v = split(jnp.einsum('btc,oc->bto', value, wv) + bv)
        o = _sliding_window_attn(q, k, v)
        o = o.transpose(0, 2, 1, 3).reshape(Bq, Tq, C)
        return jnp.einsum('btc,oc->bto', o, wo) + bo

    def _L0_ffn_ref(x, ln_gamma, ln_beta, Wr, W12, W3):
        import math
        import jax, jax.numpy as jnp
        import numpy as np
        D_MODEL = 256
        D_FF = 1024
        E = 8
        K = 2
        CF = 1.25
        CLAMP = 10000.0
        B, S, D = x.shape
        T = B * S
        xf = x.reshape(T, D)
        mu = xf.mean(-1, keepdims=True)
        var = ((xf - mu) ** 2).mean(-1, keepdims=True)
        xn = (xf - mu) / jnp.sqrt(var + 1e-05) * ln_gamma + ln_beta
        logits = jnp.clip(xn @ Wr.T, -CLAMP, CLAMP)
        m = logits.max(-1, keepdims=True)
        ex = jnp.exp(logits - m)
        probs = ex / (ex.sum(-1, keepdims=True) + 1e-12)
        top_p, top_i = jax.lax.top_k(probs, K)
        Sslots = T * K
        experts = top_i.reshape(-1)
        weights = top_p.reshape(-1)
        tokens = jnp.repeat(jnp.arange(T, dtype=jnp.int32), K)
        order = jnp.argsort(experts, stable=True)
        e_s = experts[order]
        w_s = weights[order]
        t_s = tokens[order]
        counts = jnp.bincount(e_s, length=E)
        offsets = jnp.concatenate([jnp.zeros((1,), counts.dtype), jnp.cumsum(counts)])
        rank = jnp.arange(Sslots, dtype=counts.dtype) - offsets[e_s]
        cap = max(1, math.ceil(math.ceil(T * K * CF) / E))
        kept = rank < cap
        pos = jnp.where(kept, rank, cap)
        buf = jnp.zeros((E, cap, D), x.dtype).at[e_s, pos].set(xn[t_s], mode='drop')
        gu = jnp.einsum('ecd,efd->ecf', buf, W12)
        g, u = (gu[..., :D_FF], gu[..., D_FF:])
        h = jax.nn.silu(g) * u
        y = jnp.einsum('ecf,edf->ecd', h, W3)
        y_slot = y[e_s, jnp.minimum(pos, cap - 1)] * (w_s * kept.astype(x.dtype))[:, None]
        out = jnp.zeros((T, D), x.dtype).at[t_s].add(y_slot)
        return out.reshape(B, S, D)
    x = x + jnp.tanh(g_xattn[0]) * _L0_xattn_ref(_layernorm(x, axis=-1), ctx_1024, ctx_1024, L0_xattn_wq, L0_xattn_bq, L0_xattn_wk, L0_xattn_bk, L0_xattn_wv, L0_xattn_bv, L0_xattn_wo, L0_xattn_bo)
    x = x + jnp.tanh(g_ffn[0]) * _L0_ffn_ref(_layernorm(x, axis=-1), L0_ffn_ln_gamma, L0_ffn_ln_beta, L0_ffn_Wr, L0_ffn_W12, L0_ffn_W3)
    return x

_drawn_inputs = setup_inputs


def setup_inputs(seed=0):
    import zlib

    import numpy as np

    out = dict(_drawn_inputs(seed))
    spreads = {'L0_ffn_ln_gamma': (1.0, 0.6), 'L0_ffn_ln_beta': (0.0, 0.687)}
    factors = {'L0_xattn_wq': 8.0,
     'L0_xattn_bq': 42.179,
     'L0_xattn_wk': 8.0,
     'L0_xattn_bk': 64.0,
     'L0_xattn_bv': 8.0,
     'L0_xattn_bo': 3.546}
    for name, (base, spread) in spreads.items():
        noise = np.random.default_rng([zlib.crc32(name.encode()), seed]).standard_normal(out[name].shape)
        drawn = base * np.exp(spread * noise) if base else spread * noise
        out[name] = jnp.asarray(drawn.astype(out[name].dtype))
    for name, factor in factors.items():
        out[name] = (out[name] * factor).astype(out[name].dtype)
    return out
```

```python
from contextlib import ExitStack

import concourse.bass as bass
from concourse import mybir

F32 = mybir.dt.float32
F32R = mybir.dt.float32r
BF16 = mybir.dt.bfloat16
F16 = mybir.dt.float16
I32 = mybir.dt.int32
U32 = mybir.dt.uint32
ALU = mybir.AluOpType
ACT = mybir.ActivationFunctionType
AX_X = mybir.AxisListType.X

P = 128
SEQS, T, D = 16, 128, 256
H, HD = 16, 16
DC = D // P
SB = 4
NSB = SEQS // SB
GH = 4
GPS = H // GH
NG = SB * GPS
E, K, FF = 8, 2, 1024
TOKENS = SEQS * T
CAP = -(-(-(-TOKENS * K * 5 // 4)) // E)
CT = CAP // P
ROW = D + E + 1
CHUNKS = ((0, 384), (384, 256))
FT = FF // P
UNIT = 2048
NU = 3
VW = 3 * HD + 2
NEG = -3.0e38
PSCALE = 9.704060527839234
EPS = 1e-5
CLAMP = 10000.0
LATE = 1.0e6


def gated_block(nc, x, ctxT, g_xattn, g_ffn, wqT, bq, wkT, bk, wvT, bv, woT, bo, gamma, beta, wrT, w12T, w3T, out):
    with ExitStack() as top:
        def sem(name):
            return top.enter_context(nc.semaphore(name))

        def sb(stack, name, shape, dt):
            return stack.enter_context(nc.sbuf_tensor(name, shape, dt))

        buf = nc.dram_tensor("expert_rows", (E * CAP, ROW), F32).ap()

        ident32 = sb(top, "ident32", [P, P], F32)
        stage = [sb(top, f"stage{i}", [P, UNIT], F32) for i in range(2)]
        wh0 = sb(top, "wh0", [P, NU, UNIT], F32R)
        wl0 = sb(top, "wl0", [P, NU, UNIT], F32R)
        rows = [sb(top, f"rows{i}", [P, CT, ROW], F32) for i in range(2)]

        pa = ExitStack()
        x_all = sb(pa, "x_all", [P, SEQS * D], F32)
        st_all = sb(pa, "st_all", [P, SEQS, 6], F32)
        mv_all = sb(pa, "mv_all", [P, SEQS, 2], F32)
        rs_all = sb(pa, "rs_all", [P, SEQS], F32)
        ve_all = sb(pa, "ve_all", [P, SEQS], F32)
        mean1 = sb(pa, "mean1", [P, SB], F32)
        rstd1 = sb(pa, "rstd1", [P, SB], F32)
        xn1 = sb(pa, "xn1", [P, SB, D], F32)
        cT = sb(pa, "cT", [P, DC, SB * T], F32)
        xT = sb(pa, "xT", [P, DC, SB * T], F32)
        qT = sb(pa, "qT", [P, DC, SB * T], F32)
        kT = sb(pa, "kT", [P, DC, SB * T], F32)
        kM = sb(pa, "kM", [P, H, SB * T], F32)
        vf = sb(pa, "vf", [P, SB, D], F32)
        vr = vf
        V3 = sb(pa, "V3", [P, SB, H, VW], BF16)
        nm = [sb(pa, f"nm{i}", [P, GH], F32) for i in range(2)]
        sS = [sb(pa, f"sS{i}", [P, GH, T], F32) for i in range(2)]
        p32 = [sb(pa, f"p32_{i}", [P, GH, T], F32) for i in range(2)]
        pp = [sb(pa, f"pp{i}", [P, GH, 2, T], F16) for i in range(4)]
        pT = [sb(pa, f"pT{i}", [P, GH, 2, T], F16) for i in range(2)]
        osum = sb(pa, "osum", [P, 8, HD], F32)
        orec = sb(pa, "orec", [P, 8], F32)
        oN = sb(pa, "oN", [P, D], F32)
        oT = sb(pa, "oT", [P, DC, T], F32)
        xbo = sb(pa, "xbo", [P, SB, D], F32)
        wq = sb(pa, "wq", [P, DC, D], F32)
        wk = sb(pa, "wk", [P, DC, D], F32)
        wv = sb(pa, "wv", [P, DC, D], F32)
        wo = sb(pa, "wo", [P, DC, D], F32)
        wr = sb(pa, "wr", [P, DC, E], F32)
        bqk = sb(pa, "bqk", [P, 2, DC], F32)
        bq4 = sb(pa, "bq4", [P, DC], F32)
        bvb = sb(pa, "bvb", [P, D], F32)
        bob = sb(pa, "bob", [P, D], F32)
        tbo = sb(pa, "tbo", [P, D], F32)
        gab = sb(pa, "gab", [P, D], F32)
        beb = sb(pa, "beb", [P, D], F32)
        gate = sb(pa, "gate", [P, 2], F32)
        tg = sb(pa, "tg", [P, 2], F32)
        ident16 = sb(pa, "ident16", [P, P], F16)
        identb = sb(pa, "identb", [P, P], BF16)
        causal = sb(pa, "causal", [P, GH, T], BF16)
        before = sb(pa, "before", [P, P], BF16)
        onesb = sb(pa, "onesb", [P, P], BF16)
        hmask = sb(pa, "hmask", [P, 8], F32)
        iota_i = sb(pa, "iota_i", [P, 2, E], I32)
        iota8 = sb(pa, "iota8", [P, E], F32)
        ebase = sb(pa, "ebase", [P, E], F32)
        tokid = sb(pa, "tokid", [P, SEQS], I32)
        padrow = sb(pa, "padrow", [P, ROW], F32)
        zrow = sb(pa, "zrow", [P, D], F32)
        mhalf = sb(pa, "mhalf", [P, SEQS], F32)
        pbias = sb(pa, "pbias", [P, 1], F32)
        xr = sb(pa, "xr", [P, SB, ROW], F32)
        xnT = xT
        st2 = sb(pa, "st2", [P, SB, 6], F32)
        mv2 = sb(pa, "mv2", [P, SB, 2], F32)
        lnt = [sb(pa, f"lnt{i}", [P, SB], F32) for i in range(7)]
        lgc = sb(pa, "lgc", [P, SB, E], F32)
        lgs = sb(pa, "lgs", [P, SB, E], F32)
        lmx = sb(pa, "lmx", [P, SB], F32)
        lex = sb(pa, "lex", [P, SB, E], F32)
        lsm = sb(pa, "lsm", [P, SB], F32)
        lse = sb(pa, "lse", [P, SB], F32)
        lrc = sb(pa, "lrc", [P, SB], F32)
        prob = sb(pa, "prob", [P, SB, E], F32)
        top8 = sb(pa, "top8", [P, SB, 8], F32)
        topi = sb(pa, "topi", [P, SB, 8], U32)
        ixf = sb(pa, "ixf", [P, K, SB], F32)
        pick = sb(pa, "pick", [P, K, SB, E], F32)
        member = sb(pa, "member", [P, SB, E], BF16)
        seen = sb(pa, "seen", [P, E], BF16)
        seen_add = sb(pa, "seen_add", [P, E], F32)
        late = sb(pa, "late", [P, SB, E], F32)
        slot0 = sb(pa, "slot0", [P, SB, E], F32)
        slot = sb(pa, "slot", [P, SB, E], F32)
        pslot = sb(pa, "pslot", [P, K, SB, E], F32)
        slotf = sb(pa, "slotf", [P, K, SB], F32)
        slotu = sb(pa, "slotu", [P, K * SB], U32)
        pa.close()

        pc = top
        wh1 = sb(pc, "wh1", [P, NU, UNIT], F32R)
        wl1 = sb(pc, "wl1", [P, NU, UNIT], F32R)
        bXh = sb(pc, "bXh", [P, DC, CAP], F32R)
        bXl = sb(pc, "bXl", [P, DC, CAP], F32R)
        hH = [sb(pc, f"hH{c}", [P, FT, w], F32R) for c, (_, w) in enumerate(CHUNKS)]
        hL = [sb(pc, f"hL{c}", [P, FT, w], F32R) for c, (_, w) in enumerate(CHUNKS)]
        sil = [sb(pc, f"sil{i}", [P, 384], F32) for i in range(2)]
        hF = [sb(pc, f"hF{i}", [P, 384], F32) for i in range(2)]
        ysc = [sb(pc, f"ysc{i}", [P, D], F32) for i in range(2)]
        Wh, Wl = [wh0, wh1], [wl0, wl1]

        bank = [top.enter_context(nc.psum_tensor(f"bank{i}", [P, 512], F32)) for i in range(8)]
        S, Tb, O, X = bank[0:2], bank[2:4], bank[4:6], bank[6:8]
        Gb, Ub, Yb, Xc = bank[0:2], bank[2:4], bank[4:6], bank[6:8]

        ld_x = [sem(f"ld_x{i}") for i in range(NSB)]
        ld_ctx, ld_w, ld_c = sem("ld_ctx"), sem("ld_w"), sem("ld_c")
        ld_pad, st_x2 = sem("ld_pad"), sem("st_x2")
        ld_st = [sem(f"ld_st{i}") for i in range(2)]
        ld_rows = [sem(f"ld_rows{i}") for i in range(2)]
        const_mem, const_ok, pool_chain = sem("const_mem"), sem("const_ok"), sem("pool_chain")
        gates_ok, pool_ln1, pool_st1, pool_xbo = sem("gates_ok"), sem("pool_ln1"), sem("pool_st1"), sem("pool_xbo")
        dve_st, dve_mv1, dve_xn1 = sem("dve_st"), sem("dve_mv1"), sem("dve_xn1")
        pe_xT, act_xT, pe_q, act_q, pe_k, act_k = (sem(n) for n in ("pe_xT", "act_xT", "pe_q", "act_q", "pe_k", "act_k"))
        dve_km, pool_km = sem("dve_km"), sem("pool_km")
        pe_v, dve_vf, pool_v1, dve_vr, pool_v2, dve_v3 = (sem(n) for n in ("pe_v", "dve_vf", "pool_v1", "dve_vr", "pool_v2", "dve_v3"))
        pe_s, dve_max, dve_sub, act_exp, pool_hi, dve_lo = (sem(n) for n in ("pe_s", "dve_max", "dve_sub", "act_exp", "pool_hi", "dve_lo"))
        pe_t, act_pt, pe_pv, dve_os, dve_rec, dve_on = (sem(n) for n in ("pe_t", "act_pt", "pe_pv", "dve_os", "dve_rec", "dve_on"))
        pe_oT, act_oT, pe_y, dve_x2 = (sem(n) for n in ("pe_oT", "act_oT", "pe_y", "dve_x2"))
        dve_st2, dve_mv2, pool_rs2, dve_xc, pool_xg, pool_xr = (sem(n) for n in ("dve_st2", "dve_mv2", "pool_rs2", "dve_xc", "pool_xg", "pool_xr"))
        pe_x2T, act_x2T, pe_lg, dve_lg, dve_r, act_ex = (sem(n) for n in ("pe_x2T", "act_x2T", "pe_lg", "dve_lg", "dve_r", "act_ex"))
        dve_lgs, dve_mem, dve_wp, pe_rk, dve_rk, dve_idx = (sem(n) for n in ("dve_lgs", "dve_mem", "dve_wp", "pe_rk", "dve_rk", "dve_idx"))
        scattered = sem("scattered")
        act_wh, dve_wl = sem("act_wh"), sem("dve_wl")
        pe_bT, act_bh, dve_bl = sem("pe_bT"), sem("act_bh"), sem("dve_bl")
        pe_gu, act_sil, dve_h, act_hh, dve_hl = (sem(n) for n in ("pe_gu", "act_sil", "dve_h", "act_hh", "dve_hl"))
        dve_passed, pool_passed = sem("dve_passed"), sem("pool_passed")
        pe_out, dve_ysc, added = sem("pe_out"), sem("dve_ysc"), sem("added")

        xrows = x.rearrange("(i p) d -> p i d", p=P)
        xv = x_all[:, :].rearrange("p (i d) -> p i d", d=D)
        R_CHAIN = 9
        PIECES = 12
        QW = UNIT // 4

        def x_tile(i):
            return x_all[:, bass.ds(i * D, D)]

        block = top.enter_context(nc.Block())

        @block.sync
        def _(sp):
            for s in range(NSB):
                sp.dma_start(xv[:, SB * s:SB * s + SB, :], xrows[:, SB * s:SB * s + SB, :]).then_inc(ld_x[s], 16)
                if s == 0:
                    sp.dma_start(wq[:, :, :], wqT.rearrange("(c p) o -> p c o", p=P)).then_inc(ld_w, 16)

            def load_ctx(n):
                sp.dma_start(cT[:, :, :], ctxT[:, bass.ds(n * SB * T, SB * T)].rearrange("(c p) t -> p c t", p=P))\
                  .then_inc(ld_ctx, 16)

            def load_stage(u, src):
                sp.dma_start(stage[u % 2][:, :], src).then_inc(ld_st[u % 2], 16)

            load_ctx(0)
            for dst, src in ((wk, wkT), (wv, wvT), (wo, woT)):
                sp.dma_start(dst[:, :, :], src.rearrange("(c p) o -> p c o", p=P)).then_inc(ld_w, 16)
            sp.dma_start(wr[:, :, :], wrT.rearrange("(c p) e -> p c e", p=P)).then_inc(ld_w, 16)
            sp.wait_ge(const_ok, 1)
            sp.dma_start(buf.rearrange("(j p) w -> p j w", p=P),
                         padrow[:, :].unsqueeze(1).to_broadcast([P, E * CT, ROW])).then_inc(ld_pad, 16)
            sp.dma_start(out[TOKENS:TOKENS + P, :], zrow[:, :]).then_inc(ld_pad, 16)
            load_stage(0, w12T[0, 0:P, :])
            load_stage(1, w12T[0, P:2 * P, :])

            def store_x2(n):
                sp.wait_ge(dve_x2, SB * n + SB)
                sp.dma_start(out[0:TOKENS, :].rearrange("(i p) d -> p i d", p=P)[:, bass.ds(n * SB, SB), :],
                             x_all[:, bass.ds(n * SB * D, SB * D)].rearrange("p (i d) -> p i d", d=D)).then_inc(st_x2, 16)

            def turn(n):
                sp.wait_ge(pe_v, 2 * n)
                load_ctx(n)
                store_x2(n - 1)

            with sp.Fori(1, NSB) as n:
                turn(n)
            store_x2(NSB - 1)

            def w3_piece(e):
                return w3T[e].rearrange("(f p) d -> p f d", p=P)

            def load_rows(e, par):
                sp.dma_start(rows[par][:, :, :], buf[bass.ds(e * CAP, CAP), :].rearrange("(c p) w -> p c w", p=P))\
                  .then_inc(ld_rows[par], 16)

            def load_weights(e, first_piece, base_u, par_u):
                for k in range(first_piece, NU):
                    u = base_u + k
                    s = (par_u + k) % 2
                    sp.wait_ge(act_wh, 4 * (u - 1))
                    sp.wait_ge(dve_wl, 4 * (u - 1))
                    if k < DC:
                        sp.dma_start(stage[s][:, :], w12T[e, k * P:(k + 1) * P, :] if isinstance(e, int)
                                     else w12T[bass.ds(e, 1), k * P:(k + 1) * P, :].rearrange("a p f -> p (a f)"))\
                          .then_inc(ld_st[s], 16)
                    else:
                        sp.dma_start(stage[s][:, :].rearrange("p (f d) -> p f d", d=D),
                                     w3_piece(e) if isinstance(e, int)
                                     else w3T[bass.ds(e, 1), :, :].rearrange("a (f p) d -> p (a f) d", p=P))\
                          .then_inc(ld_st[s], 16)

            load_weights(0, 2, 0, 0)
            sp.wait_ge(scattered, 16 * K * SEQS)
            load_rows(0, 0)

            def fetch(e, par):
                if not (isinstance(e, int) and e < 2):
                    sp.wait_ge(added, 16 * CT * (e - 1))
                load_rows(e, par)
                load_weights(e, 0, NU * e, par)

            fetch(1, 1)
            with sp.Fori(1, E // 2) as i:
                fetch(2 * i, 0)
                fetch(2 * i + 1, 1)

        @block.gpsimd
        def _(pool):
            chained = [0]

            def then(ins):
                chained[0] += 1
                ins.then_inc(pool_chain, 1)
                pool.wait_ge(pool_chain, chained[0])

            pool.memset(padrow[:, :], 0.0).then_inc(const_mem, 1)
            pool.memset(zrow[:, :], 0.0).then_inc(const_mem, 1)
            pool.wait_ge(const_mem, 2)
            pool.iota(padrow[:, D + E:ROW].bitcast(I32), pattern=[[1, 1]], base=TOKENS, channel_multiplier=1).then_inc(const_ok, 1)
            pool.memset(ident32[:, :], 0.0).then_inc(const_mem, 1)
            pool.memset(ident16[:, :], 0.0).then_inc(const_mem, 1)
            pool.memset(identb[:, :], 0.0).then_inc(const_mem, 1)
            pool.memset(causal[:, :, :], 0.0).then_inc(const_mem, 1)
            pool.memset(before[:, :], 1.0).then_inc(const_mem, 1)
            pool.memset(hmask[:, :], 1.0).then_inc(const_mem, 1)
            pool.wait_ge(const_mem, 8)
            for m in (ident32, ident16, identb):
                pool.affine_select(out=m[:, :], in_=m[:, :], compare_op=ALU.not_equal, fill=1.0, base=0,
                                   pattern=[[-1, P]], channel_multiplier=1).then_inc(const_ok, 1)
            pool.affine_select(out=causal[:, :, :], in_=causal[:, :, :], compare_op=ALU.is_ge, fill=NEG, base=0,
                               pattern=[[0, GH], [-1, T]], channel_multiplier=1).then_inc(const_ok, 1)
            pool.affine_select(out=before[:, :], in_=before[:, :], compare_op=ALU.is_ge, fill=0.0, base=-1,
                               pattern=[[1, P]], channel_multiplier=-1).then_inc(const_ok, 1)
            then(pool.affine_select(out=hmask[:, :], in_=hmask[:, :], compare_op=ALU.is_ge, fill=0.0, base=0,
                                    pattern=[[-HD, 8]], channel_multiplier=1))
            pool.affine_select(out=hmask[:, :], in_=hmask[:, :], compare_op=ALU.is_ge, fill=0.0, base=HD - 1,
                               pattern=[[HD, 8]], channel_multiplier=-1).then_inc(const_ok, 1)
            pool.memset(onesb[:, :], 1.0).then_inc(const_ok, 1)
            pool.memset(seen[:, :], 0.0).then_inc(const_ok, 1)
            pool.memset(pbias[:, :], PSCALE).then_inc(const_ok, 1)
            pool.memset(V3[:, :, :, 3 * HD:3 * HD + 1], 1.0).then_inc(const_ok, 1)
            pool.memset(V3[:, :, :, 3 * HD + 1:VW], 0.0).then_inc(const_ok, 1)
            pool.iota(tokid[:, :], pattern=[[P, SEQS]], base=0, channel_multiplier=1).then_inc(const_ok, 1)
            pool.iota(iota_i[:, 0, :], pattern=[[1, E]], base=0, channel_multiplier=0).then_inc(const_mem, 1)
            pool.iota(iota_i[:, 1, :], pattern=[[CAP, E]], base=0, channel_multiplier=0).then_inc(const_mem, 1)
            pool.wait_ge(const_mem, 10)
            pool.tensor_copy(iota8[:, :], iota_i[:, 0, :]).then_inc(const_ok, 1)
            pool.tensor_copy(ebase[:, :], iota_i[:, 1, :]).then_inc(const_ok, 1)
            then(pool.memset(mhalf[:, :], -0.5))
            pool.wait_ge(dve_mv1, SEQS)
            then(pool.tensor_scalar(ve_all[:, :], mv_all[:, :, 1], EPS, None, ALU.add))
            pool.tensor_tensor(rs_all[:, :], ve_all[:, :], mhalf[:, :], ALU.pow).then_inc(pool_ln1, 1)
            pool.wait_ge(pool_ln1, 1)
            pool.wait_ge(ld_c, 16 * 8)
            pool.tensor_scalar(bq4[:, :], bqk[:, 0, :], HD ** -0.5, None, ALU.mult).then_inc(const_ok, 1)
            pool.wait_ge(gates_ok, 1)
            then(pool.tensor_scalar(tbo[:, :], bob[:, :], tg[:, 0:1], None, ALU.mult))

            def prepare(n, first):
                if not first:
                    pool.wait_ge(dve_xn1, SB * n).then_inc(pool_passed, 1)
                pool.tensor_copy(mean1[:, :], mv_all[:, bass.ds(n * SB, SB), 0]).then_inc(pool_st1, 1)
                pool.tensor_copy(rstd1[:, :], rs_all[:, bass.ds(n * SB, SB)]).then_inc(pool_st1, 1)

            def head_keys(n, first):
                if not first:
                    pool.wait_ge(pe_s, NG * n).then_inc(pool_passed, 1)
                pool.wait_ge(act_k, DC * n + 2).then_inc(pool_passed, 1)
                for h in range(8, H):
                    pool.tensor_scalar(kM[:, h, :], kT[:, h // 8, :], hmask[:, h % 8:h % 8 + 1], None, ALU.mult)\
                        .then_inc(pool_km, 1)

            def values(n, first):
                if not first:
                    pool.wait_ge(pe_pv, NG * n).then_inc(pool_passed, 1)
                pool.wait_ge(dve_vf, 2 * n + 2).then_inc(pool_passed, 1)
                vh = V3[:, :, :, 0:HD]
                pool.tensor_copy(vh, vf[:, :, :].rearrange("p b (h d) -> p b h d", d=HD)).then_inc(pool_v1, 1)
                pool.wait_ge(dve_vr, n + 1).then_inc(pool_passed, 1)
                pool.tensor_copy(V3[:, :, :, HD:2 * HD], vr[:, :, :].rearrange("p b (h d) -> p b h d", d=HD)).then_inc(pool_v2, 1)

            def residual(n, first):
                if not first:
                    pool.wait_ge(dve_x2, SB * n)
                pool.tensor_tensor(xbo[:, :, :], x_all[:, bass.ds(n * SB * D, SB * D)].rearrange("p (i d) -> p i d", d=D),
                                   tbo[:, :].unsqueeze(1).to_broadcast([P, SB, D]), ALU.add).then_inc(pool_xbo, 1)

            def norm2(m):
                pool.wait_ge(dve_mv2, SB * m + SB).then_inc(pool_passed, 1)
                var = mv2[:, :, 1]
                c = [0]

                def link(ins):
                    c[0] += 1
                    ins.then_inc(pool_rs2, 1)
                    pool.wait_ge(pool_rs2, 7 * m + c[0]).then_inc(pool_passed, 1)

                link(pool.tensor_scalar(lnt[0][:, :], var, EPS, None, ALU.add))
                link(pool.tensor_tensor(lnt[1][:, :], lnt[0][:, :], mhalf[:, 0:SB], ALU.pow))
                link(pool.tensor_tensor(lnt[2][:, :], lnt[1][:, :], lnt[1][:, :], ALU.mult))
                link(pool.tensor_tensor(lnt[3][:, :], lnt[2][:, :], var, ALU.mult))
                link(pool.tensor_scalar(lnt[4][:, :], lnt[3][:, :], EPS, None, ALU.add))
                link(pool.tensor_tensor(lnt[5][:, :], lnt[4][:, :], mhalf[:, 0:SB], ALU.pow))
                pool.tensor_tensor(lnt[6][:, :], lnt[1][:, :], lnt[5][:, :], ALU.mult).then_inc(pool_rs2, 1)

            def affine2(m):
                pool.wait_ge(dve_xc, SB * m + SB)
                pool.tensor_tensor(xr[:, :, 0:D], xr[:, :, 0:D], gab[:, :].unsqueeze(1).to_broadcast([P, SB, D]), ALU.mult)\
                    .then_inc(pool_xg, 1)
                pool.wait_ge(pool_xg, m + 1)
                pool.tensor_tensor(xr[:, :, 0:D], xr[:, :, 0:D], beb[:, :].unsqueeze(1).to_broadcast([P, SB, D]), ALU.add)\
                    .then_inc(pool_xr, 1)
                pool.tensor_copy(xr[:, :, D + E:ROW].bitcast(I32), tokid[:, bass.ds(m * SB, SB)].unsqueeze(2)).then_inc(pool_xr, 1)

            def dispatch(m):
                pool.wait_ge(dve_idx, m + 1).then_inc(pool_passed, 1)
                pool.wait_ge(dve_wp, m + 1).then_inc(pool_passed, 1)
                pool.wait_ge(pool_xr, 2 * m + 2).then_inc(pool_passed, 1)
                for r in range(K):
                    for j in range(SB):
                        c = r * SB + j
                        pool.indirect_dma_start(out=buf, out_offset=bass.IndirectOffsetOnAxis(slotu[:, c:c + 1], 0),
                                                in_=xr[:, j, :], in_offset=None, bounds_check=E * CAP - 1,
                                                oob_is_err=False).then_inc(scattered, 16)

            def body(n, first):
                if first:
                    pool.wait_ge(ld_x[0], 16)
                prepare(n, first)
                head_keys(n, first)
                values(n, first)
                if first:
                    for s in range(1, NSB):
                        pool.wait_ge(ld_x[s], 16)
                residual(n, first)
                if not first:
                    norm2(n - 1)
                for g in range(NG):
                    G = NG * n + g
                    pool.wait_ge(act_exp, G + 1).then_inc(pool_passed, 1)
                    if not first or g >= 4:
                        pool.wait_ge(pe_t, G - 3).then_inc(pool_passed, 1)
                    pool.tensor_copy(pp[g % 4][:, :, 0, :], p32[g % 2][:, :, :]).then_inc(pool_hi, 1)
                    if not first and g == 3:
                        affine2(n - 1)
                if not first:
                    pool.wait_ge(ld_pad, 32)
                    dispatch(n - 1)

            body(0, True)
            with pool.Fori(1, NSB) as n:
                body(n, False)
            norm2(NSB - 1)
            affine2(NSB - 1)
            dispatch(NSB - 1)

            pool.wait_ge(st_x2, 16 * NSB)

            def add_rows(e, par):
                for c in range(CT):
                    q = CT * e + c
                    pool.wait_ge(dve_ysc, q + 1).then_inc(pool_passed, 1)
                    if not (isinstance(e, int) and e == 0 and c == 0):
                        pool.wait_ge(added, 16 * q).then_inc(pool_passed, 1)
                    pool.indirect_dma_start(out=out, out_offset=bass.IndirectOffsetOnAxis(rows[par][:, c, D + E:ROW].bitcast(U32), 0),
                                            in_=ysc[(par + c) % 2][:, :], in_offset=None, bounds_check=TOKENS + P - 1,
                                            oob_is_err=True, compute_op=ALU.add).then_inc(added, 16)

            add_rows(0, 0)
            add_rows(1, 1)
            with pool.Fori(1, E // 2) as i:
                add_rows(2 * i, 0)
                add_rows(2 * i + 1, 1)
            pool.wait_ge(added, 16 * E * CT)

        @block.scalar
        def _(act):
            act.dma_start(gate[:, 0:1], g_xattn.partition_broadcast(P)).then_inc(ld_c, 16)
            act.dma_start(gate[:, 1:2], g_ffn.partition_broadcast(P)).then_inc(ld_c, 16)
            act.dma_start(bqk[:, 0, :], bq).then_inc(ld_c, 16)
            act.dma_start(bqk[:, 1, :], bk).then_inc(ld_c, 16)
            for dst, src in ((bvb, bv), (bob, bo), (gab, gamma), (beb, beta)):
                act.dma_start(dst[:, :], src.partition_broadcast(P)).then_inc(ld_c, 16)
            act.wait_ge(ld_c, 16 * 8)
            act.activation(tg[:, :], gate[:, :], ACT.Tanh).then_inc(gates_ok, 1)

            def exps_of_logits(m):
                act.wait_ge(dve_lgs, m + 1)
                act.activation(lex[:, :, :], lgs[:, :, :], ACT.Exp).then_inc(act_ex, 1)

            def x2_columns(m):
                for c in range(DC):
                    act.wait_ge(pe_x2T, DC * m + c + 1)
                    act.activation(xnT[:, c, :], X[c][:, :], ACT.Copy).then_inc(act_x2T, 1)

            def body(n, first):
                for c in range(DC):
                    act.wait_ge(pe_xT, DC * n + c + 1)
                    act.activation(xT[:, c, :], X[c][:, :], ACT.Copy).then_inc(act_xT, 1)
                if first:
                    act.wait_ge(const_ok, 16)
                for t in range(DC):
                    act.wait_ge(pe_q, DC * n + t + 1)
                    act.activation(qT[:, t, :], X[t][:, :], ACT.Identity, bias=bq4[:, t:t + 1], scale=HD ** -0.5).then_inc(act_q, 1)
                if not first:
                    act.wait_ge(dve_km, 8 * n)
                    act.wait_ge(pool_km, 8 * n)
                for t in range(DC):
                    act.wait_ge(pe_k, DC * n + t + 1)
                    act.activation(kT[:, t, :], X[t][:, :], ACT.Identity, bias=bqk[:, 1, t:t + 1]).then_inc(act_k, 1)
                for g in range(NG + 6):
                    G = NG * n + g
                    if g < NG:
                        act.wait_ge(dve_sub, G + 1)
                        if not first or g >= 2:
                            act.wait_ge(pool_hi, G - 1)
                            act.wait_ge(dve_lo, G - 1)
                        act.activation(p32[g % 2][:, :, :], sS[g % 2][:, :, :], ACT.Exp, bias=pbias[:, 0:1]).then_inc(act_exp, 1)
                    gg = g - 2
                    if 0 <= gg < NG:
                        act.wait_ge(pe_t, G - 1)
                        if not first or gg >= 2:
                            act.wait_ge(pe_pv, G - 3)
                        act.activation(pT[gg % 2][:, :, :, :], Tb[gg % 2][:, :].bitcast(F16).rearrange("p (h s t) -> p h s t", h=GH, s=2),
                                       ACT.Copy).then_inc(act_pt, 1)
                    if not first and g == 6:
                        x2_columns(n - 1)
                    if not first and g == 11:
                        exps_of_logits(n - 1)
                    if g >= 8 and (g - 8) % 4 == 0:
                        b = (g - 8) // 4
                        act.wait_ge(pe_oT, SB * n + b + 1)
                        act.activation(oT[:, :, :], X[0][:, 0:D].rearrange("p (c t) -> p c t", c=DC), ACT.Copy).then_inc(act_oT, 1)

            body(0, True)
            with act.Fori(1, NSB) as n:
                body(n, False)
            x2_columns(NSB - 1)
            exps_of_logits(NSB - 1)

            def stage_uses(i, par, k):
                s = (par + k) % 2
                return 3 * i + sum(1 for pp_, kk in ((0, 0), (0, 1), (0, 2), (1, 0), (1, 1), (1, 2))
                                   if (pp_ + kk) % 2 == s and (pp_, kk) <= (par, k))

            def high(i, par, q12):
                k, q = q12 // 4, q12 % 4
                s = (par + k) % 2
                if q == 0:
                    act.wait_ge(ld_st[s], 16 * stage_uses(i, par, k))
                act.activation(Wh[par][:, k, q * QW:(q + 1) * QW], stage[s][:, q * QW:(q + 1) * QW], ACT.Copy)\
                    .then_inc(act_wh, 1)

            def rows_high(e):
                for a in range(4):
                    c, d = a // 2, a % 2
                    o, w = CHUNKS[c]
                    act.wait_ge(pe_bT, 4 * e + a + 1)
                    act.activation(bXh[:, d, o:o + w], Xc[a % 2][:, 0:w], ACT.Copy).then_inc(act_bh, 1)

            def hidden_high(e, j):
                c, f = j // FT, j % FT
                w = CHUNKS[c][1]
                act.wait_ge(dve_h, 16 * e + j + 1)
                act.activation(hH[c][:, f, :], hF[j % 2][:, 0:w], ACT.Copy).then_inc(act_hh, 1)

            for q12 in range(PIECES):
                high(0, 0, q12)
            rows_high(0)

            def expert(i, par, last, first):
                e = 2 * i + par
                for j in range(2 * FT + 1):
                    if j < 2 * FT:
                        c = j // FT
                        w = CHUNKS[c][1]
                        act.wait_ge(pe_gu, 16 * e + j + 1)
                        if not first or j >= 2:
                            act.wait_ge(dve_h, 16 * e + j - 1)
                        act.activation(sil[j % 2][:, 0:w], Gb[j % 2][:, 0:w], ACT.Silu).then_inc(act_sil, 1)
                    if j >= 1:
                        if j == 1 and not first:
                            act.wait_ge(pe_out, CT * e)
                        hidden_high(e, j - 1)
                    if not last and 2 <= j < 2 + PIECES:
                        high(i + (par == 1), 1 - par, j - 2)
                if not last:
                    rows_high(e + 1)

            expert(0, 0, False, True)
            expert(0, 1, False, False)
            with act.Fori(1, E // 2 - 1) as i:
                expert(i, 0, False, False)
                expert(i, 1, False, False)
            expert(E // 2 - 1, 0, False, False)
            expert(E // 2 - 1, 1, True, False)

        @block.vector
        def _(dve):
            for i in range(SEQS):
                if i % SB == 0:
                    dve.wait_ge(ld_x[i // SB], 16)
                dve.bn_stats(st_all[:, i, :], xv[:, i, :]).then_inc(dve_st, 1)
            for i in range(SEQS):
                dve.wait_ge(dve_st, i + 1)
                dve.bn_aggr(mv_all[:, i, :], st_all[:, i, :]).then_inc(dve_mv1, 1)

            def normalize_inputs(n, first):
                dve.wait_ge(pool_st1, 2 * n + 2)
                if not first:
                    dve.wait_ge(pe_xT, DC * n)
                for j in range(SB):
                    dve.tensor_scalar(xn1[:, j, :], x_tile(SB * n + j), mean1[:, j:j + 1], rstd1[:, j:j + 1],
                                      ALU.subtract, ALU.mult).then_inc(dve_xn1, 1)

            def head_keys(n, first):
                dve.wait_ge(act_k, DC * n + 1)
                if not first:
                    dve.wait_ge(pe_s, NG * n)
                for h in range(8):
                    dve.tensor_scalar(kM[:, h, :], kT[:, 0, :], hmask[:, h:h + 1], None, ALU.mult).then_inc(dve_km, 1)

            def values(n, first):
                for t in range(2):
                    dve.wait_ge(pe_v, 2 * n + t + 1)
                    if not first:
                        dve.wait_ge(pool_v1, n)
                    dve.tensor_tensor(vf[:, 2 * t:2 * t + 2, :], X[t][:, :].rearrange("p (b d) -> p b d", d=D),
                                      bvb[:, :].unsqueeze(1).to_broadcast([P, 2, D]), ALU.add).then_inc(dve_vf, 1)
                dve.wait_ge(pool_v1, n + 1)
                hv = "p b (h d) -> p b h d"
                for b in range(SB):
                    ins = dve.tensor_tensor(vr[:, b, :].rearrange("p (h d) -> p h d", d=HD),
                                            vf[:, b, :].rearrange("p (h d) -> p h d", d=HD), V3[:, b, :, 0:HD], ALU.subtract)
                ins.then_inc(dve_vr, 1)
                dve.wait_ge(pool_v2, n + 1)
                for b in range(SB):
                    ins = dve.tensor_tensor(V3[:, b, :, 2 * HD:3 * HD], vr[:, b, :].rearrange("p (h d) -> p h d", d=HD),
                                            V3[:, b, :, HD:2 * HD], ALU.subtract)
                ins.then_inc(dve_v3, 1)

            def stats2(m):
                for j in range(SB):
                    dve.wait_ge(dve_x2, SB * m + j + 1)
                    dve.bn_stats(st2[:, j, :], x_tile(SB * m + j)).then_inc(dve_st2, 1)
                for j in range(SB):
                    dve.wait_ge(dve_st2, SB * m + j + 1).then_inc(dve_passed, 1)
                    dve.bn_aggr(mv2[:, j, :], st2[:, j, :]).then_inc(dve_mv2, 1)

            def normalize2(m, first):
                dve.wait_ge(pool_rs2, 7 * m + 7)
                if not first:
                    dve.wait_ge(scattered, 16 * K * SB * m)
                for j in range(SB):
                    dve.tensor_scalar(xr[:, j, 0:D], x_tile(SB * m + j), mv2[:, j, 0:1], lnt[6][:, j:j + 1],
                                      ALU.subtract, ALU.mult).then_inc(dve_xc, 1)

            def logits(m):
                dve.wait_ge(pe_lg, m + 1)
                dve.tensor_scalar(lgc[:, :, :], X[0][:, 0:SB * E].rearrange("p (j e) -> p j e", e=E), -CLAMP, CLAMP, ALU.max, ALU.min)\
                   .then_inc(dve_lg, 1)
                dve.wait_ge(dve_lg, m + 1)
                dve.tensor_reduce(lmx[:, :], lgc[:, :, :], AX_X, ALU.max).then_inc(dve_r, 1)
                dve.wait_ge(dve_r, R_CHAIN * m + 1)
                dve.tensor_tensor(lgs[:, :, :], lgc[:, :, :], lmx[:, :].unsqueeze(2).to_broadcast([P, SB, E]), ALU.subtract)\
                   .then_inc(dve_lgs, 1)

            def route(m):
                c = [1]

                def link(ins, alone=False):
                    c[0] += 1
                    ins.then_inc(dve_r, 1)
                    if alone:
                        dve.wait_ge(dve_r, R_CHAIN * m + c[0]).then_inc(dve_passed, 1)
                    else:
                        dve.wait_ge(dve_r, R_CHAIN * m + c[0])

                dve.wait_ge(act_ex, m + 1)
                link(dve.tensor_reduce(lsm[:, :], lex[:, :, :], AX_X, ALU.add))
                link(dve.tensor_scalar(lse[:, :], lsm[:, :], 1e-12, None, ALU.add))
                link(dve.reciprocal(lrc[:, :], lse[:, :]))
                link(dve.tensor_tensor(prob[:, :, :], lex[:, :, :], lrc[:, :].unsqueeze(2).to_broadcast([P, SB, E]), ALU.mult), alone=True)
                for j in range(SB):
                    ins = dve.max(top8[:, j, :], prob[:, j, :])
                link(ins, alone=True)
                for j in range(SB):
                    ins = dve.max_index(topi[:, j, :], top8[:, j, :], prob[:, j, :])
                link(ins)
                link(dve.tensor_copy(ixf[:, :, :], topi[:, :, 0:K].rearrange("p j r -> p r j")))
                link(dve.tensor_tensor(pick[:, :, :, :], iota8[:, :].unsqueeze(1).unsqueeze(1).to_broadcast([P, K, SB, E]),
                                       ixf[:, :, :].unsqueeze(3).to_broadcast([P, K, SB, E]), ALU.is_equal))
                dve.tensor_tensor(member[:, :, :], pick[:, 0, :, :], pick[:, 1, :, :], ALU.add).then_inc(dve_mem, 1)
                dve.tensor_scalar(xr[:, :, D:D + E], prob[:, :, :], tg[:, 1:2], None, ALU.mult).then_inc(dve_wp, 1)

            def slots(m):
                dve.wait_ge(pe_rk, m + 1)
                rk = X[1][:, 0:SB * E].rearrange("p (j e) -> p j e", e=E)
                dve.tensor_scalar(late[:, :, :], rk, float(CAP), LATE, ALU.is_ge, ALU.mult).then_inc(dve_rk, 1)
                dve.tensor_tensor(slot0[:, :, :], rk, ebase[:, :].unsqueeze(1).to_broadcast([P, SB, E]), ALU.add).then_inc(dve_rk, 1)
                dve.tensor_reduce(seen_add[:, :], member[:, :, :].rearrange("p j e -> p e j"), AX_X, ALU.add).then_inc(dve_rk, 1)
                dve.wait_ge(dve_rk, 6 * m + 3)
                dve.tensor_tensor(slot[:, :, :], slot0[:, :, :], late[:, :, :], ALU.add).then_inc(dve_rk, 1)
                dve.tensor_tensor(seen[:, :], seen[:, :], seen_add[:, :], ALU.add)
                dve.wait_ge(dve_rk, 6 * m + 4)
                dve.tensor_tensor(pslot[:, :, :, :], pick[:, :, :, :], slot[:, :, :].unsqueeze(1).to_broadcast([P, K, SB, E]), ALU.mult)\
                   .then_inc(dve_rk, 1)
                dve.wait_ge(dve_rk, 6 * m + 5)
                dve.tensor_reduce(slotf[:, :, :], pslot[:, :, :, :], AX_X, ALU.add).then_inc(dve_rk, 1)
                dve.wait_ge(dve_rk, 6 * m + 6)
                dve.tensor_copy(slotu[:, :], slotf[:, :, :].rearrange("p r j -> p (r j)")).then_inc(dve_idx, 1)

            def body(n, first):
                normalize_inputs(n, first)
                if not first:
                    stats2(n - 1)
                head_keys(n, first)
                values(n, first)
                for g in range(NG + 7):
                    G = NG * n + g
                    if g < NG:
                        dve.wait_ge(pe_s, G + 1)
                        dve.tensor_reduce(nm[g % 2][:, :], S[g % 2][:, :].rearrange("p (h t) -> p h t", t=T), AX_X, ALU.max)\
                           .then_inc(dve_max, 1)
                    gg = g - 1
                    if 0 <= gg < NG:
                        dve.wait_ge(act_exp, G)
                        dve.wait_ge(pool_hi, G)
                        if not first or gg >= 4:
                            dve.wait_ge(pe_t, G - 4)
                        dve.tensor_tensor(pp[gg % 4][:, :, 1, :], p32[gg % 2][:, :, :], pp[gg % 4][:, :, 0, :], ALU.subtract)\
                           .then_inc(dve_lo, 1)
                    if g < NG:
                        dve.wait_ge(dve_max, G + 1)
                        if not first or g >= 2:
                            dve.wait_ge(act_exp, G - 1)
                        dve.tensor_tensor(sS[g % 2][:, :, :], S[g % 2][:, :].rearrange("p (h t) -> p h t", t=T),
                                          nm[g % 2][:, :].unsqueeze(2).to_broadcast([P, GH, T]), ALU.subtract).then_inc(dve_sub, 1)
                    if g >= 6 and (g - 6) % 2 == 0 and (g - 6) // 2 < 2 * SB:
                        k = (g - 6) // 2
                        kk = 2 * SB * n + k
                        ob = O[k % 2][:, 0:8 * VW].rearrange("p (h w) -> p h w", w=VW)
                        dve.wait_ge(pe_pv, NG * n + 2 * k + 2)
                        if not first or k > 0:
                            dve.wait_ge(dve_on, kk)
                        dve.tensor_reduce(osum[:, :, :], ob[:, :, 0:3 * HD].rearrange("p h (c d) -> p h d c", d=HD), AX_X, ALU.add)\
                           .then_inc(dve_os, 1)
                        dve.reciprocal(orec[:, :], ob[:, :, 3 * HD]).then_inc(dve_rec, 1)
                        dve.wait_ge(dve_os, kk + 1)
                        dve.wait_ge(dve_rec, kk + 1)
                        if k % 2 == 0 and (not first or k > 0):
                            dve.wait_ge(pe_oT, SB * n + k // 2)
                        dve.tensor_tensor(oN[:, (k % 2) * P:(k % 2 + 1) * P].rearrange("p (h d) -> p h d", d=HD), osum[:, :, :],
                                          orec[:, :].unsqueeze(2).to_broadcast([P, 8, HD]), ALU.mult).then_inc(dve_on, 1)
                    if g >= 10 and (g - 10) % 4 == 0:
                        b = (g - 10) // 4
                        dve.wait_ge(pe_y, SB * n + b + 1)
                        dve.wait_ge(pool_xbo, n + 1)
                        dve.scalar_tensor_tensor(x_tile(SB * n + b), X[1][:, 0:D], tg[:, 0:1], xbo[:, b, :], ALU.mult, ALU.add)\
                           .then_inc(dve_x2, 1)
                    if not first:
                        if g == 2:
                            normalize2(n - 1, False)
                        if g == 10:
                            logits(n - 1)
                        if g == 12:
                            route(n - 1)
                        if g == 16:
                            slots(n - 1)

            dve.wait_ge(const_ok, 15)
            dve.wait_ge(gates_ok, 1)
            body(0, True)
            with dve.Fori(1, NSB) as n:
                body(n, False)
            stats2(NSB - 1)
            normalize2(NSB - 1, False)
            logits(NSB - 1)
            route(NSB - 1)
            slots(NSB - 1)

            def stage_uses(i, par, k):
                s = (par + k) % 2
                return 3 * i + sum(1 for pp_, kk in ((0, 0), (0, 1), (0, 2), (1, 0), (1, 1), (1, 2))
                                   if (pp_ + kk) % 2 == s and (pp_, kk) <= (par, k))

            def low(i, par, q12):
                k, q = q12 // 4, q12 % 4
                s = (par + k) % 2
                if q == 0:
                    dve.wait_ge(ld_st[s], 16 * stage_uses(i, par, k))
                dve.wait_ge(act_wh, PIECES * (2 * i + par) + q12 + 1)
                cols = slice(q * QW, (q + 1) * QW)
                dve.tensor_tensor(Wl[par][:, k, cols], stage[s][:, cols], Wh[par][:, k, cols].bitcast(F32), ALU.subtract)\
                   .then_inc(dve_wl, 1)

            def rows_low(e):
                for a in range(4):
                    c, d = a // 2, a % 2
                    o, w = CHUNKS[c]
                    dve.wait_ge(act_bh, 4 * e + a + 1)
                    dve.tensor_tensor(bXl[:, d, o:o + w], Xc[a % 2][:, 0:w], bXh[:, d, o:o + w].bitcast(F32), ALU.subtract)\
                       .then_inc(dve_bl, 1)

            for q12 in range(PIECES):
                low(0, 0, q12)
            rows_low(0)

            def expert(i, par, last, first):
                e = 2 * i + par
                for j in range(2 * FT + 2):
                    if j < 2 * FT:
                        w = CHUNKS[j // FT][1]
                        dve.wait_ge(act_sil, 16 * e + j + 1)
                        if not first or j >= 2:
                            dve.wait_ge(act_hh, 16 * e + j - 1)
                            dve.wait_ge(dve_hl, 16 * e + j - 1)
                        dve.tensor_tensor(hF[j % 2][:, 0:w], sil[j % 2][:, 0:w], Ub[j % 2][:, 0:w], ALU.mult).then_inc(dve_h, 1)
                    jj = j - 1
                    if 0 <= jj < 2 * FT:
                        c, f = jj // FT, jj % FT
                        w = CHUNKS[c][1]
                        dve.wait_ge(act_hh, 16 * e + jj + 1)
                        dve.tensor_tensor(hL[c][:, f, :], hF[jj % 2][:, 0:w], hH[c][:, f, :].bitcast(F32), ALU.subtract)\
                           .then_inc(dve_hl, 1)
                    if not last and 2 <= j < 2 + PIECES:
                        low(i + (par == 1), 1 - par, j - 2)
                if not last:
                    rows_low(e + 1)
                for c in range(CT):
                    q = CT * e + c
                    dve.wait_ge(pe_out, q + 1)
                    if not first or c >= 2:
                        dve.wait_ge(added, 16 * (q - 1))
                    dve.tensor_scalar(ysc[(par + c) % 2][:, :], Yb[(par + c) % 2][:, 0:D], rows[par][:, c, bass.ds(D + e, 1)], None, ALU.mult)\
                       .then_inc(dve_ysc, 1)

            expert(0, 0, False, True)
            expert(0, 1, False, False)
            with dve.Fori(1, E // 2 - 1) as i:
                expert(i, 0, False, False)
                expert(i, 1, False, False)
            expert(E // 2 - 1, 0, False, False)
            expert(E // 2 - 1, 1, True, False)

        @block.tensor
        def _(pe):
            def project(n, first):
                pe.wait_ge(dve_xn1, SB * n + SB)
                for c in range(DC):
                    if not first:
                        if c == 0:
                            pe.wait_ge(act_oT, SB * n)
                        else:
                            pe.wait_ge(dve_x2, SB * n)
                    for j in range(SB):
                        ins = nc.tensor.transpose(X[c][:, j * T:(j + 1) * T], xn1[:, j, c * P:(c + 1) * P], ident32[:, :])
                    ins.then_inc(pe_xT, 1)
                if first:
                    pe.wait_ge(ld_w, 16 * 5)
                pe.wait_ge(act_xT, DC * n + 2)
                for t in range(DC):
                    for c in range(DC):
                        ins = nc.tensor.matmul(X[t][:, :], wq[:, c, t * P:(t + 1) * P], xT[:, c, :], start=(c == 0), stop=(c == DC - 1))
                    ins.then_inc(pe_q, 1)
                pe.wait_ge(ld_ctx, 16 * n + 16)
                for t in range(DC):
                    pe.wait_ge(act_q, DC * n + t + 1)
                    for c in range(DC):
                        ins = nc.tensor.matmul(X[t][:, :], wk[:, c, t * P:(t + 1) * P], cT[:, c, :], start=(c == 0), stop=(c == DC - 1))
                    ins.then_inc(pe_k, 1)
                for t in range(2):
                    pe.wait_ge(act_k, DC * n + t + 1)
                    for b in range(2 * t, 2 * t + 2):
                        for c in range(DC):
                            ins = nc.tensor.matmul(X[t][:, (b % 2) * D:(b % 2 + 1) * D], cT[:, c, b * T:(b + 1) * T], wv[:, c, :],
                                                   start=(c == 0), stop=(c == DC - 1))
                    ins.then_inc(pe_v, 1)

            def x2_columns(m, n, first_use):
                pe.wait_ge(pool_xr, 2 * m + 1)
                for c in range(DC):
                    first_use(c)
                    for j in range(SB):
                        ins = nc.tensor.transpose(X[c][:, j * T:(j + 1) * T], xr[:, j, c * P:(c + 1) * P], ident32[:, :])
                    ins.then_inc(pe_x2T, 1)

            def logits(m):
                pe.wait_ge(act_x2T, DC * m + 2)
                for j in range(SB):
                    for c in range(DC):
                        ins = nc.tensor.matmul(X[0][:, j * E:(j + 1) * E], xnT[:, c, j * T:(j + 1) * T], wr[:, c, :],
                                               start=(c == 0), stop=(c == DC - 1))
                ins.then_inc(pe_lg, 1)

            def ranks(m, first):
                pe.wait_ge(dve_mem, m + 1)
                rk = X[1][:, 0:SB * E].rearrange("p (j e) -> p j e", e=E)
                nc.tensor.matmul(rk, before[:, :], member[:, :, :], start=True, stop=False)
                for j in range(1, SB):
                    nc.tensor.matmul(rk[:, j:SB, :], onesb[:, :], member[:, 0:SB - j, :], start=False, stop=False)
                nc.tensor.matmul(rk, onesb[:, :], seen[:, :].unsqueeze(1).to_broadcast([P, SB, E]), start=False, stop=True)\
                    .then_inc(pe_rk, 1)

            def body(n, first):
                project(n, first)
                for g in range(NG + 6):
                    G = NG * n + g
                    if g < NG:
                        b, hq = g // GPS, g % GPS
                        if g < GPS:
                            if g < 2:
                                pe.wait_ge(dve_km, 8 * n + GH * hq + GH)
                            else:
                                pe.wait_ge(pool_km, 8 * n + GH * (hq - 2) + GH)
                        if not first or g >= 2:
                            pe.wait_ge(dve_sub, G - 1)
                        nc.tensor.matmul(S[g % 2][:, :], identb[:, :], causal[:, :, :], start=True, stop=False)
                        nc.tensor.matmul(S[g % 2][:, :], qT[:, hq // 2, b * T:(b + 1) * T], kM[:, GH * hq:GH * hq + GH, b * T:(b + 1) * T],
                                         start=False, stop=True).then_inc(pe_s, 1)
                    gg = g - 2
                    if 0 <= gg < NG:
                        pe.wait_ge(dve_lo, G - 1)
                        pe.wait_ge(pool_hi, G - 1)
                        if not first or gg >= 2:
                            pe.wait_ge(act_pt, G - 3)
                        tb = Tb[gg % 2][:, :].bitcast(F16).rearrange("p (h s t) -> p h s t", h=GH, s=2)
                        for h in range(GH):
                            for s in range(2):
                                ins = nc.tensor.transpose(tb[:, h, s, :], pp[gg % 4][:, h, s, :], ident16[:, :])
                        ins.then_inc(pe_t, 1)
                    gg = g - 3
                    if 0 <= gg < NG:
                        b, hq = gg // GPS, gg % GPS
                        k = gg // 2
                        if gg == 0:
                            pe.wait_ge(dve_v3, n + 1)
                        if gg % 2 == 0 and (not first or k >= 2):
                            pe.wait_ge(dve_on, 2 * SB * n + k - 1)
                        pe.wait_ge(act_pt, G - 2)
                        for h in range(GH):
                            o = ((gg % 2) * GH + h) * VW
                            for s in range(2):
                                ins = nc.tensor.matmul(O[k % 2][:, o:o + VW], pT[gg % 2][:, h, s, :], V3[:, b, GH * hq + h, :],
                                                       start=(s == 0), stop=(s == 1))
                        ins.then_inc(pe_pv, 1)
                    if not first and g == 6:
                        x2_columns(n - 1, n, lambda c: pe.wait_ge(dve_vf, 2 * n + c + 1))
                    if g >= 8 and (g - 8) % 4 == 0:
                        b = (g - 8) // 4
                        pe.wait_ge(dve_on, 2 * SB * n + 2 * b + 2)
                        if b == 0:
                            pe.wait_ge(dve_vf, 2 * n + 2)
                            if not first:
                                pe.wait_ge(act_x2T, DC * n)
                        elif b == 1 and not first:
                            pe.wait_ge(dve_lg, n)
                        for c in range(DC):
                            ins = nc.tensor.transpose(X[0][:, c * T:(c + 1) * T], oN[:, c * P:(c + 1) * P], ident32[:, :])
                        ins.then_inc(pe_oT, 1)
                    if g >= 9 and (g - 9) % 4 == 0:
                        b = (g - 9) // 4
                        pe.wait_ge(act_oT, SB * n + b + 1)
                        if b > 0:
                            pe.wait_ge(dve_x2, SB * n + b)
                        if b == 2 and not first:
                            pe.wait_ge(dve_rk, 6 * n)
                        for c in range(DC):
                            ins = nc.tensor.matmul(X[1][:, 0:D], oT[:, c, :], wo[:, c, :], start=(c == 0), stop=(c == DC - 1))
                        ins.then_inc(pe_y, 1)
                    if not first and g == 10:
                        logits(n - 1)
                    if not first and g == 15:
                        pe.wait_ge(dve_x2, SB * n + 2)
                        ranks(n - 1, False)

            pe.wait_ge(const_ok, 12)
            body(0, True)
            with pe.Fori(1, NSB) as n:
                body(n, False)
            m = NSB - 1
            x2_columns(m, NSB, lambda c: pe.wait_ge(act_oT if c == 0 else dve_x2, SEQS))
            logits(m)
            ranks(m, False)

            def rows_columns(e, par, use):
                pe.wait_ge(ld_rows[par], 16 * use)
                for a in range(4):
                    c, d = a // 2, a % 2
                    o, w = CHUNKS[c]
                    if not (isinstance(e, int) and e == 0 and a < 2):
                        pe.wait_ge(dve_bl, 4 * e + a - 1)
                    for t in range(w // P):
                        ins = nc.tensor.transpose(Xc[a % 2][:, t * P:(t + 1) * P], rows[par][:, o // P + t, d * P:(d + 1) * P], ident32[:, :])
                    ins.then_inc(pe_bT, 1)

            def three(out_ap, parts, start, stop):
                (ah, al), (bh, bl) = parts
                nc.tensor.matmul(out_ap, ah, bh, start=start, stop=False)
                nc.tensor.matmul(out_ap, ah, bl, start=False, stop=False)
                return nc.tensor.matmul(out_ap, al, bh, start=False, stop=stop)

            pe.wait_ge(dve_rk, 6 * NSB)
            rows_columns(0, 0, 1)

            def expert(i, par, last, first):
                e = 2 * i + par
                pe.wait_ge(dve_wl, PIECES * e + PIECES)
                for j in range(2 * FT):
                    c, f = j // FT, j % FT
                    o, w = CHUNKS[c]
                    if f == 0:
                        pe.wait_ge(dve_bl, 4 * e + 2 * c + 2)
                    if not first or j >= 2:
                        pe.wait_ge(dve_h, 16 * e + j - 1)
                    for half, dst in ((0, Gb), (1, Ub)):
                        fo = half * FF + f * P
                        for d in range(DC):
                            ins = three(dst[j % 2][:, 0:w],
                                        ((Wh[par][:, d, fo:fo + P], Wl[par][:, d, fo:fo + P]),
                                         (bXh[:, d, o:o + w], bXl[:, d, o:o + w])), d == 0, d == DC - 1)
                    ins.then_inc(pe_gu, 1)
                if not last:
                    rows_columns(e + 1, 1 - par, i + 1 + par)
                for t in range(CT):
                    c = 0 if t * P < CHUNKS[1][0] else 1
                    o = t * P - CHUNKS[c][0]
                    q = CT * e + t
                    if t == 0 or t * P == CHUNKS[1][0]:
                        pe.wait_ge(dve_hl, 16 * e + FT * (c + 1))
                    if not first or t >= 2:
                        pe.wait_ge(dve_ysc, q - 1)
                    for f in range(FT):
                        ins = three(Yb[(par + t) % 2][:, 0:D],
                                    ((hH[c][:, f, o:o + P], hL[c][:, f, o:o + P]),
                                     (Wh[par][:, DC, f * D:(f + 1) * D], Wl[par][:, DC, f * D:(f + 1) * D])), f == 0, f == FT - 1)
                    ins.then_inc(pe_out, 1)

            expert(0, 0, False, True)
            expert(0, 1, False, False)
            with pe.Fori(1, E // 2 - 1) as i:
                expert(i, 0, False, False)
                expert(i, 1, False, False)
            expert(E // 2 - 1, 0, False, False)
            expert(E // 2 - 1, 1, True, False)


def kernel(**inputs):
    import numpy as _np
    import concourse.bacc as _bacc
    from concourse import mybir as _mybir
    from concourse.bass_utils import run_bass_kernel_spmd as _run

    a = {k: _np.asarray(v) for k, v in inputs.items()}
    flat = a["x"].reshape(TOKENS, D)
    ops = {
        "x": flat,
        "ctxT": a["ctx_1024"].reshape(TOKENS, D).T,
        "g_xattn": a["g_xattn"],
        "g_ffn": a["g_ffn"],
        "wqT": a["L0_xattn_wq"].T, "bq": a["L0_xattn_bq"].reshape(DC, P).T,
        "wkT": a["L0_xattn_wk"].T, "bk": a["L0_xattn_bk"].reshape(DC, P).T,
        "wvT": a["L0_xattn_wv"].T, "bv": a["L0_xattn_bv"],
        "woT": a["L0_xattn_wo"].T, "bo": a["L0_xattn_bo"],
        "gamma": a["L0_ffn_ln_gamma"], "beta": a["L0_ffn_ln_beta"],
        "wrT": a["L0_ffn_Wr"].T,
        "w12T": a["L0_ffn_W12"].transpose(0, 2, 1),
        "w3T": a["L0_ffn_W3"].transpose(0, 2, 1),
    }
    nc = _bacc.Bacc("TRN2", target_bir_lowering=False, num_devices=1)
    arrays, args = {}, []
    for name, v in ops.items():
        v = _np.ascontiguousarray(v)
        arrays[f"in_{name}"] = v
        args.append(nc.dram_tensor(f"in_{name}", v.shape, _mybir.dt.from_np(v.dtype), kind="ExternalInput").ap())
    args.append(nc.dram_tensor("out_tokens", (TOKENS + P, D), _mybir.dt.float32, kind="ExternalOutput").ap())
    gated_block(nc, *args)
    r = _run(nc, [arrays], core_ids=[0])
    return r.results[0]["out_tokens"][:TOKENS].reshape(SEQS, T, D)
```

```python
from contextlib import ExitStack

import concourse.bass as bass
from concourse import mybir

F32 = mybir.dt.float32
F32R = mybir.dt.float32r
BF16 = mybir.dt.bfloat16
F16 = mybir.dt.float16
I32 = mybir.dt.int32
U32 = mybir.dt.uint32
ALU = mybir.AluOpType
ACT = mybir.ActivationFunctionType
AX_X = mybir.AxisListType.X

P = 128
SEQS, T, D = 16, 128, 256
H, HD = 16, 16
DC = D // P
SB = 2
XP = 4
NSB = SEQS // SB
GH = 4
GPS = H // GH
NG = SB * GPS
E, K, FF = 8, 2, 1024
TOKENS = SEQS * T
CAP = -(-(-(-TOKENS * K * 5 // 4)) // E)
CT = CAP // P
ROW = D + E + 1
CHUNKS = ((0, 384), (384, 256))
FT = FF // P
CT0 = CHUNKS[0][1] // P
UNIT = 2048
NU = 3
VW = 3 * HD + 2
NEG = -3.0e38
PSCALE = 9.704060527839234
EPS = 1e-5
CLAMP = 10000.0
CONSTS = 12 + 3 * E - 1
KEY_STEPS = {3: range(0, 5), 4: range(5, 11), 5: range(11, H)}
LATE = 1.0e6


def gated_block(nc, x, ctxT, g_xattn, g_ffn, wqT, bq, wkT, bk, wvT, bv, woT, bo, gamma, beta, wrT, w12T, w3T, out):
    with ExitStack() as top:
        def sem(name):
            return top.enter_context(nc.semaphore(name))

        def sb(stack, name, shape, dt):
            return stack.enter_context(nc.sbuf_tensor(name, shape, dt))

        buf = nc.dram_tensor("expert_rows", (E * CAP, ROW), F32).ap()

        ident32 = sb(top, "ident32", [P, P], F32)
        stage = [sb(top, f"stage{i}", [P, UNIT], F32) for i in range(2)]
        wh0 = sb(top, "wh0", [P, NU, UNIT], F32R)
        wl0 = sb(top, "wl0", [P, NU, UNIT], F32R)
        flag = sb(top, "flag", [P, 1], I32)
        past = sb(top, "past", [P, E], I32)
        rows = [sb(top, f"rows{i}", [P, CT, ROW], F32) for i in range(2)]

        pa = ExitStack()
        x_all = sb(pa, "x_all", [P, SEQS * D], F32)
        st_all = sb(pa, "st_all", [P, SEQS, 6], F32)
        mv_all = sb(pa, "mv_all", [P, SEQS, 2], F32)
        rs_all = sb(pa, "rs_all", [P, SEQS], F32)
        ve_all = sb(pa, "ve_all", [P, SEQS], F32)
        xn1 = sb(pa, "xn1", [P, SB, D], F32)
        cT = [sb(pa, f"cT{i}", [P, DC, SB * T], F32) for i in range(2)]
        xT = sb(pa, "xT", [P, DC, SB * T], F32)
        qT = [sb(pa, f"qT{i}", [P, DC, SB * T], F32) for i in range(2)]
        kM = [sb(pa, f"kM{i}", [P, H, SB * T], F32) for i in range(2)]
        vf = sb(pa, "vf", [P, SB, D], F32)
        vr = vf
        V3 = [sb(pa, f"V3_{i}", [P, SB, H, VW], BF16) for i in range(2)]
        nm = [sb(pa, f"nm{i}", [P, GH], F32) for i in range(2)]
        sS = [sb(pa, f"sS{i}", [P, GH, T], F32) for i in range(2)]
        p32 = [sb(pa, f"p32_{i}", [P, GH, T], F32) for i in range(2)]
        pT = [sb(pa, f"pT{i}", [P, 2, GH, T], F16) for i in range(2)]
        osum = sb(pa, "osum", [P, 8, HD], F32)
        orec = sb(pa, "orec", [P, 8], F32)
        oN = sb(pa, "oN", [P, D], F32)
        oT = sb(pa, "oT", [P, DC, T], F32)
        xbo = [sb(pa, f"xbo{i}", [P, SB, D], F32) for i in range(2)]
        wq = sb(pa, "wq", [P, DC, D], F32)
        wk = sb(pa, "wk", [P, DC, D], F32)
        wv = sb(pa, "wv", [P, DC, D], F32)
        wo = sb(pa, "wo", [P, DC, D], F32)
        wr = sb(pa, "wr", [P, DC, E], F32)
        bqk = sb(pa, "bqk", [P, 2, DC], F32)
        bq4 = sb(pa, "bq4", [P, DC], F32)
        bvb = sb(pa, "bvb", [P, D], F32)
        bob = sb(pa, "bob", [P, D], F32)
        tbo = sb(pa, "tbo", [P, D], F32)
        gab = sb(pa, "gab", [P, D], F32)
        beb = sb(pa, "beb", [P, D], F32)
        gate = sb(pa, "gate", [P, 2], F32)
        tg = sb(pa, "tg", [P, 2], F32)
        identb = sb(pa, "identb", [P, P], BF16)
        causal = sb(pa, "causal", [P, GH, T], BF16)
        before = sb(pa, "before", [P, P], BF16)
        onesb = sb(pa, "onesb", [P, P], BF16)
        hmask = sb(pa, "hmask", [P, 8], F32)
        bkm = sb(pa, "bkm", [P, H], F32)
        iota_i = sb(pa, "iota_i", [P, 2, E], I32)
        iota8 = sb(pa, "iota8", [P, E], F32)
        ebase = sb(pa, "ebase", [P, E], F32)
        tokid = sb(pa, "tokid", [P, SEQS], I32)
        padrow = sb(pa, "padrow", [P, ROW], F32)
        zrow = sb(pa, "zrow", [P, D], F32)
        mhalf = sb(pa, "mhalf", [P, SEQS], F32)
        pbias = sb(pa, "pbias", [P, 1], F32)
        xr = [sb(pa, f"xr{i}", [P, SB, ROW], F32) for i in range(2)]
        xnT = sb(pa, "xnT", [P, DC, SB * T], F32)
        st2 = sb(pa, "st2", [P, SB, 6], F32)
        mv2 = sb(pa, "mv2", [P, SB, 2], F32)
        lnt = [sb(pa, f"lnt{i}", [P, SB], F32) for i in range(7)]
        lgc = sb(pa, "lgc", [P, SB, E], F32)
        lgs = sb(pa, "lgs", [P, SB, E], F32)
        lmx = sb(pa, "lmx", [P, SB], F32)
        lex = sb(pa, "lex", [P, SB, E], F32)
        lsm = sb(pa, "lsm", [P, SB], F32)
        lse = sb(pa, "lse", [P, SB], F32)
        lrc = sb(pa, "lrc", [P, SB], F32)
        prob = sb(pa, "prob", [P, SB, E], F32)
        top8 = sb(pa, "top8", [P, SB, 8], F32)
        topi = sb(pa, "topi", [P, SB, 8], U32)
        ixf = sb(pa, "ixf", [P, K, SB], F32)
        pick = sb(pa, "pick", [P, K, SB, E], F32)
        member = sb(pa, "member", [P, SB, E], BF16)
        seen = sb(pa, "seen", [P, E], BF16)
        seen_add = sb(pa, "seen_add", [P, E], F32)
        late = sb(pa, "late", [P, SB, E], F32)
        slot0 = sb(pa, "slot0", [P, SB, E], F32)
        slot = sb(pa, "slot", [P, SB, E], F32)
        pslot = sb(pa, "pslot", [P, K, SB, E], F32)
        slotf = sb(pa, "slotf", [P, K, SB], F32)
        two_e = sb(pa, "two_e", [P, E], F32)
        many = sb(pa, "many", [P, E], F32)
        many_e = sb(pa, "many_e", [P, E], F32)
        flagf = sb(pa, "flagf", [P, 1], F32)
        lower = sb(pa, "lower", [P, E, E], F32)
        many_l = sb(pa, "many_l", [P, E, E], F32)
        pastf = sb(pa, "pastf", [P, E], F32)
        slotu = [sb(pa, f"slotu{i}", [P, K * SB], U32) for i in range(2)]
        pa.close()

        pc = top
        wh1 = sb(pc, "wh1", [P, NU, UNIT], F32R)
        wl1 = sb(pc, "wl1", [P, NU, UNIT], F32R)
        bXh = [sb(pc, f"bXh{i}", [P, DC, CAP], F32R) for i in range(2)]
        bXl = [sb(pc, f"bXl{i}", [P, DC, CAP], F32R) for i in range(2)]
        hH = [sb(pc, f"hH{c}", [P, FT, w], F32R) for c, (_, w) in enumerate(CHUNKS)]
        hL = [sb(pc, f"hL{c}", [P, FT, w], F32R) for c, (_, w) in enumerate(CHUNKS)]
        sil = [sb(pc, f"sil{i}", [P, 384], F32) for i in range(2)]
        hF = [sb(pc, f"hF{i}", [P, 384], F32) for i in range(2)]
        ysc = [sb(pc, f"ysc{i}", [P, CT, D], F32) for i in range(2)]
        Wh, Wl = [wh0, wh1], [wl0, wl1]

        bank = [top.enter_context(nc.psum_tensor(f"bank{i}", [P, 512], F32)) for i in range(8)]
        S, Tb, O = bank[0:2], bank[2:4], bank[4:6]
        Xo, Xp = bank[6], bank[7]
        Gb, Ub, Yb, Xc = bank[0:2], bank[2:4], bank[4:6], bank[6:8]

        ld_x = [sem(f"ld_x{i}") for i in range(SEQS // XP)]
        ld_ctx = [sem(f"ld_ctx{i}") for i in range(2)]
        ld_w, ld_c = sem("ld_w"), sem("ld_c")
        ld_pad, st_x2 = sem("ld_pad"), sem("st_x2")
        ld_st = [sem(f"ld_st{i}") for i in range(2)]
        ld_rows = [sem(f"ld_rows{i}") for i in range(2)]
        const_mem, pool_chain = sem("const_mem"), sem("pool_chain")
        pad_ok, ident_ok, const_ok, bias_ok = sem("pad_ok"), sem("ident_ok"), sem("const_ok"), sem("bias_ok")
        gates_ok, pool_ln1, pool_xbo = sem("gates_ok"), sem("pool_ln1"), sem("pool_xbo")
        dve_st, dve_mv1, dve_xn1 = sem("dve_st"), sem("dve_mv1"), sem("dve_xn1")
        pe_xT, act_xT, pe_q, act_q, pe_k, act_km = (sem(n) for n in ("pe_xT", "act_xT", "pe_q", "act_q", "pe_k", "act_km"))
        pe_v, dve_vf, act_v1, dve_vr, act_v2, dve_v3 = (sem(n) for n in ("pe_v", "dve_vf", "act_v1", "dve_vr", "act_v2", "dve_v3"))
        pe_s, dve_max, dve_sub, act_exp = (sem(n) for n in ("pe_s", "dve_max", "dve_sub", "act_exp"))
        pe_t, act_hi, dve_lo, pe_pv, dve_os, dve_rec, dve_on = (sem(n) for n in ("pe_t", "act_hi", "dve_lo", "pe_pv", "dve_os", "dve_rec", "dve_on"))
        pe_oT, act_oT, pe_y, dve_x2 = (sem(n) for n in ("pe_oT", "act_oT", "pe_y", "dve_x2"))
        dve_st2, dve_mv2, pool_rs2, dve_xc, pool_xg, pool_xr = (sem(n) for n in ("dve_st2", "dve_mv2", "pool_rs2", "dve_xc", "pool_xg", "pool_xr"))
        pe_x2T, act_x2T, pe_lg, dve_lg, dve_r, act_ex = (sem(n) for n in ("pe_x2T", "act_x2T", "pe_lg", "dve_lg", "dve_r", "act_ex"))
        dve_lgs, dve_mem, dve_wp, pe_rk, dve_rk, dve_idx = (sem(n) for n in ("dve_lgs", "dve_mem", "dve_wp", "pe_rk", "dve_rk", "dve_idx"))
        scattered = [sem(f"scattered{i}") for i in range(2)]
        pe_cnt, dve_cnt, flag_ok = sem("pe_cnt"), sem("dve_cnt"), sem("flag_ok")
        act_wh, dve_wl = sem("act_wh"), sem("dve_wl")
        pe_bT, act_bh, dve_bl = sem("pe_bT"), sem("act_bh"), sem("dve_bl")
        pe_gu, act_sil, dve_h, act_hh, dve_hl = (sem(n) for n in ("pe_gu", "act_sil", "dve_h", "act_hh", "dve_hl"))
        dve_passed, pool_passed = sem("dve_passed"), sem("pool_passed")
        pe_out, dve_ysc = sem("pe_out"), sem("dve_ysc")
        added, added2, expert_added = sem("added"), sem("added2"), sem("expert_added")

        xrows = x.rearrange("(i p) d -> p i d", p=P)
        xv = x_all[:, :].rearrange("p (i d) -> p i d", d=D)
        R_CHAIN = 9
        PIECES = 12
        QW = UNIT // 4

        def more_rows(flags, e):
            return ((flags >> e) & 1) > 0

        def x_tile(i):
            return x_all[:, bass.ds(i * D, D)]

        block = top.enter_context(nc.Block())

        @block.sync
        def _(sp):
            for s in range(SEQS // XP):
                sp.dma_start(xv[:, XP * s:XP * s + XP, :], xrows[:, XP * s:XP * s + XP, :]).then_inc(ld_x[s], 16)
                if s == 0:
                    sp.dma_start(wq[:, :, :], wqT.rearrange("(c p) o -> p c o", p=P)).then_inc(ld_w, 16)

            def load_ctx(n, par):
                sp.dma_start(cT[par][:, :, :], ctxT[:, bass.ds(n * SB * T, SB * T)].rearrange("(c p) t -> p c t", p=P))\
                  .then_inc(ld_ctx[par], 16)

            def load_stage(u, src):
                sp.dma_start(stage[u % 2][:, :], src).then_inc(ld_st[u % 2], 16)

            load_ctx(0, 0)
            for dst, src in ((wk, wkT), (wv, wvT), (wo, woT)):
                sp.dma_start(dst[:, :, :], src.rearrange("(c p) o -> p c o", p=P)).then_inc(ld_w, 16)
            sp.dma_start(wr[:, :, :], wrT.rearrange("(c p) e -> p c e", p=P)).then_inc(ld_w, 16)
            load_ctx(1, 1)
            sp.wait_ge(pad_ok, 1)
            sp.dma_start(buf.rearrange("(j p) w -> p j w", p=P),
                         padrow[:, :].unsqueeze(1).to_broadcast([P, E * CT, ROW])).then_inc(ld_pad, 16)
            sp.dma_start(out[TOKENS:TOKENS + P, :], zrow[:, :]).then_inc(ld_pad, 16)
            load_stage(0, w12T[0, 0:P, :])
            load_stage(1, w12T[0, P:2 * P, :])

            def store_x2(n):
                sp.wait_ge(dve_x2, SB * n + SB)
                sp.dma_start(out[0:TOKENS, :].rearrange("(i p) d -> p i d", p=P)[:, bass.ds(n * SB, SB), :],
                             x_all[:, bass.ds(n * SB * D, SB * D)].rearrange("p (i d) -> p i d", d=D)).then_inc(st_x2, 16)

            def turn(n, par):
                sp.wait_ge(pe_v, n - 1)
                load_ctx(n, par)
                store_x2(n - 2)

            with sp.Fori(0, NSB // 2 - 1) as i:
                turn(2 * i + 2, 0)
                turn(2 * i + 3, 1)
            store_x2(NSB - 2)
            store_x2(NSB - 1)

            def w3_piece(e):
                return w3T[e].rearrange("(f p) d -> p f d", p=P)

            def load_rows(e, par):
                sp.dma_start(rows[par][:, :, :], buf[bass.ds(e * CAP, CAP), :].rearrange("(c p) w -> p c w", p=P))\
                  .then_inc(ld_rows[par], 16)

            def load_weights(e, par, pieces):
                for k in pieces:
                    u = NU * e + k
                    s = (par + k) % 2
                    sp.wait_ge(act_wh, 4 * (u - 1))
                    sp.wait_ge(dve_wl, 4 * (u - 1))
                    if k < DC:
                        sp.dma_start(stage[s][:, :], w12T[e, k * P:(k + 1) * P, :] if isinstance(e, int)
                                     else w12T[bass.ds(e, 1), k * P:(k + 1) * P, :].rearrange("a p f -> p (a f)"))\
                          .then_inc(ld_st[s], 16)
                    else:
                        sp.dma_start(stage[s][:, :].rearrange("p (f d) -> p f d", d=D),
                                     w3_piece(e) if isinstance(e, int)
                                     else w3T[bass.ds(e, 1), :, :].rearrange("a (f p) d -> p (a f) d", p=P))\
                          .then_inc(ld_st[s], 16)

            load_weights(0, 0, (2,))
            for s in range(2):
                sp.wait_ge(scattered[s], 16 * K * SEQS // 2)
            load_rows(0, 0)

            def fetch(e, par):
                load_weights(e, par, (0, 1))
                if not (isinstance(e, int) and e < 2):
                    sp.wait_ge(expert_added, e - 1)
                load_rows(e, par)
                load_weights(e, par, (2,))

            fetch(1, 1)
            with sp.Fori(1, E // 2) as i:
                fetch(2 * i, 0)
                fetch(2 * i + 1, 1)

        @block.gpsimd
        def _(pool):
            chained = [0]

            def then(ins):
                chained[0] += 1
                ins.then_inc(pool_chain, 1)
                pool.wait_ge(pool_chain, chained[0])

            pool.memset(ident32[:, :], 0.0).then_inc(const_mem, 1)
            pool.memset(identb[:, :], 0.0).then_inc(const_mem, 1)
            pool.memset(causal[:, :, :], 0.0).then_inc(const_mem, 1)
            pool.memset(before[:, :], 1.0).then_inc(const_mem, 1)
            pool.memset(hmask[:, :], 1.0).then_inc(const_mem, 1)
            pool.memset(padrow[:, :], 0.0).then_inc(const_mem, 1)
            pool.memset(zrow[:, :], 0.0).then_inc(const_mem, 1)
            pool.memset(mhalf[:, :], -0.5).then_inc(const_mem, 1)
            pool.iota(iota_i[:, 0, :], pattern=[[1, E]], base=0, channel_multiplier=0).then_inc(const_mem, 1)
            pool.iota(iota_i[:, 1, :], pattern=[[CAP, E]], base=0, channel_multiplier=0).then_inc(const_mem, 1)
            pool.wait_ge(const_mem, 10)
            pool.affine_select(out=ident32[:, :], in_=ident32[:, :], compare_op=ALU.not_equal, fill=1.0, base=0,
                               pattern=[[-1, P]], channel_multiplier=1).then_inc(ident_ok, 1)
            pool.iota(padrow[:, D + E:ROW].bitcast(I32), pattern=[[1, 1]], base=TOKENS, channel_multiplier=1).then_inc(pad_ok, 1)

            def rstd1(a, b):
                pool.wait_ge(dve_mv1, b)
                then(pool.tensor_scalar(ve_all[:, a:b], mv_all[:, a:b, 1], EPS, None, ALU.add))
                pool.tensor_tensor(rs_all[:, a:b], ve_all[:, a:b], mhalf[:, a:b], ALU.pow).then_inc(pool_ln1, 1)

            pool.affine_select(out=identb[:, :], in_=identb[:, :], compare_op=ALU.not_equal, fill=1.0, base=0,
                               pattern=[[-1, P]], channel_multiplier=1).then_inc(const_ok, 1)
            pool.affine_select(out=causal[:, :, :], in_=causal[:, :, :], compare_op=ALU.is_ge, fill=NEG, base=0,
                               pattern=[[0, GH], [-1, T]], channel_multiplier=1).then_inc(const_ok, 1)
            pool.affine_select(out=before[:, :], in_=before[:, :], compare_op=ALU.is_ge, fill=0.0, base=-1,
                               pattern=[[1, P]], channel_multiplier=-1).then_inc(const_ok, 1)
            then(pool.affine_select(out=hmask[:, :], in_=hmask[:, :], compare_op=ALU.is_ge, fill=0.0, base=0,
                                    pattern=[[-HD, 8]], channel_multiplier=1))
            then(pool.affine_select(out=hmask[:, :], in_=hmask[:, :], compare_op=ALU.is_ge, fill=0.0, base=HD - 1,
                                    pattern=[[HD, 8]], channel_multiplier=-1))
            rstd1(0, XP)
            pool.memset(onesb[:, :], 1.0).then_inc(const_ok, 1)
            pool.memset(seen[:, :], 0.0).then_inc(const_ok, 1)
            pool.memset(pbias[:, :], PSCALE).then_inc(const_ok, 1)
            for v3 in V3:
                pool.memset(v3[:, :, :, 3 * HD:3 * HD + 1], 1.0).then_inc(const_ok, 1)
                pool.memset(v3[:, :, :, 3 * HD + 1:VW], 0.0).then_inc(const_ok, 1)
            for e in range(E):
                pool.memset(two_e[:, e:e + 1], float(2 ** e)).then_inc(const_ok, 1)
            pool.tensor_copy(iota8[:, :], iota_i[:, 0, :]).then_inc(const_ok, 1)
            pool.tensor_copy(ebase[:, :], iota_i[:, 1, :]).then_inc(const_ok, 1)
            for e in range(E):
                if e > 0:
                    pool.memset(lower[:, e, 0:e], 1.0).then_inc(const_ok, 1)
                pool.memset(lower[:, e, e:E], 0.0).then_inc(const_ok, 1)
            then(pool.iota(tokid[:, :], pattern=[[P, SEQS]], base=0, channel_multiplier=1))
            pool.wait_ge(ld_c, 16 * 8)
            pool.tensor_scalar(bq4[:, :], bqk[:, 0, :], HD ** -0.5, None, ALU.mult).then_inc(bias_ok, 1)
            for t in range(DC):
                pool.tensor_scalar(bkm[:, 8 * t:8 * t + 8], hmask[:, :], bqk[:, 1, t:t + 1], None, ALU.mult).then_inc(bias_ok, 1)
            rstd1(XP, SEQS)
            pool.wait_ge(gates_ok, 1)
            then(pool.tensor_scalar(tbo[:, :], bob[:, :], tg[:, 0:1], None, ALU.mult))

            def residual(n, par, prev1):
                if prev1:
                    pool.wait_ge(dve_x2, SB * n - SB)
                pool.tensor_tensor(xbo[par][:, :, :], x_all[:, bass.ds(n * SB * D, SB * D)].rearrange("p (i d) -> p i d", d=D),
                                   tbo[:, :].unsqueeze(1).to_broadcast([P, SB, D]), ALU.add).then_inc(pool_xbo, 1)

            def norm2(m):
                pool.wait_ge(dve_mv2, SB * m + SB).then_inc(pool_passed, 1)
                var = mv2[:, :, 1]
                c = [0]

                def link(ins):
                    c[0] += 1
                    ins.then_inc(pool_rs2, 1)
                    pool.wait_ge(pool_rs2, 7 * m + c[0]).then_inc(pool_passed, 1)

                link(pool.tensor_scalar(lnt[0][:, :], var, EPS, None, ALU.add))
                link(pool.tensor_tensor(lnt[1][:, :], lnt[0][:, :], mhalf[:, 0:SB], ALU.pow))
                link(pool.tensor_tensor(lnt[2][:, :], lnt[1][:, :], lnt[1][:, :], ALU.mult))
                link(pool.tensor_tensor(lnt[3][:, :], lnt[2][:, :], var, ALU.mult))
                link(pool.tensor_scalar(lnt[4][:, :], lnt[3][:, :], EPS, None, ALU.add))
                link(pool.tensor_tensor(lnt[5][:, :], lnt[4][:, :], mhalf[:, 0:SB], ALU.pow))
                pool.tensor_tensor(lnt[6][:, :], lnt[1][:, :], lnt[5][:, :], ALU.mult).then_inc(pool_rs2, 1)

            def affine2(m, mpar):
                pool.wait_ge(dve_xc, SB * m + SB)
                r = xr[mpar]
                pool.tensor_tensor(r[:, :, 0:D], r[:, :, 0:D], gab[:, :].unsqueeze(1).to_broadcast([P, SB, D]), ALU.mult)\
                    .then_inc(pool_xg, 1)
                pool.wait_ge(pool_xg, m + 1)
                pool.tensor_tensor(r[:, :, 0:D], r[:, :, 0:D], beb[:, :].unsqueeze(1).to_broadcast([P, SB, D]), ALU.add)\
                    .then_inc(pool_xr, 1)
                pool.tensor_copy(r[:, :, D + E:ROW].bitcast(I32), tokid[:, bass.ds(m * SB, SB)].unsqueeze(2)).then_inc(pool_xr, 1)

            def dispatch(m, mpar):
                pool.wait_ge(dve_wp, m + 1).then_inc(pool_passed, 1)
                pool.wait_ge(pool_xr, 2 * m + 2).then_inc(pool_passed, 1)
                pool.wait_ge(dve_idx, m + 1).then_inc(pool_passed, 1)
                for r in range(K):
                    for j in range(SB):
                        c = r * SB + j
                        pool.indirect_dma_start(out=buf, out_offset=bass.IndirectOffsetOnAxis(slotu[mpar][:, c:c + 1], 0),
                                                in_=xr[mpar][:, j, :], in_offset=None, bounds_check=E * CAP - 1,
                                                oob_is_err=False).then_inc(scattered[mpar], 16)

            def body(n, par, prev1, prev2, cur):
                if cur:
                    residual(n, par, prev1)
                if prev1:
                    norm2(n - 1)
                if prev1 and not cur:
                    affine2(n - 1, 1 - par)
                if prev2:
                    dispatch(n - 2, par)
                if prev1 and cur:
                    affine2(n - 1, 1 - par)

            for s in range(SEQS // XP):
                pool.wait_ge(ld_x[s], 16)
            pool.wait_ge(ld_pad, 32)
            body(0, 0, False, False, True)
            body(1, 1, True, False, True)
            with pool.Fori(1, NSB // 2) as i:
                body(2 * i, 0, True, True, True)
                body(2 * i + 1, 1, True, True, True)
            body(NSB, 0, True, True, False)
            body(NSB + 1, 1, False, True, False)

            pool.wait_ge(st_x2, 16 * NSB)

            pool.wait_ge(flag_ok, 2)
            flags = pool.value_load(flag[0:1, 0:1], min_val=0, max_val=2 ** E - 1)

            def add_tile(e, par, c, done):
                pool.wait_ge(dve_ysc, CT * e + c + 1).then_inc(pool_passed, 1)
                pool.indirect_dma_start(out=out, out_offset=bass.IndirectOffsetOnAxis(rows[par][:, c, D + E:ROW].bitcast(U32), 0),
                                        in_=ysc[par][:, c, :], in_offset=None, bounds_check=TOKENS + P - 1,
                                        oob_is_err=True, compute_op=ALU.add).then_inc(done, 16)

            def add_rows(e, par):
                for c in range(CT0):
                    add_tile(e, par, c, added)
                    if c < CT0 - 1:
                        pool.wait_ge(added, 16 * (CT0 * e + c + 1)).then_inc(pool_passed, 1)
                before_e = pool.value_load(past[0:1, bass.ds(e, 1)], min_val=0, max_val=E - 1)
                with pool.If(more_rows(flags, e)):
                    pool.wait_ge(added, 16 * CT0 * (e + 1)).then_inc(pool_passed, 1)
                    for c in range(CT0, CT):
                        add_tile(e, par, c, added2)
                        if c < CT - 1:
                            pool.wait_ge(added2, 16 * ((CT - CT0) * before_e + c + 1 - CT0)).then_inc(pool_passed, 1)
                    pool.wait_ge(added2, 16 * (CT - CT0) * (before_e + 1)).then_inc(expert_added, 1)
                with pool.Else():
                    pool.wait_ge(added, 16 * CT0 * (e + 1)).then_inc(expert_added, 1)

            add_rows(0, 0)
            add_rows(1, 1)
            with pool.Fori(1, E // 2) as i:
                add_rows(2 * i, 0)
                add_rows(2 * i + 1, 1)
            pool.wait_ge(expert_added, E)

        @block.scalar
        def _(act):
            act.dma_start(gate[:, 0:1], g_xattn.partition_broadcast(P)).then_inc(ld_c, 16)
            act.dma_start(gate[:, 1:2], g_ffn.partition_broadcast(P)).then_inc(ld_c, 16)
            act.dma_start(bqk[:, 0, :], bq).then_inc(ld_c, 16)
            act.dma_start(bqk[:, 1, :], bk).then_inc(ld_c, 16)
            for dst, src in ((bvb, bv), (bob, bo), (gab, gamma), (beb, beta)):
                act.dma_start(dst[:, :], src.partition_broadcast(P)).then_inc(ld_c, 16)
            act.wait_ge(ld_c, 16 * 8)
            act.activation(tg[:, :], gate[:, :], ACT.Tanh).then_inc(gates_ok, 1)

            def exps_of_logits(m):
                act.wait_ge(dve_lgs, m + 1)
                act.activation(lex[:, :, :], lgs[:, :, :], ACT.Exp).then_inc(act_ex, 1)

            def x2_columns(m):
                act.wait_ge(pe_x2T, m + 1)
                act.activation(xnT[:, :, :], Xo[:, :].rearrange("p (c t) -> p c t", c=DC), ACT.Copy).then_inc(act_x2T, 1)

            def input_columns(n):
                act.wait_ge(pe_xT, n + 1)
                act.activation(xT[:, :, :], Xp[:, :].rearrange("p (c t) -> p c t", c=DC), ACT.Copy).then_inc(act_xT, 1)

            def queries(n, par):
                act.wait_ge(pe_q, n + 1)
                for t in range(DC):
                    ins = act.activation(qT[par][:, t, :], Xp[:, t * SB * T:(t + 1) * SB * T], ACT.Identity,
                                         bias=bq4[:, t:t + 1], scale=HD ** -0.5)
                ins.then_inc(act_q, 1)

            def head_keys(n, par, heads):
                for h in heads:
                    t = h // 8
                    if h == 0:
                        act.wait_ge(pe_k, n + 1)
                    act.activation(kM[par][:, h, :], Xp[:, t * SB * T:(t + 1) * SB * T], ACT.Identity,
                                   bias=bkm[:, h:h + 1], scale=hmask[:, h % 8:h % 8 + 1]).then_inc(act_km, 1)

            def values1(n, par):
                act.wait_ge(dve_vf, n + 1)
                act.activation(V3[par][:, :, :, 0:HD], vf[:, :, :].rearrange("p b (h d) -> p b h d", d=HD), ACT.Copy).then_inc(act_v1, 1)

            def values2(n, par):
                act.wait_ge(dve_vr, n + 1)
                act.activation(V3[par][:, :, :, HD:2 * HD], vr[:, :, :].rearrange("p b (h d) -> p b h d", d=HD), ACT.Copy).then_inc(act_v2, 1)

            def output_columns(i):
                act.wait_ge(pe_oT, i + 1)
                act.activation(oT[:, :, :], Xo[:, 0:D].rearrange("p (c t) -> p c t", c=DC), ACT.Copy).then_inc(act_oT, 1)

            def exps(G, g, early):
                act.wait_ge(dve_sub, G + 1)
                if not early:
                    act.wait_ge(pe_t, G - 1)
                act.activation(p32[g % 2][:, :, :], sS[g % 2][:, :, :], ACT.Exp, bias=pbias[:, 0:1]).then_inc(act_exp, 1)

            def high_probs(G, g, early):
                act.wait_ge(pe_t, G + 1)
                if not early:
                    act.wait_ge(pe_pv, G - 1)
                act.activation(pT[g % 2][:, 0, :, :], Tb[g % 2][:, :].rearrange("p (h t) -> p h t", h=GH), ACT.Copy).then_inc(act_hi, 1)

            def body(n, par, prev1, prev2, cur, nxt):
                for g in range(NG):
                    G = NG * n + g
                    if (cur and g > 0) or (prev1 and g == 0):
                        high_probs(G - 1, (g - 1) % 2, not prev1 and g < 3)
                    if cur:
                        exps(G, g, not prev1 and g < 2)
                    if g == 0 and nxt:
                        input_columns(n + 1)
                    if g == 0 and prev2:
                        x2_columns(n - 2)
                    if g == 0 and cur:
                        values2(n, par)
                    if g == 1 and nxt:
                        queries(n + 1, 1 - par)
                    if g == 2 and prev2:
                        exps_of_logits(n - 2)
                    if g == 2 and prev1:
                        output_columns(SB * (n - 1) + 1)
                    if g in KEY_STEPS and nxt:
                        head_keys(n + 1, 1 - par, KEY_STEPS[g])
                    if g == 6 and cur:
                        output_columns(SB * n)
                    if g == 7 and nxt:
                        values1(n + 1, 1 - par)

            act.wait_ge(ident_ok, 1)
            input_columns(0)
            act.wait_ge(bias_ok, 3)
            queries(0, 0)
            head_keys(0, 0, range(H))
            act.wait_ge(const_ok, CONSTS)
            values1(0, 0)
            body(0, 0, False, False, True, True)
            body(1, 1, True, False, True, True)
            with act.Fori(1, NSB // 2 - 1) as i:
                body(2 * i, 0, True, True, True, True)
                body(2 * i + 1, 1, True, True, True, True)
            body(NSB - 2, 0, True, True, True, True)
            body(NSB - 1, 1, True, True, True, False)
            body(NSB, 0, True, True, False, False)
            body(NSB + 1, 1, False, True, False, False)

            def stage_uses(i, par, k):
                s = (par + k) % 2
                return 3 * i + sum(1 for pp_, kk in ((0, 0), (0, 1), (0, 2), (1, 0), (1, 1), (1, 2))
                                   if (pp_ + kk) % 2 == s and (pp_, kk) <= (par, k))

            def high(i, par, q12):
                k, q = q12 // 4, q12 % 4
                s = (par + k) % 2
                if q == 0:
                    act.wait_ge(ld_st[s], 16 * stage_uses(i, par, k))
                act.activation(Wh[par][:, k, q * QW:(q + 1) * QW], stage[s][:, q * QW:(q + 1) * QW], ACT.Copy)\
                    .then_inc(act_wh, 1)

            def rows_high(e, par, a):
                c, d = a // 2, a % 2
                o, w = CHUNKS[c]
                act.wait_ge(pe_bT, 4 * e + a + 1)
                act.activation(bXh[par][:, d, o:o + w], Xc[a % 2][:, 0:w], ACT.Copy).then_inc(act_bh, 1)

            def hidden_high(e, j):
                c, f = j // FT, j % FT
                w = CHUNKS[c][1]
                act.wait_ge(dve_h, 16 * e + j + 1)
                act.activation(hH[c][:, f, :], hF[j % 2][:, 0:w], ACT.Copy).then_inc(act_hh, 1)

            for q12 in range(PIECES):
                high(0, 0, q12)
            for a in range(4):
                rows_high(0, 0, a)

            act.wait_ge(flag_ok, 1)
            flags = act.value_load(flag[0:1, 0:1], min_val=0, max_val=2 ** E - 1)

            def steps(i, par, c, last, first):
                e = 2 * i + par
                w = CHUNKS[c][1]
                for f in range(FT + 1):
                    j = c * FT + f
                    if f < FT:
                        act.wait_ge(pe_gu, 16 * e + j + 1)
                        if not first or j >= 2:
                            act.wait_ge(dve_h, 16 * e + j - 1)
                        act.activation(sil[j % 2][:, 0:w], Gb[j % 2][:, 0:w], ACT.Silu).then_inc(act_sil, 1)
                    if f >= 1:
                        if j == 1 and not first:
                            act.wait_ge(pe_out, CT * e)
                        hidden_high(e, j - 1)
                    if c == 0 and f < FT and not last:
                        high(i + par, 1 - par, f)

            def expert(i, par, last, first):
                e = 2 * i + par
                steps(i, par, 0, last, first)
                if not last:
                    for k in range(2):
                        high(i + par, 1 - par, FT + 2 * k)
                        high(i + par, 1 - par, FT + 2 * k + 1)
                        rows_high(e + 1, 1 - par, 2 * k)
                        rows_high(e + 1, 1 - par, 2 * k + 1)
                with act.If(more_rows(flags, e)):
                    steps(i, par, 1, last, first)
                with act.Else():
                    act.wait_ge(act_sil, 16 * e + FT).then_inc(act_sil, FT)
                    act.wait_ge(act_hh, 16 * e + FT).then_inc(act_hh, FT)

            expert(0, 0, False, True)
            expert(0, 1, False, False)
            with act.Fori(1, E // 2 - 1) as i:
                expert(i, 0, False, False)
                expert(i, 1, False, False)
            expert(E // 2 - 1, 0, False, False)
            expert(E // 2 - 1, 1, True, False)

        @block.vector
        def _(dve):
            def stats1(a, b):
                for i in range(a, b):
                    if i % XP == 0:
                        dve.wait_ge(ld_x[i // XP], 16)
                    dve.bn_stats(st_all[:, i, :], xv[:, i, :]).then_inc(dve_st, 1)
                for i in range(a, b):
                    dve.wait_ge(dve_st, i + 1)
                    dve.bn_aggr(mv_all[:, i, :], st_all[:, i, :]).then_inc(dve_mv1, 1)

            def normalize_inputs(n):
                for j in range(SB):
                    i = SB * n + j
                    dve.tensor_scalar(xn1[:, j, :], x_tile(i), mv_all[:, bass.ds(i, 1), 0], rs_all[:, bass.ds(i, 1)],
                                      ALU.subtract, ALU.mult).then_inc(dve_xn1, 1)

            hv = "p b (h d) -> p b h d"

            def values0(n):
                dve.wait_ge(pe_v, n + 1)
                dve.tensor_tensor(vf[:, :, :], Xp[:, :].rearrange("p (b d) -> p b d", d=D),
                                  bvb[:, :].unsqueeze(1).to_broadcast([P, SB, D]), ALU.add).then_inc(dve_vf, 1)

            def values1(n, par):
                dve.wait_ge(act_v1, n + 1)
                for b in range(SB):
                    ins = dve.tensor_tensor(vr[:, b, :].rearrange("p (h d) -> p h d", d=HD),
                                            vf[:, b, :].rearrange("p (h d) -> p h d", d=HD), V3[par][:, b, :, 0:HD], ALU.subtract)
                ins.then_inc(dve_vr, 1)

            def values2(n, par):
                dve.wait_ge(act_v2, n + 1)
                for b in range(SB):
                    ins = dve.tensor_tensor(V3[par][:, b, :, 2 * HD:3 * HD], vr[:, b, :].rearrange("p (h d) -> p h d", d=HD),
                                            V3[par][:, b, :, HD:2 * HD], ALU.subtract)
                ins.then_inc(dve_v3, 1)

            def stats2(m):
                for j in range(SB):
                    dve.wait_ge(dve_x2, SB * m + j + 1)
                    dve.bn_stats(st2[:, j, :], x_tile(SB * m + j)).then_inc(dve_st2, 1)
                for j in range(SB):
                    dve.wait_ge(dve_st2, SB * m + j + 1).then_inc(dve_passed, 1)
                    dve.bn_aggr(mv2[:, j, :], st2[:, j, :]).then_inc(dve_mv2, 1)

            def normalize2(m, mpar, reuse):
                dve.wait_ge(pool_rs2, 7 * m + 7)
                if reuse is not None:
                    dve.wait_ge(scattered[mpar], 16 * K * SB * reuse)
                for j in range(SB):
                    dve.tensor_scalar(xr[mpar][:, j, 0:D], x_tile(SB * m + j), mv2[:, j, 0:1], lnt[6][:, j:j + 1],
                                      ALU.subtract, ALU.mult).then_inc(dve_xc, 1)

            def logits(m):
                dve.wait_ge(pe_lg, m + 1)
                dve.tensor_scalar(lgc[:, :, :], Xo[:, 0:SB * E].rearrange("p (j e) -> p j e", e=E), -CLAMP, CLAMP, ALU.max, ALU.min)\
                   .then_inc(dve_lg, 1)
                dve.wait_ge(dve_lg, m + 1)
                dve.tensor_reduce(lmx[:, :], lgc[:, :, :], AX_X, ALU.max).then_inc(dve_r, 1)
                dve.wait_ge(dve_r, R_CHAIN * m + 1)
                dve.tensor_tensor(lgs[:, :, :], lgc[:, :, :], lmx[:, :].unsqueeze(2).to_broadcast([P, SB, E]), ALU.subtract)\
                   .then_inc(dve_lgs, 1)

            def route(m, mpar):
                c = [1]

                def link(ins, alone=False):
                    c[0] += 1
                    ins.then_inc(dve_r, 1)
                    if alone:
                        dve.wait_ge(dve_r, R_CHAIN * m + c[0]).then_inc(dve_passed, 1)
                    else:
                        dve.wait_ge(dve_r, R_CHAIN * m + c[0])

                dve.wait_ge(act_ex, m + 1)
                link(dve.tensor_reduce(lsm[:, :], lex[:, :, :], AX_X, ALU.add))
                link(dve.tensor_scalar(lse[:, :], lsm[:, :], 1e-12, None, ALU.add))
                link(dve.reciprocal(lrc[:, :], lse[:, :]))
                link(dve.tensor_tensor(prob[:, :, :], lex[:, :, :], lrc[:, :].unsqueeze(2).to_broadcast([P, SB, E]), ALU.mult), alone=True)
                for j in range(SB):
                    ins = dve.max(top8[:, j, :], prob[:, j, :])
                link(ins, alone=True)
                for j in range(SB):
                    ins = dve.max_index(topi[:, j, :], top8[:, j, :], prob[:, j, :])
                link(ins)
                link(dve.tensor_copy(ixf[:, :, :], topi[:, :, 0:K].rearrange("p j r -> p r j")))
                link(dve.tensor_tensor(pick[:, :, :, :], iota8[:, :].unsqueeze(1).unsqueeze(1).to_broadcast([P, K, SB, E]),
                                       ixf[:, :, :].unsqueeze(3).to_broadcast([P, K, SB, E]), ALU.is_equal))
                dve.tensor_tensor(member[:, :, :], pick[:, 0, :, :], pick[:, 1, :, :], ALU.add).then_inc(dve_mem, 1)
                dve.tensor_scalar(xr[mpar][:, :, D:D + E], prob[:, :, :], tg[:, 1:2], None, ALU.mult).then_inc(dve_wp, 1)

            def slots(m, mpar):
                dve.wait_ge(pe_rk, m + 1)
                rk = Xo[:, 0:SB * E].rearrange("p (j e) -> p j e", e=E)
                dve.tensor_scalar(late[:, :, :], rk, float(CAP), LATE, ALU.is_ge, ALU.mult).then_inc(dve_rk, 1)
                dve.tensor_tensor(slot0[:, :, :], rk, ebase[:, :].unsqueeze(1).to_broadcast([P, SB, E]), ALU.add).then_inc(dve_rk, 1)
                dve.tensor_reduce(seen_add[:, :], member[:, :, :].rearrange("p j e -> p e j"), AX_X, ALU.add).then_inc(dve_rk, 1)
                dve.wait_ge(dve_rk, 6 * m + 3)
                dve.tensor_tensor(slot[:, :, :], slot0[:, :, :], late[:, :, :], ALU.add).then_inc(dve_rk, 1)
                dve.tensor_tensor(seen[:, :], seen[:, :], seen_add[:, :], ALU.add)
                dve.wait_ge(dve_rk, 6 * m + 4)
                dve.tensor_tensor(pslot[:, :, :, :], pick[:, :, :, :], slot[:, :, :].unsqueeze(1).to_broadcast([P, K, SB, E]), ALU.mult)\
                   .then_inc(dve_rk, 1)
                dve.wait_ge(dve_rk, 6 * m + 5)
                dve.tensor_reduce(slotf[:, :, :], pslot[:, :, :, :], AX_X, ALU.add).then_inc(dve_rk, 1)
                dve.wait_ge(dve_rk, 6 * m + 6)
                dve.tensor_copy(slotu[mpar][:, :], slotf[:, :, :].rearrange("p r j -> p (r j)")).then_inc(dve_idx, 1)

            def largest(G, g):
                dve.wait_ge(pe_s, G + 1)
                dve.tensor_reduce(nm[g % 2][:, :], S[g % 2][:, :].rearrange("p (h t) -> p h t", t=T), AX_X, ALU.max)\
                   .then_inc(dve_max, 1)

            def shift(G, g, early):
                dve.wait_ge(dve_max, G + 1)
                if not early:
                    dve.wait_ge(act_exp, G - 1)
                dve.tensor_tensor(sS[g % 2][:, :, :], S[g % 2][:, :].rearrange("p (h t) -> p h t", t=T),
                                  nm[g % 2][:, :].unsqueeze(2).to_broadcast([P, GH, T]), ALU.subtract).then_inc(dve_sub, 1)

            def low_probs(G, g):
                dve.wait_ge(act_hi, G + 1)
                dve.tensor_tensor(pT[g % 2][:, 1, :, :], Tb[g % 2][:, :].rearrange("p (h t) -> p h t", h=GH), pT[g % 2][:, 0, :, :],
                                  ALU.subtract).then_inc(dve_lo, 1)

            def heads_out(kk, k, early):
                ob = O[k % 2][:, 0:8 * VW].rearrange("p (h w) -> p h w", w=VW)
                dve.wait_ge(pe_pv, 2 * kk + 2)
                if not early:
                    dve.wait_ge(dve_on, kk)
                dve.tensor_reduce(osum[:, :, :], ob[:, :, 0:3 * HD].rearrange("p h (c d) -> p h d c", d=HD), AX_X, ALU.add)\
                   .then_inc(dve_os, 1)
                dve.reciprocal(orec[:, :], ob[:, :, 3 * HD]).then_inc(dve_rec, 1)
                dve.wait_ge(dve_os, kk + 1)
                dve.wait_ge(dve_rec, kk + 1)
                return ob

            def heads_scale(kk, k, seq_before):
                if k % 2 == 0 and seq_before is not None:
                    dve.wait_ge(pe_oT, seq_before + 1)
                dve.tensor_tensor(oN[:, (k % 2) * P:(k % 2 + 1) * P].rearrange("p (h d) -> p h d", d=HD), osum[:, :, :],
                                  orec[:, :].unsqueeze(2).to_broadcast([P, 8, HD]), ALU.mult).then_inc(dve_on, 1)

            def gated(n, par, b):
                i = SB * n + b
                dve.wait_ge(pe_y, i + 1)
                dve.wait_ge(pool_xbo, n + 1)
                dve.scalar_tensor_tensor(x_tile(i), Xo[:, 0:D], tg[:, 0:1], xbo[par][:, b, :], ALU.mult, ALU.add).then_inc(dve_x2, 1)

            def body(half, par, prev1, prev2, cur, nxt, prev3):
                n = 2 * half + par
                HPS = 2 * SB
                for g in range(NG):
                    G = NG * n + g
                    if g == 0 and nxt:
                        normalize_inputs(n + 1)
                    if cur:
                        largest(G, g)
                        shift(G, g, not prev1 and g < 2)
                    if (cur and g > 0) or (prev1 and g == 0):
                        low_probs(G - 1, (g - 1) % 2)
                    if g == 0 and cur:
                        values2(n, par)
                    if g == 1 and prev1:
                        heads_out(HPS * n - 1, HPS - 1, False)
                        heads_scale(HPS * n - 1, HPS - 1, None)
                    if g == 2 and prev2:
                        logits(n - 2)
                    if g == 3 and prev1:
                        gated(n - 1, 1 - par, 1)
                    if g == 3 and prev2:
                        route(n - 2, par)
                    if g in (3, 5, 7) and cur:
                        k = (g - 3) // 2
                        heads_out(HPS * n + k, k, not prev1 and k == 0)
                        heads_scale(HPS * n + k, k, SB * n - 1 + k // 2 if prev1 or k > 0 else None)
                    if g == 4 and prev1:
                        stats2(n - 1)
                    if g == 5 and prev2:
                        slots(n - 2, par)
                    if g == 6 and prev1:
                        normalize2(n - 1, 1 - par, half - 1 + par if prev3 else None)
                    if g == 6 and nxt:
                        values0(n + 1)
                    if g == 7 and nxt:
                        values1(n + 1, 1 - par)
                    if g == 7 and cur:
                        gated(n, par, 0)

            stats1(0, XP)
            dve.wait_ge(pool_ln1, 1)
            normalize_inputs(0)
            stats1(XP, SEQS)
            dve.wait_ge(ld_c, 16 * 8)
            values0(0)
            values1(0, 0)
            dve.wait_ge(gates_ok, 1)
            dve.wait_ge(const_ok, CONSTS)
            dve.wait_ge(pool_ln1, 2)
            body(0, 0, False, False, True, True, False)
            body(0, 1, True, False, True, True, False)
            body(1, 0, True, True, True, True, False)
            body(1, 1, True, True, True, True, True)
            with dve.Fori(2, NSB // 2 - 1) as i:
                body(i, 0, True, True, True, True, True)
                body(i, 1, True, True, True, True, True)
            body(NSB // 2 - 1, 0, True, True, True, True, True)
            body(NSB // 2 - 1, 1, True, True, True, False, True)
            body(NSB // 2, 0, True, True, False, False, True)
            body(NSB // 2, 1, False, True, False, False, True)

            dve.wait_ge(pe_cnt, 1)
            dve.tensor_scalar(many[:, :], Xo[:, 0:E], float(CHUNKS[0][1]), None, ALU.is_gt).then_inc(dve_cnt, 1)
            dve.wait_ge(dve_cnt, 1)
            dve.tensor_tensor(many_e[:, :], many[:, :], two_e[:, :], ALU.mult).then_inc(dve_cnt, 1)
            dve.wait_ge(dve_cnt, 2)
            dve.tensor_reduce(flagf[:, :], many_e[:, :], AX_X, ALU.add).then_inc(dve_cnt, 1)
            dve.wait_ge(dve_cnt, 3)
            dve.tensor_copy(flag[:, :], flagf[:, :]).then_inc(flag_ok, 1)
            dve.tensor_tensor(many_l[:, :, :], many[:, :].unsqueeze(1).to_broadcast([P, E, E]), lower[:, :, :], ALU.mult).then_inc(dve_cnt, 1)
            dve.wait_ge(dve_cnt, 4)
            dve.tensor_reduce(pastf[:, :], many_l[:, :, :], AX_X, ALU.add).then_inc(dve_cnt, 1)
            dve.wait_ge(dve_cnt, 5)
            dve.tensor_copy(past[:, :], pastf[:, :]).then_inc(flag_ok, 1)

            def stage_uses(i, par, k):
                s = (par + k) % 2
                return 3 * i + sum(1 for pp_, kk in ((0, 0), (0, 1), (0, 2), (1, 0), (1, 1), (1, 2))
                                   if (pp_ + kk) % 2 == s and (pp_, kk) <= (par, k))

            def low(i, par, q12):
                k, q = q12 // 4, q12 % 4
                s = (par + k) % 2
                if q == 0:
                    dve.wait_ge(ld_st[s], 16 * stage_uses(i, par, k))
                dve.wait_ge(act_wh, PIECES * (2 * i + par) + q12 + 1)
                cols = slice(q * QW, (q + 1) * QW)
                dve.tensor_tensor(Wl[par][:, k, cols], stage[s][:, cols], Wh[par][:, k, cols].bitcast(F32), ALU.subtract)\
                   .then_inc(dve_wl, 1)

            def rows_low(e, par, a):
                c, d = a // 2, a % 2
                o, w = CHUNKS[c]
                dve.wait_ge(act_bh, 4 * e + a + 1)
                dve.tensor_tensor(bXl[par][:, d, o:o + w], Xc[a % 2][:, 0:w], bXh[par][:, d, o:o + w].bitcast(F32), ALU.subtract)\
                   .then_inc(dve_bl, 1)

            for q12 in range(PIECES):
                low(0, 0, q12)
            for a in range(4):
                rows_low(0, 0, a)

            dve.wait_ge(flag_ok, 1)
            flags = dve.value_load(flag[0:1, 0:1], min_val=0, max_val=2 ** E - 1)

            def steps(i, par, c, last, first):
                e = 2 * i + par
                w = CHUNKS[c][1]
                for f in range(FT + 1):
                    j = c * FT + f
                    if f < FT:
                        dve.wait_ge(act_sil, 16 * e + j + 1)
                        if not first or j >= 2:
                            dve.wait_ge(act_hh, 16 * e + j - 1)
                            dve.wait_ge(dve_hl, 16 * e + j - 1)
                        dve.tensor_tensor(hF[j % 2][:, 0:w], sil[j % 2][:, 0:w], Ub[j % 2][:, 0:w], ALU.mult).then_inc(dve_h, 1)
                    if f >= 1:
                        jj = j - 1
                        dve.wait_ge(act_hh, 16 * e + jj + 1)
                        dve.tensor_tensor(hL[c][:, f - 1, :], hF[jj % 2][:, 0:w], hH[c][:, f - 1, :].bitcast(F32), ALU.subtract)\
                           .then_inc(dve_hl, 1)
                    if c == 0 and f < FT and not last:
                        low(i + par, 1 - par, f)

            def weigh(e, par, t, first):
                if t == 0 and not (isinstance(e, int) and e < 2):
                    dve.wait_ge(expert_added, e - 1)
                dve.wait_ge(pe_out, CT * e + t + 1)
                dve.tensor_scalar(ysc[par][:, t, :], Yb[(par + t) % 2][:, 0:D], rows[par][:, t, bass.ds(D + e, 1)], None, ALU.mult)\
                   .then_inc(dve_ysc, 1)

            def expert(i, par, last, first):
                e = 2 * i + par
                steps(i, par, 0, last, first)
                for t in range(CT0):
                    if t < 2 and not last:
                        low(i + par, 1 - par, FT + 2 * t)
                        low(i + par, 1 - par, FT + 2 * t + 1)
                    weigh(e, par, t, first)
                    if t < 2 and not last:
                        rows_low(e + 1, 1 - par, 2 * t)
                        rows_low(e + 1, 1 - par, 2 * t + 1)
                with dve.If(more_rows(flags, e)):
                    steps(i, par, 1, last, first)
                    for t in range(CT0, CT):
                        weigh(e, par, t, first)
                with dve.Else():
                    dve.wait_ge(dve_h, 16 * e + FT).then_inc(dve_h, FT)
                    dve.wait_ge(dve_hl, 16 * e + FT).then_inc(dve_hl, FT)
                    dve.wait_ge(dve_ysc, CT * e + CT0).then_inc(dve_ysc, CT - CT0)

            expert(0, 0, False, True)
            expert(0, 1, False, False)
            with dve.Fori(1, E // 2 - 1) as i:
                expert(i, 0, False, False)
                expert(i, 1, False, False)
            expert(E // 2 - 1, 0, False, False)
            expert(E // 2 - 1, 1, True, False)

        @block.tensor
        def _(pe):
            def input_columns(n, first):
                pe.wait_ge(dve_xn1, SB * n + SB)
                if not first:
                    pe.wait_ge(dve_vf, n)
                for c in range(DC):
                    for j in range(SB):
                        ins = nc.tensor.transpose(Xp[:, (c * SB + j) * T:(c * SB + j + 1) * T], xn1[:, j, c * P:(c + 1) * P], ident32[:, :])
                ins.then_inc(pe_xT, 1)

            def queries(n):
                pe.wait_ge(act_xT, n + 1)
                for t in range(DC):
                    for c in range(DC):
                        ins = nc.tensor.matmul(Xp[:, t * SB * T:(t + 1) * SB * T], wq[:, c, t * P:(t + 1) * P], xT[:, c, :],
                                               start=(c == 0), stop=(c == DC - 1))
                ins.then_inc(pe_q, 1)

            def keys(n, par, use):
                pe.wait_ge(ld_ctx[par], 16 * use)
                pe.wait_ge(act_q, n + 1)
                for t in range(DC):
                    for c in range(DC):
                        ins = nc.tensor.matmul(Xp[:, t * SB * T:(t + 1) * SB * T], wk[:, c, t * P:(t + 1) * P], cT[par][:, c, :],
                                               start=(c == 0), stop=(c == DC - 1))
                ins.then_inc(pe_k, 1)

            def values(n, par):
                pe.wait_ge(act_km, H * n + H)
                for b in range(SB):
                    for c in range(DC):
                        ins = nc.tensor.matmul(Xp[:, b * D:(b + 1) * D], cT[par][:, c, b * T:(b + 1) * T], wv[:, c, :],
                                               start=(c == 0), stop=(c == DC - 1))
                ins.then_inc(pe_v, 1)

            def x2_columns(m, mpar):
                pe.wait_ge(pool_xr, 2 * m + 1)
                for c in range(DC):
                    for j in range(SB):
                        ins = nc.tensor.transpose(Xo[:, (c * SB + j) * T:(c * SB + j + 1) * T], xr[mpar][:, j, c * P:(c + 1) * P], ident32[:, :])
                ins.then_inc(pe_x2T, 1)

            def logits(m):
                pe.wait_ge(act_x2T, m + 1)
                for j in range(SB):
                    for c in range(DC):
                        ins = nc.tensor.matmul(Xo[:, j * E:(j + 1) * E], xnT[:, c, j * T:(j + 1) * T], wr[:, c, :],
                                               start=(c == 0), stop=(c == DC - 1))
                ins.then_inc(pe_lg, 1)

            def ranks(m):
                pe.wait_ge(dve_mem, m + 1)
                rk = Xo[:, 0:SB * E].rearrange("p (j e) -> p j e", e=E)
                nc.tensor.matmul(rk, before[:, :], member[:, :, :], start=True, stop=False)
                for j in range(1, SB):
                    nc.tensor.matmul(rk[:, j:SB, :], onesb[:, :], member[:, 0:SB - j, :], start=False, stop=False)
                nc.tensor.matmul(rk, onesb[:, :], seen[:, :].unsqueeze(1).to_broadcast([P, SB, E]), start=False, stop=True)\
                    .then_inc(pe_rk, 1)

            def scores(G, g, n, par, early):
                b, hq = g // GPS, g % GPS
                if b == 0:
                    pe.wait_ge(act_km, H * n + GH * hq + GH)
                if not early:
                    pe.wait_ge(dve_sub, G - 1)
                nc.tensor.matmul(S[g % 2][:, :], identb[:, :], causal[:, :, :], start=True, stop=False)
                nc.tensor.matmul(S[g % 2][:, :], qT[par][:, hq // 2, b * T:(b + 1) * T], kM[par][:, GH * hq:GH * hq + GH, b * T:(b + 1) * T],
                                 start=False, stop=True).then_inc(pe_s, 1)

            def prob_columns(G, g, early):
                pe.wait_ge(act_exp, G + 1)
                if not early:
                    pe.wait_ge(dve_lo, G - 1)
                for h in range(GH):
                    ins = nc.tensor.transpose(Tb[g % 2][:, h * T:(h + 1) * T], p32[g % 2][:, h, :], ident32[:, :])
                ins.then_inc(pe_t, 1)

            def weigh_values(G, g, n, par, early):
                b, hq, k = g // GPS, g % GPS, g // 2
                if g == 0:
                    pe.wait_ge(dve_v3, n + 1)
                if g % 2 == 0 and not early:
                    pe.wait_ge(dve_on, 2 * SB * n + k - 1)
                pe.wait_ge(dve_lo, G + 1)
                for h in range(GH):
                    o = ((g % 2) * GH + h) * VW
                    for s in range(2):
                        ins = nc.tensor.matmul(O[k % 2][:, o:o + VW], pT[g % 2][:, s, h, :], V3[par][:, b, GH * hq + h, :],
                                               start=(s == 0), stop=(s == 1))
                ins.then_inc(pe_pv, 1)

            def output_columns(i):
                pe.wait_ge(dve_on, 2 * i + 2)
                for c in range(DC):
                    ins = nc.tensor.transpose(Xo[:, c * T:(c + 1) * T], oN[:, c * P:(c + 1) * P], ident32[:, :])
                ins.then_inc(pe_oT, 1)

            def project_out(i):
                pe.wait_ge(act_oT, i + 1)
                for c in range(DC):
                    ins = nc.tensor.matmul(Xo[:, 0:D], oT[:, c, :], wo[:, c, :], start=(c == 0), stop=(c == DC - 1))
                ins.then_inc(pe_y, 1)

            def body(n, par, prev1, prev2, cur, nxt, use):
                for g in range(NG):
                    G = NG * n + g
                    if cur:
                        scores(G, g, n, par, not prev1 and g < 2)
                    if (cur and g > 0) or (prev1 and g == 0):
                        prob_columns(G - 1, (g - 1) % 2, not prev1 and g < 3)
                    if nxt:
                        if g == 0:
                            input_columns(n + 1, False)
                        elif g == 1:
                            queries(n + 1)
                        elif g == 2:
                            keys(n + 1, 1 - par, use)
                        elif g == 6:
                            values(n + 1, 1 - par)
                    if g == 0 and prev2:
                        if prev1:
                            pe.wait_ge(dve_x2, SB * n - 1)
                        else:
                            pe.wait_ge(dve_rk, 6 * (n - 2))
                        x2_columns(n - 2, par)
                    elif g == 1 and prev2:
                        logits(n - 2)
                    elif g == 2 and prev1:
                        if prev2:
                            pe.wait_ge(dve_lg, n - 1)
                        else:
                            pe.wait_ge(dve_x2, SB * n - 1)
                        output_columns(SB * n - 1)
                    elif g == 3 and prev1:
                        project_out(SB * n - 1)
                    elif g == 5 and prev2:
                        if prev1:
                            pe.wait_ge(dve_x2, SB * n)
                        ranks(n - 2)
                    elif g == 6 and cur:
                        if prev2:
                            pe.wait_ge(dve_rk, 6 * (n - 2) + 2)
                        elif prev1:
                            pe.wait_ge(dve_x2, SB * n)
                        output_columns(SB * n)
                    elif g == 7 and cur:
                        project_out(SB * n)
                    if cur and g >= 2:
                        weigh_values(G - 2, g - 2, n, par, not prev1 and g < 6)
                    elif prev1 and g < 2:
                        weigh_values(G - 2, NG + g - 2, n - 1, 1 - par, False)

            pe.wait_ge(ident_ok, 1)
            input_columns(0, True)
            pe.wait_ge(ld_w, 16 * 5)
            queries(0)
            keys(0, 0, 1)
            values(0, 0)
            pe.wait_ge(const_ok, CONSTS)
            body(0, 0, False, False, True, True, 1)
            body(1, 1, True, False, True, True, 2)
            with pe.Fori(1, NSB // 2 - 1) as i:
                body(2 * i, 0, True, True, True, True, i + 1)
                body(2 * i + 1, 1, True, True, True, True, i + 2)
            body(NSB - 2, 0, True, True, True, True, NSB // 2)
            body(NSB - 1, 1, True, True, True, False, None)
            body(NSB, 0, True, True, False, False, None)
            body(NSB + 1, 1, False, True, False, False, None)

            pe.wait_ge(dve_idx, NSB)
            nc.tensor.matmul(Xo[:, 0:E], onesb[:, :], seen[:, :], start=True, stop=True).then_inc(pe_cnt, 1)

            def rows_columns(e, par, use, a):
                if a == 0:
                    pe.wait_ge(ld_rows[par], 16 * use)
                c, d = a // 2, a % 2
                o, w = CHUNKS[c]
                if isinstance(e, int) and e == 0 and a < 2:
                    pe.wait_ge(dve_cnt, 1)
                else:
                    pe.wait_ge(dve_bl, 4 * e + a - 1)
                for t in range(w // P):
                    ins = nc.tensor.transpose(Xc[a % 2][:, t * P:(t + 1) * P], rows[par][:, o // P + t, d * P:(d + 1) * P], ident32[:, :])
                ins.then_inc(pe_bT, 1)

            def three(out_ap, parts, start, stop):
                (ah, al), (bh, bl) = parts
                nc.tensor.matmul(out_ap, ah, bh, start=start, stop=False)
                nc.tensor.matmul(out_ap, ah, bl, start=False, stop=False)
                return nc.tensor.matmul(out_ap, al, bh, start=False, stop=stop)

            for a in range(4):
                rows_columns(0, 0, 1, a)

            pe.wait_ge(flag_ok, 1)
            flags = pe.value_load(flag[0:1, 0:1], min_val=0, max_val=2 ** E - 1)

            def up(i, par, c, first):
                e = 2 * i + par
                o, w = CHUNKS[c]
                for f in range(FT):
                    j = c * FT + f
                    if f == 0:
                        pe.wait_ge(dve_bl, 4 * e + 2 * c + 2)
                    if not first or j >= 2:
                        pe.wait_ge(dve_h, 16 * e + j - 1)
                    for half, dst in ((0, Gb), (1, Ub)):
                        fo = half * FF + f * P
                        for d in range(DC):
                            ins = three(dst[j % 2][:, 0:w],
                                        ((Wh[par][:, d, fo:fo + P], Wl[par][:, d, fo:fo + P]),
                                         (bXh[par][:, d, o:o + w], bXl[par][:, d, o:o + w])), d == 0, d == DC - 1)
                    ins.then_inc(pe_gu, 1)

            def down(e, par, c, t, first):
                o = t * P - CHUNKS[c][0]
                if not first or t >= 2:
                    pe.wait_ge(dve_ysc, CT * e + t - 1)
                for f in range(FT):
                    if o == 0:
                        pe.wait_ge(dve_hl, 16 * e + FT * c + f + 1)
                    ins = three(Yb[(par + t) % 2][:, 0:D],
                                ((hH[c][:, f, o:o + P], hL[c][:, f, o:o + P]),
                                 (Wh[par][:, DC, f * D:(f + 1) * D], Wl[par][:, DC, f * D:(f + 1) * D])), f == 0, f == FT - 1)
                ins.then_inc(pe_out, 1)

            def expert(i, par, last, first):
                e = 2 * i + par
                pe.wait_ge(dve_wl, PIECES * e + PIECES)
                up(i, par, 0, first)
                for t in range(CT0):
                    down(e, par, 0, t, first)
                    if t < 2 and not last:
                        rows_columns(e + 1, 1 - par, i + 1 + par, 2 * t)
                        rows_columns(e + 1, 1 - par, i + 1 + par, 2 * t + 1)
                with pe.If(more_rows(flags, e)):
                    up(i, par, 1, first)
                    for t in range(CT0, CT):
                        down(e, par, 1, t, first)
                with pe.Else():
                    pe.wait_ge(pe_gu, 16 * e + FT).then_inc(pe_gu, FT)
                    pe.wait_ge(pe_out, CT * e + CT0).then_inc(pe_out, CT - CT0)

            expert(0, 0, False, True)
            expert(0, 1, False, False)
            with pe.Fori(1, E // 2 - 1) as i:
                expert(i, 0, False, False)
                expert(i, 1, False, False)
            expert(E // 2 - 1, 0, False, False)
            expert(E // 2 - 1, 1, True, False)


def kernel(**inputs):
    import numpy as _np
    import concourse.bacc as _bacc
    from concourse import mybir as _mybir
    from concourse.bass_utils import run_bass_kernel_spmd as _run

    a = {k: _np.asarray(v) for k, v in inputs.items()}
    flat = a["x"].reshape(TOKENS, D)
    ops = {
        "x": flat,
        "ctxT": a["ctx_1024"].reshape(TOKENS, D).T,
        "g_xattn": a["g_xattn"],
        "g_ffn": a["g_ffn"],
        "wqT": a["L0_xattn_wq"].T, "bq": a["L0_xattn_bq"].reshape(DC, P).T,
        "wkT": a["L0_xattn_wk"].T, "bk": a["L0_xattn_bk"].reshape(DC, P).T,
        "wvT": a["L0_xattn_wv"].T, "bv": a["L0_xattn_bv"],
        "woT": a["L0_xattn_wo"].T, "bo": a["L0_xattn_bo"],
        "gamma": a["L0_ffn_ln_gamma"], "beta": a["L0_ffn_ln_beta"],
        "wrT": a["L0_ffn_Wr"].T,
        "w12T": a["L0_ffn_W12"].transpose(0, 2, 1),
        "w3T": a["L0_ffn_W3"].transpose(0, 2, 1),
    }
    nc = _bacc.Bacc("TRN2", target_bir_lowering=False, num_devices=1)
    arrays, args = {}, []
    for name, v in ops.items():
        v = _np.ascontiguousarray(v)
        arrays[f"in_{name}"] = v
        args.append(nc.dram_tensor(f"in_{name}", v.shape, _mybir.dt.from_np(v.dtype), kind="ExternalInput").ap())
    args.append(nc.dram_tensor("out_tokens", (TOKENS + P, D), _mybir.dt.float32, kind="ExternalOutput").ap())
    gated_block(nc, *args)
    r = _run(nc, [arrays], core_ids=[0])
    return r.results[0]["out_tokens"][:TOKENS].reshape(SEQS, T, D)
```

```python
from contextlib import ExitStack

import concourse.bass as bass
from concourse import mybir

F32 = mybir.dt.float32
F32R = mybir.dt.float32r
BF16 = mybir.dt.bfloat16
F16 = mybir.dt.float16
I32 = mybir.dt.int32
U32 = mybir.dt.uint32
ALU = mybir.AluOpType
ACT = mybir.ActivationFunctionType
AX_X = mybir.AxisListType.X

P = 128
SEQS, T, D = 16, 128, 256
H, HD = 16, 16
DC = D // P
SB = 2
XCUT = (0, 2, 6, 11, 16)
NSB = SEQS // SB
GH = 4
GPS = H // GH
NG = SB * GPS
E, K, FF = 8, 2, 1024
TOKENS = SEQS * T
CAP = -(-(-(-TOKENS * K * 5 // 4)) // E)
CT = CAP // P
ROW = D + E + 1
CHUNKS = ((0, 384), (384, 256))
FT = FF // P
CT0 = CHUNKS[0][1] // P
UNIT = 2048
NU = 3
VW = 3 * HD + 2
NEG = -3.0e38
PSCALE = 9.704060527839234
EPS = 1e-5
CLAMP = 10000.0
CONSTS = 11 + 3 * E - 1
HR = P // HD
KM = 16 * HR // 2
LATE = 1.0e6


def gated_block(nc, x, ctxT, gates, biases, wqT, wkT, wvT, woT, bo, gamma, beta, wrT, w12T, w3T, out):
    with ExitStack() as top:
        def sem(name):
            return top.enter_context(nc.semaphore(name))

        def sb(stack, name, shape, dt):
            return stack.enter_context(nc.sbuf_tensor(name, shape, dt))

        buf = nc.dram_tensor("expert_rows", (E * CAP, ROW), F32).ap()

        ident32 = sb(top, "ident32", [P, P], F32)
        stage = [sb(top, f"stage{i}", [P, UNIT], F32) for i in range(2)]
        flag = sb(top, "flag", [P, 1], I32)
        past = sb(top, "past", [P, E], I32)
        rows = [sb(top, f"rows{i}", [P, CT, ROW], F32) for i in range(2)]

        pa = ExitStack()
        kM = [sb(pa, f"kM{i}", [P, 2, H, SB * T], F32R) for i in range(2)]
        x_all = sb(pa, "x_all", [P, SEQS * D], F32)
        st_all = sb(pa, "st_all", [P, SEQS, 6], F32)
        mv_all = sb(pa, "mv_all", [P, SEQS, 2], F32)
        rs_all = sb(pa, "rs_all", [P, SEQS], F32)
        ve_all = sb(pa, "ve_all", [P, SEQS], F32)
        xn1 = sb(pa, "xn1", [P, SB, D], F32)
        cT = [sb(pa, f"cT{i}", [P, DC, SB * T], F32) for i in range(2)]
        xT = sb(pa, "xT", [P, DC, SB * T], F32)
        qT = sb(pa, "qT", [P, DC, SB * T], F32)
        q2 = [sb(pa, f"q2_{i}", [P, 2, DC, SB * T], F32R) for i in range(2)]
        kT = sb(pa, "kT", [P, DC, SB * T], F32)
        k2 = sb(pa, "k2", [P, 2, DC, SB * T], F32R)
        vf = sb(pa, "vf", [P, SB, D], F32)
        vr = vf
        V3 = [sb(pa, f"V3_{i}", [P, SB, H, VW], BF16) for i in range(2)]
        nm = [sb(pa, f"nm{i}", [P, GH], F32) for i in range(2)]
        nb = [sb(pa, f"nb{i}", [P, GH], F32) for i in range(2)]
        p32 = [sb(pa, f"p32_{i}", [P, GH, T], F32) for i in range(2)]
        pT = [sb(pa, f"pT{i}", [P, 2, GH, T], F16) for i in range(2)]
        osum = sb(pa, "osum", [P, 8, HD], F32)
        orec = sb(pa, "orec", [P, 8], F32)
        oN = sb(pa, "oN", [P, D], F32)
        oT = sb(pa, "oT", [P, DC, T], F32)
        xbo = [sb(pa, f"xbo{i}", [P, SB, D], F32) for i in range(2)]
        wq = sb(pa, "wq", [P, DC, D], F32)
        wk = sb(pa, "wk", [P, DC, D], F32)
        wv = sb(pa, "wv", [P, DC, D], F32)
        wo = sb(pa, "wo", [P, DC, D], F32)
        wr = sb(pa, "wr", [P, DC, E], F32)
        bqkv = sb(pa, "bqkv", [P, 3, DC], F32)
        bq4 = sb(pa, "bq4", [P, DC], F32)
        bob = sb(pa, "bob", [P, D], F32)
        tbo = sb(pa, "tbo", [P, D], F32)
        gab = sb(pa, "gab", [P, D], F32)
        beb = sb(pa, "beb", [P, D], F32)
        gate = sb(pa, "gate", [P, 2], F32)
        tg = sb(pa, "tg", [P, 2], F32)
        identb = sb(pa, "identb", [P, P], BF16)
        causal = sb(pa, "causal", [P, GH, T], BF16)
        before = sb(pa, "before", [P, P], BF16)
        onesb = sb(pa, "onesb", [P, P], BF16)
        iota_i = sb(pa, "iota_i", [P, 2, E], I32)
        iota8 = sb(pa, "iota8", [P, E], F32)
        ebase = sb(pa, "ebase", [P, E], F32)
        tokid = sb(pa, "tokid", [P, SEQS], I32)
        padrow = sb(pa, "padrow", [P, ROW], F32)
        zrow = sb(pa, "zrow", [P, D], F32)
        mhalf = sb(pa, "mhalf", [P, SEQS], F32)
        xr = [sb(pa, f"xr{i}", [P, SB, ROW], F32) for i in range(2)]
        xnT = sb(pa, "xnT", [P, DC, SB * T], F32)
        st2 = sb(pa, "st2", [P, SB, 6], F32)
        mv2 = sb(pa, "mv2", [P, SB, 2], F32)
        lnv = sb(pa, "lnv", [P, SB], F32)
        lnr = sb(pa, "lnr", [P, SB], F32)
        lgc = sb(pa, "lgc", [P, SB, E], F32)
        lgs = sb(pa, "lgs", [P, SB, E], F32)
        lmx = sb(pa, "lmx", [P, SB], F32)
        lex = sb(pa, "lex", [P, SB, E], F32)
        lsm = sb(pa, "lsm", [P, SB], F32)
        lse = sb(pa, "lse", [P, SB], F32)
        lrc = sb(pa, "lrc", [P, SB], F32)
        prob = sb(pa, "prob", [P, SB, E], F32)
        top8 = sb(pa, "top8", [P, SB, 8], F32)
        topi = sb(pa, "topi", [P, SB, 8], U32)
        ixf = sb(pa, "ixf", [P, K, SB], F32)
        pick = sb(pa, "pick", [P, K, SB, E], F32)
        member = sb(pa, "member", [P, SB, E], BF16)
        seen = sb(pa, "seen", [P, E], BF16)
        seen_add = sb(pa, "seen_add", [P, E], F32)
        late = sb(pa, "late", [P, SB, E], F32)
        slot0 = sb(pa, "slot0", [P, SB, E], F32)
        slot = sb(pa, "slot", [P, SB, E], F32)
        pslot = sb(pa, "pslot", [P, K, SB, E], F32)
        slotf = sb(pa, "slotf", [P, K, SB], F32)
        two_e = sb(pa, "two_e", [P, E], F32)
        many = sb(pa, "many", [P, E], F32)
        many_e = sb(pa, "many_e", [P, E], F32)
        flagf = sb(pa, "flagf", [P, 1], F32)
        lower = sb(pa, "lower", [P, E, E], F32)
        many_l = sb(pa, "many_l", [P, E, E], F32)
        pastf = sb(pa, "pastf", [P, E], F32)
        slotu = [sb(pa, f"slotu{i}", [P, K * SB], U32) for i in range(2)]
        pa.close()

        pc = top
        wh0 = sb(pc, "wh0", [P, NU, UNIT], F32R)
        wl0 = sb(pc, "wl0", [P, NU, UNIT], F32R)
        wh1 = sb(pc, "wh1", [P, NU, UNIT], F32R)
        wl1 = sb(pc, "wl1", [P, NU, UNIT], F32R)
        bXh = [sb(pc, f"bXh{i}", [P, DC, CAP], F32R) for i in range(2)]
        bXl = [sb(pc, f"bXl{i}", [P, DC, CAP], F32R) for i in range(2)]
        hH = [sb(pc, f"hH{c}", [P, FT, w], F32R) for c, (_, w) in enumerate(CHUNKS)]
        hL = [sb(pc, f"hL{c}", [P, FT, w], F32R) for c, (_, w) in enumerate(CHUNKS)]
        sil = [sb(pc, f"sil{i}", [P, 384], F32) for i in range(2)]
        hF = [sb(pc, f"hF{i}", [P, 384], F32) for i in range(2)]
        ysc = [sb(pc, f"ysc{i}", [P, CT, D], F32) for i in range(2)]
        Wh, Wl = [wh0, wh1], [wl0, wl1]

        bank = [top.enter_context(nc.psum_tensor(f"bank{i}", [P, 512], F32)) for i in range(8)]
        S, Tb, O = bank[0:2], bank[2:4], bank[4:6]
        Xo, Xp = bank[6], bank[7]
        K0, Q0 = bank[4:6]
        Gb, Ub, Yb, Xc = bank[0:2], bank[2:4], bank[4:6], bank[6:8]

        ld_x = [sem(f"ld_x{i}") for i in range(len(XCUT) - 1)]
        ld_ctx = [sem(f"ld_ctx{i}") for i in range(2)]
        ld_wq, ld_wk, ld_wv, ld_wo, ld_wr = (sem(n) for n in ("ld_wq", "ld_wk", "ld_wv", "ld_wo", "ld_wr"))
        ld_b, ld_g, ld_c = sem("ld_b"), sem("ld_g"), sem("ld_c")
        ld_pad, st_x2 = sem("ld_pad"), sem("st_x2")
        ld_st = [sem(f"ld_st{i}") for i in range(2)]
        ld_rows = [sem(f"ld_rows{i}") for i in range(2)]
        ld_rows_rest = sem("ld_rows_rest")
        const_mem, pool_chain = sem("const_mem"), sem("pool_chain")
        pad_ok, ident_ok, const_ok, bias_ok = sem("pad_ok"), sem("ident_ok"), sem("const_ok"), sem("bias_ok")
        gates_ok, pool_ln1, pool_xbo = sem("gates_ok"), sem("pool_ln1"), sem("pool_xbo")
        dve_st, dve_mv1, dve_xn1 = sem("dve_st"), sem("dve_mv1"), sem("dve_xn1")
        pool_xc, pool_xn1 = sem("pool_xc"), sem("pool_xn1")
        pe_xT, act_xT, pe_q, act_q, pe_k, act_kT = (sem(n) for n in ("pe_xT", "act_xT", "pe_q", "act_q", "pe_k", "act_kT"))
        act_q32, act_k32, pool_kl, pool_ql = (sem(n) for n in ("act_q32", "act_k32", "pool_kl", "pool_ql"))
        km_zero, ld_km = [sem("km_zero0"), sem("km_zero1")], [sem("ld_km0"), sem("ld_km1")]
        pe_v, pe_bo, dve_bo, act_vf, act_v1, pool_vr, act_v2, pool_v3 = (sem(n) for n in ("pe_v", "pe_bo", "dve_bo", "act_vf", "act_v1", "pool_vr", "act_v2", "pool_v3"))
        pe_s, dve_max, dve_bias, act_exp = (sem(n) for n in ("pe_s", "dve_max", "dve_bias", "act_exp"))
        pe_t, act_hi, dve_lo, pe_pv, dve_os, dve_rec, dve_on = (sem(n) for n in ("pe_t", "act_hi", "dve_lo", "pe_pv", "dve_os", "dve_rec", "dve_on"))
        pe_oT, act_oT, pe_y, dve_x2 = (sem(n) for n in ("pe_oT", "act_oT", "pe_y", "dve_x2"))
        dve_st2, dve_mv2, pool_rs2, pool_xg, pool_xr, dve_xg, dve_xr, pool_tok = (sem(n) for n in (
            "dve_st2", "dve_mv2", "pool_rs2", "pool_xg", "pool_xr", "dve_xg", "dve_xr", "pool_tok"))
        pe_x2T, act_x2T, pe_lg, dve_lg, dve_r, act_ex = (sem(n) for n in ("pe_x2T", "act_x2T", "pe_lg", "dve_lg", "dve_r", "act_ex"))
        dve_lgs, dve_mem, dve_wp, pe_rk, dve_rk, dve_idx = (sem(n) for n in ("dve_lgs", "dve_mem", "dve_wp", "pe_rk", "dve_rk", "dve_idx"))
        scattered = [sem(f"scattered{i}") for i in range(2)]
        pe_cnt, dve_cnt, flag_ok = sem("pe_cnt"), sem("dve_cnt"), sem("flag_ok")
        act_wh, dve_wl = sem("act_wh"), sem("dve_wl")
        pe_bT, act_bh, dve_bl = sem("pe_bT"), sem("act_bh"), sem("dve_bl")
        pe_gu, act_sil, dve_h, act_hh, dve_hl = (sem(n) for n in ("pe_gu", "act_sil", "dve_h", "act_hh", "dve_hl"))
        dve_passed, pool_passed = sem("dve_passed"), sem("pool_passed")
        pe_out, dve_ysc = sem("pe_out"), sem("dve_ysc")
        added, added2, expert_added = sem("added"), sem("added2"), sem("expert_added")

        xrows = x.rearrange("(i p) d -> p i d", p=P)
        xv = x_all[:, :].rearrange("p (i d) -> p i d", d=D)
        R_CHAIN = 9
        PIECES = 12
        QW = UNIT // 4

        def more_rows(flags, e):
            return ((flags >> e) & 1) > 0

        def x_tile(i):
            return x_all[:, bass.ds(i * D, D)]

        block = top.enter_context(nc.Block())

        @block.sync
        def _(sp):
            def load_x(s):
                a, b = XCUT[s], XCUT[s + 1]
                sp.dma_start(xv[:, a:b, :], xrows[:, a:b, :]).then_inc(ld_x[s], 16)

            def load_w(dst, src, done):
                sp.dma_start(dst[:, :, :], src.rearrange("(c p) o -> p c o", p=P)).then_inc(done, 16)

            def load_ctx(n, par):
                sp.dma_start(cT[par][:, :, :], ctxT[:, bass.ds(n * SB * T, SB * T)].rearrange("(c p) t -> p c t", p=P))\
                  .then_inc(ld_ctx[par], 16)

            def load_stage(u, src):
                sp.dma_start(stage[u % 2][:, :], src).then_inc(ld_st[u % 2], 16)

            load_ctx(0, 0)
            load_w(wk, wkT, ld_wk)
            load_x(0)
            load_w(wv, wvT, ld_wv)
            load_w(wq, wqT, ld_wq)
            load_w(wo, woT, ld_wo)
            for s in range(1, len(XCUT) - 1):
                load_x(s)
            load_w(wr, wrT, ld_wr)
            for dst, src in ((bob, bo), (gab, gamma), (beb, beta)):
                sp.dma_start(dst[:, :], src.partition_broadcast(P)).then_inc(ld_c, 16)
            load_ctx(1, 1)

            def spread_keys(n, par):
                sp.wait_ge(pool_kl, n + 1)
                for a in range(HR):
                    r = slice(a * HD, (a + 1) * HD)
                    sp.dma_start(kM[par][r, :, a:H:HR, :].bitcast(F32), k2[r, :, :, :].bitcast(F32)).then_inc(ld_km[a // GH], 16)

            def pad(experts):
                for e in experts:
                    sp.dma_start(buf[e * CAP:(e + 1) * CAP, :].rearrange("(j p) w -> p j w", p=P),
                                 padrow[:, :].unsqueeze(1).to_broadcast([P, CT, ROW])).then_inc(ld_pad, 16)

            sp.wait_ge(km_zero[0], 4)
            spread_keys(0, 0)
            sp.wait_ge(pad_ok, 1)
            sp.wait_ge(const_mem, 9)
            pad(range(E // 2))
            sp.wait_ge(km_zero[1], 3)
            spread_keys(1, 1)

            def store_x2(n):
                sp.wait_ge(dve_x2, SB * n + SB)
                sp.dma_start(out[0:TOKENS, :].rearrange("(i p) d -> p i d", p=P)[:, bass.ds(n * SB, SB), :],
                             x_all[:, bass.ds(n * SB * D, SB * D)].rearrange("p (i d) -> p i d", d=D)).then_inc(st_x2, 16)

            def turn(n, par):
                sp.wait_ge(pe_v, n - 1)
                load_ctx(n, par)
                if isinstance(n, int) and n == 2:
                    pad(range(E // 2, E))
                    sp.dma_start(out[TOKENS:TOKENS + P, :], zrow[:, :]).then_inc(ld_pad, 16)
                spread_keys(n, par)
                store_x2(n - 2)

            turn(2, 0)
            with sp.Fori(1, NSB // 2 - 1) as i:
                turn(2 * i + 1, 1)
                turn(2 * i + 2, 0)
            turn(NSB - 1, 1)
            load_stage(0, w12T[0, 0:P, :])
            load_stage(1, w12T[0, P:2 * P, :])
            store_x2(NSB - 2)
            store_x2(NSB - 1)

            def w3_piece(e):
                return w3T[e].rearrange("(f p) d -> p f d", p=P)

            def load_rows(e, par):
                sp.dma_start(rows[par][:, :, :], buf[bass.ds(e * CAP, CAP), :].rearrange("(c p) w -> p c w", p=P))\
                  .then_inc(ld_rows[par], 16)

            def load_weights(e, par, pieces):
                for k in pieces:
                    u = NU * e + k
                    s = (par + k) % 2
                    sp.wait_ge(act_wh, 4 * (u - 1))
                    sp.wait_ge(dve_wl, 4 * (u - 1))
                    if k < DC:
                        sp.dma_start(stage[s][:, :], w12T[e, k * P:(k + 1) * P, :] if isinstance(e, int)
                                     else w12T[bass.ds(e, 1), k * P:(k + 1) * P, :].rearrange("a p f -> p (a f)"))\
                          .then_inc(ld_st[s], 16)
                    else:
                        sp.dma_start(stage[s][:, :].rearrange("p (f d) -> p f d", d=D),
                                     w3_piece(e) if isinstance(e, int)
                                     else w3T[bass.ds(e, 1), :, :].rearrange("a (f p) d -> p (a f) d", p=P))\
                          .then_inc(ld_st[s], 16)

            load_weights(0, 0, (2,))
            for s in range(2):
                sp.wait_ge(scattered[s], 16 * K * SEQS // 2)
            for (o, w), done in zip(CHUNKS, (ld_rows[0], ld_rows_rest)):
                sp.dma_start(rows[0][:, o // P:(o + w) // P, :], buf[o:o + w, :].rearrange("(c p) w -> p c w", p=P)).then_inc(done, 16)

            def fetch(e, par):
                load_weights(e, par, (0, 1))
                if not (isinstance(e, int) and e < 2):
                    sp.wait_ge(expert_added, e - 1)
                load_rows(e, par)
                load_weights(e, par, (2,))

            fetch(1, 1)
            with sp.Fori(1, E // 2) as i:
                fetch(2 * i, 0)
                fetch(2 * i + 1, 1)

        @block.gpsimd
        def _(pool):
            chained = [0]

            def then(ins):
                chained[0] += 1
                ins.then_inc(pool_chain, 1)
                pool.wait_ge(pool_chain, chained[0])

            pool.memset(ident32[:, :], 0.0).then_inc(const_mem, 1)
            pool.memset(identb[:, :], 0.0).then_inc(const_mem, 1)
            pool.memset(causal[:, :, :], 0.0).then_inc(const_mem, 1)
            pool.memset(before[:, :], 1.0).then_inc(const_mem, 1)
            pool.memset(padrow[:, :], 0.0).then_inc(const_mem, 1)
            pool.memset(zrow[:, :], 0.0).then_inc(const_mem, 1)
            pool.memset(mhalf[:, :], -0.5).then_inc(const_mem, 1)
            pool.iota(iota_i[:, 0, :], pattern=[[1, E]], base=0, channel_multiplier=0).then_inc(const_mem, 1)
            pool.iota(iota_i[:, 1, :], pattern=[[CAP, E]], base=0, channel_multiplier=0).then_inc(const_mem, 1)
            pool.wait_ge(const_mem, 9)
            pool.affine_select(out=ident32[:, :], in_=ident32[:, :], compare_op=ALU.not_equal, fill=1.0, base=0,
                               pattern=[[-1, P]], channel_multiplier=1).then_inc(ident_ok, 1)
            pool.iota(padrow[:, D + E:ROW].bitcast(I32), pattern=[[1, 1]], base=TOKENS, channel_multiplier=1).then_inc(pad_ok, 1)

            def keys_low(n):
                pool.wait_ge(act_kT, n + 1)
                pool.tensor_tensor(k2[:, 1, :, :], kT[:, :, :], k2[:, 0, :, :].bitcast(F32), ALU.subtract).then_inc(pool_kl, 1)

            def queries_low(n, par):
                pool.wait_ge(act_q, n + 1)
                pool.tensor_tensor(q2[par][:, 1, :, :], qT[:, :, :], q2[par][:, 0, :, :].bitcast(F32), ALU.subtract).then_inc(pool_ql, 1)

            def rstd1(a, b):
                pool.wait_ge(dve_mv1, b)
                then(pool.tensor_scalar(ve_all[:, a:b], mv_all[:, a:b, 1], EPS, None, ALU.add))
                pool.tensor_tensor(rs_all[:, a:b], ve_all[:, a:b], mhalf[:, a:b], ALU.pow).then_inc(pool_ln1, 1)

            pool.affine_select(out=identb[:, :], in_=identb[:, :], compare_op=ALU.not_equal, fill=1.0, base=0,
                               pattern=[[-1, P]], channel_multiplier=1).then_inc(const_ok, 1)
            pool.affine_select(out=causal[:, :, :], in_=causal[:, :, :], compare_op=ALU.is_ge, fill=NEG, base=0,
                               pattern=[[0, GH], [-1, T]], channel_multiplier=1).then_inc(const_ok, 1)
            pool.affine_select(out=before[:, :], in_=before[:, :], compare_op=ALU.is_ge, fill=0.0, base=-1,
                               pattern=[[1, P]], channel_multiplier=-1).then_inc(const_ok, 1)
            rstd1(0, SB)
            pool.wait_ge(ld_b, 16)
            pool.tensor_scalar(bq4[:, :], bqkv[:, 0, :], HD ** -0.5, None, ALU.mult).then_inc(bias_ok, 1)
            pool.memset(onesb[:, :], 1.0).then_inc(const_ok, 1)
            pool.memset(seen[:, :], 0.0).then_inc(const_ok, 1)
            for v3 in V3:
                pool.memset(v3[:, :, :, 3 * HD:3 * HD + 1], 1.0).then_inc(const_ok, 1)
                pool.memset(v3[:, :, :, 3 * HD + 1:VW], 0.0).then_inc(const_ok, 1)
            for e in range(E):
                pool.memset(two_e[:, e:e + 1], float(2 ** e)).then_inc(const_ok, 1)
            pool.tensor_copy(iota8[:, :], iota_i[:, 0, :]).then_inc(const_ok, 1)
            pool.tensor_copy(ebase[:, :], iota_i[:, 1, :]).then_inc(const_ok, 1)
            for e in range(E):
                if e > 0:
                    pool.memset(lower[:, e, 0:e], 1.0).then_inc(const_ok, 1)
                pool.memset(lower[:, e, e:E], 0.0).then_inc(const_ok, 1)
            then(pool.iota(tokid[:, :], pattern=[[P, SEQS]], base=0, channel_multiplier=1))
            keys_low(0)
            rstd1(*XCUT[1:3])

            vh = "p b (h d) -> p b h d"

            def values_rest(n, par):
                pool.wait_ge(act_v1, n + 1)
                pool.tensor_tensor(vr[:, :, :].rearrange(vh, d=HD), vf[:, :, :].rearrange(vh, d=HD), V3[par][:, :, :, 0:HD], ALU.subtract)\
                    .then_inc(pool_vr, 1)

            def values_third(n, par):
                pool.wait_ge(act_v2, n + 1)
                pool.tensor_tensor(V3[par][:, :, :, 2 * HD:3 * HD], vr[:, :, :].rearrange(vh, d=HD), V3[par][:, :, :, HD:2 * HD], ALU.subtract)\
                    .then_inc(pool_v3, 1)

            def residual(n, par, prev1):
                if prev1:
                    pool.wait_ge(dve_x2, SB * n - SB)
                pool.tensor_tensor(xbo[par][:, :, :], x_all[:, bass.ds(n * SB * D, SB * D)].rearrange("p (i d) -> p i d", d=D),
                                   tbo[:, :].unsqueeze(1).to_broadcast([P, SB, D]), ALU.add).then_inc(pool_xbo, 1)

            def normalize_inputs(n):
                pool.wait_ge(pe_xT, n)
                seqs = bass.ds(n * SB, SB)
                pool.tensor_tensor(xn1[:, :, :], x_all[:, bass.ds(n * SB * D, SB * D)].rearrange("p (i d) -> p i d", d=D),
                                   mv_all[:, seqs, 0].unsqueeze(2).to_broadcast([P, SB, D]), ALU.subtract).then_inc(pool_xc, 1)
                pool.wait_ge(pool_xc, n - 1)
                pool.tensor_tensor(xn1[:, :, :], xn1[:, :, :], rs_all[:, seqs].unsqueeze(2).to_broadcast([P, SB, D]), ALU.mult)\
                    .then_inc(pool_xn1, 1)

            def norm2(m, j):
                i = SB * m + j
                pool.wait_ge(dve_mv2, i + 1).then_inc(pool_passed, 1)
                pool.tensor_scalar(lnv[:, j:j + 1], mv2[:, j, 1:2], 1.0 + EPS, EPS * EPS, ALU.mult, ALU.add).then_inc(pool_rs2, 1)
                pool.wait_ge(pool_rs2, 2 * i + 1)
                pool.tensor_tensor(lnr[:, j:j + 1], lnv[:, j:j + 1], mhalf[:, 0:1], ALU.pow).then_inc(pool_rs2, 1)

            def normalize2(m, mpar, j, reuse):
                i = SB * m + j
                if j == 0 and reuse is not None:
                    pool.wait_ge(scattered[mpar], 16 * K * SB * reuse)
                r = xr[mpar][:, j, 0:D]
                pool.tensor_tensor(r, x_tile(i), mv2[:, j, 0:1].to_broadcast([P, D]), ALU.subtract).then_inc(pool_xg, 1)
                pool.wait_ge(pool_rs2, 2 * i + 2)
                pool.wait_ge(pool_xg, 3 * i + 1)
                pool.tensor_tensor(r, r, lnr[:, j:j + 1].to_broadcast([P, D]), ALU.mult).then_inc(pool_xg, 1)
                pool.wait_ge(pool_xg, 3 * i + 2)
                pool.tensor_tensor(r, r, gab[:, :], ALU.mult).then_inc(pool_xg, 1)
                pool.wait_ge(pool_xg, 3 * i + 3)
                pool.tensor_tensor(r, r, beb[:, :], ALU.add).then_inc(pool_xr, 1)

            def dispatch(m, mpar):
                pool.wait_ge(dve_wp, m + 1).then_inc(pool_passed, 1)
                if isinstance(m, int) and m == NSB - 1:
                    pool.wait_ge(dve_xr, SB).then_inc(pool_passed, 1)
                pool.tensor_copy(xr[mpar][:, :, D + E:ROW].bitcast(I32), tokid[:, bass.ds(m * SB, SB)].unsqueeze(2)).then_inc(pool_tok, 1)
                pool.wait_ge(pool_tok, m + 1).then_inc(pool_passed, 1)
                pool.wait_ge(dve_idx, m + 1).then_inc(pool_passed, 1)
                for r in range(K):
                    for j in range(SB):
                        c = r * SB + j
                        pool.indirect_dma_start(out=buf, out_offset=bass.IndirectOffsetOnAxis(slotu[mpar][:, c:c + 1], 0),
                                                in_=xr[mpar][:, j, :], in_offset=None, bounds_check=E * CAP - 1,
                                                oob_is_err=False).then_inc(scattered[mpar], 16)

            def body(n, par, prev1, prev2, cur, nxt, nxt2, reuse):
                if cur:
                    values_third(n, par)
                    residual(n, par, prev1)
                if nxt:
                    keys_low(n + 1)
                if prev1:
                    norm2(n - 1, 0)
                    if cur:
                        normalize2(n - 1, 1 - par, 0, reuse)
                if nxt2:
                    normalize_inputs(n + 2)
                if nxt:
                    queries_low(n + 1, 1 - par)
                if prev1:
                    norm2(n - 1, 1)
                    if cur:
                        normalize2(n - 1, 1 - par, 1, reuse)
                if nxt:
                    values_rest(n + 1, 1 - par)
                if prev2:
                    dispatch(n - 2, par)

            queries_low(0, 0)
            pool.wait_ge(dve_bo, 1)
            pool.wait_ge(gates_ok, 1)
            then(pool.tensor_scalar(tbo[:, :], bob[:, :], tg[:, 0:1], None, ALU.mult))
            for s in range(len(XCUT) - 1):
                pool.wait_ge(ld_x[s], 16)
            values_rest(0, 0)
            body(0, 0, False, False, True, True, True, None)
            rstd1(XCUT[2], SEQS)
            body(1, 1, True, False, True, True, True, None)
            pool.wait_ge(ld_pad, 16 * (E + 1))
            body(2, 0, True, True, True, True, True, None)
            body(3, 1, True, True, True, True, True, 1)
            with pool.Fori(2, NSB // 2 - 1) as i:
                body(2 * i, 0, True, True, True, True, True, i - 1)
                body(2 * i + 1, 1, True, True, True, True, True, i)
            body(NSB - 2, 0, True, True, True, True, False, NSB // 2 - 2)
            body(NSB - 1, 1, True, True, True, False, False, NSB // 2 - 1)
            body(NSB, 0, True, True, False, False, False, None)
            body(NSB + 1, 1, False, True, False, False, False, None)

            pool.wait_ge(st_x2, 16 * NSB)

            pool.wait_ge(flag_ok, 2)
            flags = pool.value_load(flag[0:1, 0:1], min_val=0, max_val=2 ** E - 1)

            def add_tile(e, par, c, done):
                pool.wait_ge(dve_ysc, CT * e + c + 1).then_inc(pool_passed, 1)
                pool.indirect_dma_start(out=out, out_offset=bass.IndirectOffsetOnAxis(rows[par][:, c, D + E:ROW].bitcast(U32), 0),
                                        in_=ysc[par][:, c, :], in_offset=None, bounds_check=TOKENS + P - 1,
                                        oob_is_err=True, compute_op=ALU.add).then_inc(done, 16)

            def add_rows(e, par):
                for c in range(CT0):
                    add_tile(e, par, c, added)
                    if c < CT0 - 1:
                        pool.wait_ge(added, 16 * (CT0 * e + c + 1)).then_inc(pool_passed, 1)
                before_e = pool.value_load(past[0:1, bass.ds(e, 1)], min_val=0, max_val=E - 1)
                with pool.If(more_rows(flags, e)):
                    pool.wait_ge(added, 16 * CT0 * (e + 1)).then_inc(pool_passed, 1)
                    for c in range(CT0, CT):
                        add_tile(e, par, c, added2)
                        if c < CT - 1:
                            pool.wait_ge(added2, 16 * ((CT - CT0) * before_e + c + 1 - CT0)).then_inc(pool_passed, 1)
                    pool.wait_ge(added2, 16 * (CT - CT0) * (before_e + 1)).then_inc(expert_added, 1)
                with pool.Else():
                    pool.wait_ge(added, 16 * CT0 * (e + 1)).then_inc(expert_added, 1)

            add_rows(0, 0)
            add_rows(1, 1)
            with pool.Fori(1, E // 2) as i:
                add_rows(2 * i, 0)
                add_rows(2 * i + 1, 1)
            pool.wait_ge(expert_added, E)

        @block.scalar
        def _(act):
            act.dma_start(gate[:, :], gates.partition_broadcast(P)).then_inc(ld_g, 16)
            act.dma_start(bqkv[:, :, :], biases).then_inc(ld_b, 16)

            def exps_of_logits(m):
                act.wait_ge(dve_lgs, m + 1)
                act.activation(lex[:, :, :], lgs[:, :, :], ACT.Exp).then_inc(act_ex, 1)

            def x2_columns(m, bank):
                act.wait_ge(pe_x2T, m + 1)
                act.activation(xnT[:, :, :], bank[:, :].rearrange("p (c t) -> p c t", c=DC), ACT.Copy).then_inc(act_x2T, 1)

            def input_columns(n):
                act.wait_ge(pe_xT, n + 1)
                act.activation(xT[:, :, :], Xp[:, :].rearrange("p (c t) -> p c t", c=DC), ACT.Copy).then_inc(act_xT, 1)

            def queries(n, par, bank, prev1):
                act.wait_ge(pe_q, n + 1)
                if prev1:
                    act.wait_ge(pool_ql, n)
                for t in range(DC):
                    act.activation(qT[:, t, :], bank[:, t * SB * T:(t + 1) * SB * T], ACT.Identity,
                                   bias=bq4[:, t:t + 1], scale=HD ** -0.5).then_inc(act_q32, 1)
                act.wait_ge(act_q32, DC * (n + 1))
                act.activation(q2[par][:, 0, :, :], qT[:, :, :], ACT.Copy).then_inc(act_q, 1)

            def keys(n, bank, prev1):
                act.wait_ge(pe_k, n + 1)
                if prev1:
                    act.wait_ge(pool_kl, n)
                for t in range(DC):
                    act.activation(kT[:, t, :], bank[:, t * SB * T:(t + 1) * SB * T], ACT.Identity, bias=bqkv[:, 1, t:t + 1])\
                       .then_inc(act_k32, 1)
                if prev1:
                    for half in ld_km:
                        act.wait_ge(half, KM * n)
                act.wait_ge(act_k32, DC * (n + 1))
                act.activation(k2[:, 0, :, :], kT[:, :, :], ACT.Copy).then_inc(act_kT, 1)

            def values(n, bank):
                act.wait_ge(pe_v, n + 1)
                act.activation(vf[:, :, :], bank[:, :].rearrange("p (b d) -> p b d", d=D), ACT.Copy).then_inc(act_vf, 1)

            def values1(n, par):
                act.wait_ge(act_vf, n + 1)
                act.activation(V3[par][:, :, :, 0:HD], vf[:, :, :].rearrange("p b (h d) -> p b h d", d=HD), ACT.Copy).then_inc(act_v1, 1)

            def values2(n, par):
                act.wait_ge(pool_vr, n + 1)
                act.activation(V3[par][:, :, :, HD:2 * HD], vr[:, :, :].rearrange("p b (h d) -> p b h d", d=HD), ACT.Copy).then_inc(act_v2, 1)

            def output_columns(i, bank):
                act.wait_ge(pe_oT, i + 1)
                act.activation(oT[:, :, :], bank[:, 0:D].rearrange("p (c t) -> p c t", c=DC), ACT.Copy).then_inc(act_oT, 1)

            def exps(G, g, early):
                act.wait_ge(dve_bias, G + 1)
                if not early:
                    act.wait_ge(pe_t, G - 1)
                for h in range(GH):
                    ins = act.activation(p32[g % 2][:, h, :], S[g % 2][:, h * T:(h + 1) * T], ACT.Exp, bias=nb[g % 2][:, h:h + 1])
                ins.then_inc(act_exp, 1)

            def high_probs(G, g, early):
                act.wait_ge(pe_t, G + 1)
                if not early:
                    act.wait_ge(pe_pv, G - 1)
                act.activation(pT[g % 2][:, 0, :, :], Tb[g % 2][:, :].rearrange("p (h t) -> p h t", h=GH), ACT.Copy).then_inc(act_hi, 1)

            def body(n, par, prev1, prev2, cur, nxt):
                for g in range(NG):
                    G = NG * n + g
                    if (cur and g >= 2) or (prev1 and g < 2):
                        high_probs(G - 2, g % 2, not prev1 and g < 4)
                    if g == 0 and prev1:
                        output_columns(SB * (n - 1), Xo)
                    if g == 7 and nxt:
                        values(n + 1, Xp)
                    if g == 2 and prev2:
                        x2_columns(n - 2, Xo)
                    if g == 3 and nxt:
                        keys(n + 1, Xp, True)
                    if cur:
                        exps(G, g, not prev1 and g < 2)
                    if g == 7 and nxt:
                        values1(n + 1, 1 - par)
                    if g == 4 and prev2:
                        exps_of_logits(n - 2)
                    if g == 4 and prev1:
                        output_columns(SB * (n - 1) + 1, Xo)
                    if g == 4 and nxt:
                        queries(n + 1, 1 - par, Xp, True)
                    if g == 0 and nxt:
                        input_columns(n + 1)
                    if g == 1 and prev1 and cur:
                        values2(n, par)

            act.wait_ge(ld_g, 16)
            act.activation(tg[:, :], gate[:, :], ACT.Tanh).then_inc(gates_ok, 1)
            act.wait_ge(ld_b, 16)
            keys(0, K0, False)
            input_columns(0)
            values(0, Xo)
            values1(0, 0)
            act.wait_ge(bias_ok, 1)
            queries(0, 0, Q0, False)
            act.activation(kM[1][:, 1, :, :].rearrange("p h (a t) -> p (h a) t", t=P),
                           ident32[:, :].unsqueeze(1).to_broadcast([P, 2 * H, P]), ACT.Copy, scale=0.0).then_inc(km_zero[1], 1)
            values2(0, 0)
            body(0, 0, False, False, True, True)
            body(1, 1, True, False, True, True)
            with act.Fori(1, NSB // 2 - 1) as i:
                body(2 * i, 0, True, True, True, True)
                body(2 * i + 1, 1, True, True, True, True)
            body(NSB - 2, 0, True, True, True, True)
            body(NSB - 1, 1, True, True, True, False)

            for g in range(2):
                high_probs(NG * NSB - 2 + g, g, False)
                if g == 0:
                    output_columns(SEQS - 2, Xp)
            x2_columns(NSB - 2, Xo)
            output_columns(SEQS - 1, Xp)
            exps_of_logits(NSB - 2)
            x2_columns(NSB - 1, Xp)
            exps_of_logits(NSB - 1)

            def stage_uses(i, par, k):
                s = (par + k) % 2
                return 3 * i + sum(1 for pp_, kk in ((0, 0), (0, 1), (0, 2), (1, 0), (1, 1), (1, 2))
                                   if (pp_ + kk) % 2 == s and (pp_, kk) <= (par, k))

            def high(i, par, q12):
                k, q = q12 // 4, q12 % 4
                s = (par + k) % 2
                if q == 0:
                    act.wait_ge(ld_st[s], 16 * stage_uses(i, par, k))
                act.activation(Wh[par][:, k, q * QW:(q + 1) * QW], stage[s][:, q * QW:(q + 1) * QW], ACT.Copy)\
                    .then_inc(act_wh, 1)

            def rows_high(e, par, a):
                c, d = a // 2, a % 2
                o, w = CHUNKS[c]
                act.wait_ge(pe_bT, 4 * e + a + 1)
                act.activation(bXh[par][:, d, o:o + w], Xc[a % 2][:, 0:w], ACT.Copy).then_inc(act_bh, 1)

            def hidden_high(e, j):
                c, f = j // FT, j % FT
                w = CHUNKS[c][1]
                act.wait_ge(dve_h, 16 * e + j + 1)
                act.activation(hH[c][:, f, :], hF[j % 2][:, 0:w], ACT.Copy).then_inc(act_hh, 1)

            for q12 in range(4 * DC):
                high(0, 0, q12)
            for a in range(2):
                rows_high(0, 0, a)
            for q12 in range(4 * DC, PIECES):
                high(0, 0, q12)

            act.wait_ge(flag_ok, 1)
            flags = act.value_load(flag[0:1, 0:1], min_val=0, max_val=2 ** E - 1)

            def steps(i, par, c, last, first):
                e = 2 * i + par
                w = CHUNKS[c][1]
                for f in range(FT + 1):
                    j = c * FT + f
                    if f < FT:
                        act.wait_ge(pe_gu, 16 * e + j + 1)
                        if not first or j >= 2:
                            act.wait_ge(dve_h, 16 * e + j - 1)
                        act.activation(sil[j % 2][:, 0:w], Gb[j % 2][:, 0:w], ACT.Silu).then_inc(act_sil, 1)
                    if f >= 1:
                        if j == 1 and not first:
                            act.wait_ge(pe_out, CT * e)
                        hidden_high(e, j - 1)
                    if c == 0 and f < FT and not last:
                        high(i + par, 1 - par, f)

            def expert(i, par, last, first):
                e = 2 * i + par
                steps(i, par, 0, last, first)
                if isinstance(e, int) and e == 0:
                    rows_high(0, 0, 2)
                    rows_high(0, 0, 3)
                if not last:
                    for k in range(FT, PIECES):
                        high(i + par, 1 - par, k)
                    for a in range(4):
                        rows_high(e + 1, 1 - par, a)
                with act.If(more_rows(flags, e)):
                    steps(i, par, 1, last, first)
                with act.Else():
                    act.wait_ge(act_sil, 16 * e + FT).then_inc(act_sil, FT)
                    act.wait_ge(act_hh, 16 * e + FT).then_inc(act_hh, FT)

            expert(0, 0, False, True)
            expert(0, 1, False, False)
            with act.Fori(1, E // 2 - 1) as i:
                expert(i, 0, False, False)
                expert(i, 1, False, False)
            expert(E // 2 - 1, 0, False, False)
            expert(E // 2 - 1, 1, True, False)

        @block.vector
        def _(dve):
            def stats1(a, b):
                for i in range(a, b):
                    if i in XCUT:
                        dve.wait_ge(ld_x[XCUT.index(i)], 16)
                    dve.bn_stats(st_all[:, i, :], xv[:, i, :]).then_inc(dve_st, 1)
                for i in range(a, b):
                    dve.wait_ge(dve_st, i + 1)
                    dve.bn_aggr(mv_all[:, i, :], st_all[:, i, :]).then_inc(dve_mv1, 1)

            def normalize_inputs(n):
                if not (isinstance(n, int) and n == 0):
                    dve.wait_ge(pe_xT, n)
                for j in range(SB):
                    i = SB * n + j
                    dve.tensor_scalar(xn1[:, j, :], x_tile(i), mv_all[:, bass.ds(i, 1), 0], rs_all[:, bass.ds(i, 1)],
                                      ALU.subtract, ALU.mult).then_inc(dve_xn1, 1)

            def stats2(m, j):
                i = SB * m + j
                dve.wait_ge(dve_x2, i + 1)
                dve.bn_stats(st2[:, j, :], x_tile(i)).then_inc(dve_st2, 1)
                dve.wait_ge(dve_st2, i + 1).then_inc(dve_passed, 1)
                dve.bn_aggr(mv2[:, j, :], st2[:, j, :]).then_inc(dve_mv2, 1)

            def normalize2(j):
                m, mpar = NSB - 1, (NSB - 1) % 2
                i = SB * m + j
                dve.wait_ge(pool_rs2, 2 * i + 2)
                if j == 0:
                    dve.wait_ge(scattered[mpar], 16 * K * SB * (m // 2))
                r = xr[mpar][:, j, 0:D]
                dve.scalar_tensor_tensor(r, x_tile(i), mv2[:, j, 0:1], gab[:, :], ALU.subtract, ALU.mult).then_inc(dve_xg, 1)
                dve.wait_ge(dve_xg, j + 1)
                dve.scalar_tensor_tensor(r, r, lnr[:, j:j + 1], beb[:, :], ALU.mult, ALU.add).then_inc(dve_xr, 1)

            def clip_logits(m, bank):
                dve.wait_ge(pe_lg, m + 1)
                dve.tensor_scalar(lgc[:, :, :], bank[:, 0:SB * E].rearrange("p (j e) -> p j e", e=E), -CLAMP, CLAMP, ALU.max, ALU.min)\
                   .then_inc(dve_lg, 1)

            def largest_logit(m):
                dve.wait_ge(dve_lg, m + 1)
                dve.tensor_reduce(lmx[:, :], lgc[:, :, :], AX_X, ALU.max).then_inc(dve_r, 1)

            def shift_logits(m):
                dve.wait_ge(dve_r, R_CHAIN * m + 1)
                dve.tensor_tensor(lgs[:, :, :], lgc[:, :, :], lmx[:, :].unsqueeze(2).to_broadcast([P, SB, E]), ALU.subtract)\
                   .then_inc(dve_lgs, 1)

            def sum_exps(m):
                dve.wait_ge(act_ex, m + 1)
                dve.tensor_reduce(lsm[:, :], lex[:, :, :], AX_X, ALU.add).then_inc(dve_r, 1)

            def guard_sum(m):
                dve.wait_ge(dve_r, R_CHAIN * m + 2)
                dve.tensor_scalar(lse[:, :], lsm[:, :], 1e-12, None, ALU.add).then_inc(dve_r, 1)

            def invert_sum(m):
                dve.wait_ge(dve_r, R_CHAIN * m + 3)
                dve.reciprocal(lrc[:, :], lse[:, :]).then_inc(dve_r, 1)

            def expert_probs(m):
                dve.wait_ge(dve_r, R_CHAIN * m + 4)
                dve.tensor_tensor(prob[:, :, :], lex[:, :, :], lrc[:, :].unsqueeze(2).to_broadcast([P, SB, E]), ALU.mult).then_inc(dve_r, 1)

            def sort_probs(m):
                dve.wait_ge(dve_r, R_CHAIN * m + 5).then_inc(dve_passed, 1)
                for j in range(SB):
                    ins = dve.max(top8[:, j, :], prob[:, j, :])
                ins.then_inc(dve_r, 1)

            def sort_experts(m):
                dve.wait_ge(dve_r, R_CHAIN * m + 6).then_inc(dve_passed, 1)
                for j in range(SB):
                    ins = dve.max_index(topi[:, j, :], top8[:, j, :], prob[:, j, :])
                ins.then_inc(dve_r, 1)

            def chosen_numbers(m):
                dve.wait_ge(dve_r, R_CHAIN * m + 7)
                dve.tensor_copy(ixf[:, :, :], topi[:, :, 0:K].rearrange("p j r -> p r j")).then_inc(dve_r, 1)

            def pick_experts(m):
                dve.wait_ge(dve_r, R_CHAIN * m + 8)
                dve.tensor_tensor(pick[:, :, :, :], iota8[:, :].unsqueeze(1).unsqueeze(1).to_broadcast([P, K, SB, E]),
                                  ixf[:, :, :].unsqueeze(3).to_broadcast([P, K, SB, E]), ALU.is_equal).then_inc(dve_r, 1)

            def members(m, mpar):
                dve.wait_ge(dve_r, R_CHAIN * m + 9)
                dve.tensor_tensor(member[:, :, :], pick[:, 0, :, :], pick[:, 1, :, :], ALU.add).then_inc(dve_mem, 1)
                dve.tensor_scalar(xr[mpar][:, :, D:D + E], prob[:, :, :], tg[:, 1:2], None, ALU.mult).then_inc(dve_wp, 1)

            def shifted_logits(m, bank):
                clip_logits(m, bank)
                largest_logit(m)
                shift_logits(m)

            def all_probs(m):
                sum_exps(m)
                guard_sum(m)
                invert_sum(m)
                expert_probs(m)

            def choose_experts(m, mpar):
                sort_probs(m)
                sort_experts(m)
                chosen_numbers(m)
                pick_experts(m)
                members(m, mpar)

            def slots(m, mpar, bank):
                dve.wait_ge(pe_rk, m + 1)
                rk = bank[:, 0:SB * E].rearrange("p (j e) -> p j e", e=E)
                dve.tensor_scalar(late[:, :, :], rk, float(CAP), LATE, ALU.is_ge, ALU.mult).then_inc(dve_rk, 1)
                dve.tensor_tensor(slot0[:, :, :], rk, ebase[:, :].unsqueeze(1).to_broadcast([P, SB, E]), ALU.add).then_inc(dve_rk, 1)
                dve.tensor_reduce(seen_add[:, :], member[:, :, :].rearrange("p j e -> p e j"), AX_X, ALU.add).then_inc(dve_rk, 1)
                dve.wait_ge(dve_rk, 6 * m + 3)
                dve.tensor_tensor(slot[:, :, :], slot0[:, :, :], late[:, :, :], ALU.add).then_inc(dve_rk, 1)
                dve.tensor_tensor(seen[:, :], seen[:, :], seen_add[:, :], ALU.add)
                dve.wait_ge(dve_rk, 6 * m + 4)
                dve.tensor_tensor(pslot[:, :, :, :], pick[:, :, :, :], slot[:, :, :].unsqueeze(1).to_broadcast([P, K, SB, E]), ALU.mult)\
                   .then_inc(dve_rk, 1)
                dve.wait_ge(dve_rk, 6 * m + 5)
                dve.tensor_reduce(slotf[:, :, :], pslot[:, :, :, :], AX_X, ALU.add).then_inc(dve_rk, 1)
                dve.wait_ge(dve_rk, 6 * m + 6)
                dve.tensor_copy(slotu[mpar][:, :], slotf[:, :, :].rearrange("p r j -> p (r j)")).then_inc(dve_idx, 1)

            def largest(G, g):
                dve.wait_ge(pe_s, G + 1)
                dve.tensor_reduce(nm[g % 2][:, :], S[g % 2][:, :].rearrange("p (h t) -> p h t", t=T), AX_X, ALU.max)\
                   .then_inc(dve_max, 1)

            def exp_bias(G, g):
                dve.wait_ge(dve_max, G + 1)
                dve.tensor_scalar(nb[g % 2][:, :], nm[g % 2][:, :], -1.0, PSCALE, ALU.mult, ALU.add).then_inc(dve_bias, 1)

            def low_probs(G, g):
                dve.wait_ge(act_hi, G + 1)
                dve.tensor_tensor(pT[g % 2][:, 1, :, :], Tb[g % 2][:, :].rearrange("p (h t) -> p h t", h=GH), pT[g % 2][:, 0, :, :],
                                  ALU.subtract).then_inc(dve_lo, 1)

            def heads_out(kk, k, early):
                ob = O[k % 2][:, 0:8 * VW].rearrange("p (h w) -> p h w", w=VW)
                dve.wait_ge(pe_pv, 2 * kk + 2)
                if not early:
                    dve.wait_ge(dve_on, kk)
                dve.tensor_reduce(osum[:, :, :], ob[:, :, 0:3 * HD].rearrange("p h (c d) -> p h d c", d=HD), AX_X, ALU.add)\
                   .then_inc(dve_os, 1)
                dve.reciprocal(orec[:, :], ob[:, :, 3 * HD]).then_inc(dve_rec, 1)
                dve.wait_ge(dve_os, kk + 1)
                dve.wait_ge(dve_rec, kk + 1)
                return ob

            def heads_scale(kk, k, seq_before):
                if k % 2 == 0 and seq_before is not None:
                    dve.wait_ge(pe_oT, seq_before + 1)
                dve.tensor_tensor(oN[:, (k % 2) * P:(k % 2 + 1) * P].rearrange("p (h d) -> p h d", d=HD), osum[:, :, :],
                                  orec[:, :].unsqueeze(2).to_broadcast([P, 8, HD]), ALU.mult).then_inc(dve_on, 1)

            def gated(n, par, b, bank):
                i = SB * n + b
                dve.wait_ge(pe_y, i + 1)
                dve.wait_ge(pool_xbo, n + 1)
                dve.scalar_tensor_tensor(x_tile(i), bank[:, 0:D], tg[:, 0:1], xbo[par][:, b, :], ALU.mult, ALU.add).then_inc(dve_x2, 1)

            def body(half, par, prev1, prev2, prev3, cur, nxt):
                n = 2 * half + par
                HPS = 2 * SB
                for g in range(NG):
                    G = NG * n + g
                    routed = n - 2 if prev2 else None
                    if g in (2, 6) and prev1:
                        gated(n - 1, 1 - par, g // 4, Xo)
                    if g == 4 and prev2:
                        clip_logits(routed, Xo)
                    elif g == 5 and prev2:
                        sum_exps(routed)
                    elif g == 6 and prev2:
                        sort_experts(routed)
                    if cur:
                        largest(G, g)
                    if g == 4 and prev2:
                        largest_logit(routed)
                    elif g == 5 and prev2:
                        guard_sum(routed)
                    elif g == 6 and prev2:
                        chosen_numbers(routed)
                    if cur:
                        exp_bias(G, g)
                    if g == 4 and prev2:
                        shift_logits(routed)
                    elif g == 5 and prev2:
                        invert_sum(routed)
                    elif g == 6 and prev2:
                        pick_experts(routed)
                    if g < 2 and cur and not prev1:
                        stats1(*XCUT[2 + g:4 + g])
                    if g in (1, 3) and prev1:
                        k = 2 + g // 2
                        heads_out(HPS * (n - 1) + k, k, False)
                        heads_scale(HPS * (n - 1) + k, k, SB * (n - 1))
                    if g in (5, 7) and cur:
                        k = (g - 5) // 2
                        heads_out(HPS * n + k, k, not prev1 and k == 0)
                        heads_scale(HPS * n + k, k, SB * n - 1 if prev1 else None)
                    if g == 5 and prev2:
                        expert_probs(routed)
                    if (cur and g >= 2) or (prev1 and g < 2):
                        low_probs(G - 2, g % 2)
                    if g == 5 and prev2:
                        sort_probs(routed)
                    elif g == 6 and prev2:
                        members(routed, par)
                    if g in (2, 6) and prev1:
                        stats2(n - 1, g // 4)
                    if g == 7 and prev2:
                        slots(routed, par, Xo)

            def zero_keys(par, part, half):
                dve.tensor_scalar(kM[par][:, part, half * H // 2:(half + 1) * H // 2, :].rearrange("p h (a t) -> p (h a) t", t=P),
                                  ident32[:, :].unsqueeze(1).to_broadcast([P, H, P]), 0.0, None, ALU.mult).then_inc(km_zero[par], 1)

            dve.wait_ge(ident_ok, 1)
            zero_keys(0, 0, 0)
            zero_keys(0, 0, 1)
            stats1(0, SB)
            dve.wait_ge(pool_ln1, 1)
            normalize_inputs(0)
            zero_keys(0, 1, 0)
            zero_keys(0, 1, 1)
            stats1(*XCUT[1:3])
            dve.wait_ge(pool_ln1, 2)
            normalize_inputs(1)
            zero_keys(1, 0, 0)
            zero_keys(1, 0, 1)
            dve.wait_ge(ld_c, 16 * 3)
            dve.wait_ge(pe_bo, 1)
            dve.tensor_tensor(bob[:, :], bob[:, :], Tb[0][:, 0:D], ALU.add).then_inc(dve_bo, 1)
            dve.wait_ge(const_ok, CONSTS)
            dve.wait_ge(gates_ok, 1)
            body(0, 0, False, False, False, True, True)
            body(0, 1, True, False, False, True, True)
            body(1, 0, True, True, False, True, True)
            body(1, 1, True, True, True, True, True)
            with dve.Fori(2, NSB // 2 - 1) as i:
                body(i, 0, True, True, True, True, True)
                body(i, 1, True, True, True, True, True)
            body(NSB // 2 - 1, 0, True, True, True, True, True)
            body(NSB // 2 - 1, 1, True, True, True, True, False)

            halves = 2 * SEQS
            low_probs(NG * NSB - 2, 0)
            heads_out(halves - 2, 2, False)
            heads_scale(halves - 2, 2, SEQS - 2)
            low_probs(NG * NSB - 1, 1)
            gated(NSB - 1, 1, 0, Xp)
            heads_out(halves - 1, 3, False)
            heads_scale(halves - 1, 3, None)
            stats2(NSB - 1, 0)
            shifted_logits(NSB - 2, Xo)
            all_probs(NSB - 2)
            gated(NSB - 1, 1, 1, Xp)
            stats2(NSB - 1, 1)
            normalize2(0)
            normalize2(1)
            choose_experts(NSB - 2, 0)
            slots(NSB - 2, 0, Xo)
            shifted_logits(NSB - 1, Xp)
            all_probs(NSB - 1)
            choose_experts(NSB - 1, 1)
            slots(NSB - 1, 1, Xp)

            dve.wait_ge(pe_cnt, 1)
            dve.tensor_scalar(many[:, :], Xo[:, 0:E], float(CHUNKS[0][1]), None, ALU.is_gt).then_inc(dve_cnt, 1)
            dve.wait_ge(dve_cnt, 1)
            dve.tensor_tensor(many_e[:, :], many[:, :], two_e[:, :], ALU.mult).then_inc(dve_cnt, 1)
            dve.wait_ge(dve_cnt, 2)
            dve.tensor_reduce(flagf[:, :], many_e[:, :], AX_X, ALU.add).then_inc(dve_cnt, 1)
            dve.wait_ge(dve_cnt, 3)
            dve.tensor_copy(flag[:, :], flagf[:, :]).then_inc(flag_ok, 1)
            dve.tensor_tensor(many_l[:, :, :], many[:, :].unsqueeze(1).to_broadcast([P, E, E]), lower[:, :, :], ALU.mult).then_inc(dve_cnt, 1)
            dve.wait_ge(dve_cnt, 4)
            dve.tensor_reduce(pastf[:, :], many_l[:, :, :], AX_X, ALU.add).then_inc(dve_cnt, 1)
            dve.wait_ge(dve_cnt, 5)
            dve.tensor_copy(past[:, :], pastf[:, :]).then_inc(flag_ok, 1)

            def stage_uses(i, par, k):
                s = (par + k) % 2
                return 3 * i + sum(1 for pp_, kk in ((0, 0), (0, 1), (0, 2), (1, 0), (1, 1), (1, 2))
                                   if (pp_ + kk) % 2 == s and (pp_, kk) <= (par, k))

            def low(i, par, q12):
                k, q = q12 // 4, q12 % 4
                s = (par + k) % 2
                if q == 0:
                    dve.wait_ge(ld_st[s], 16 * stage_uses(i, par, k))
                dve.wait_ge(act_wh, PIECES * (2 * i + par) + q12 + 1)
                cols = slice(q * QW, (q + 1) * QW)
                dve.tensor_tensor(Wl[par][:, k, cols], stage[s][:, cols], Wh[par][:, k, cols].bitcast(F32), ALU.subtract)\
                   .then_inc(dve_wl, 1)

            def rows_low(e, par, a):
                c, d = a // 2, a % 2
                o, w = CHUNKS[c]
                dve.wait_ge(act_bh, 4 * e + a + 1)
                dve.tensor_tensor(bXl[par][:, d, o:o + w], Xc[a % 2][:, 0:w], bXh[par][:, d, o:o + w].bitcast(F32), ALU.subtract)\
                   .then_inc(dve_bl, 1)

            for q12 in range(4 * DC):
                low(0, 0, q12)
            for a in range(2):
                rows_low(0, 0, a)
            for q12 in range(4 * DC, PIECES):
                low(0, 0, q12)

            dve.wait_ge(flag_ok, 1)
            flags = dve.value_load(flag[0:1, 0:1], min_val=0, max_val=2 ** E - 1)

            def steps(i, par, c, last, first):
                e = 2 * i + par
                w = CHUNKS[c][1]
                for f in range(FT + 1):
                    j = c * FT + f
                    if f < FT:
                        dve.wait_ge(act_sil, 16 * e + j + 1)
                        if not first or j >= 2:
                            dve.wait_ge(act_hh, 16 * e + j - 1)
                            dve.wait_ge(dve_hl, 16 * e + j - 1)
                        dve.tensor_tensor(hF[j % 2][:, 0:w], sil[j % 2][:, 0:w], Ub[j % 2][:, 0:w], ALU.mult).then_inc(dve_h, 1)
                    if f >= 1:
                        jj = j - 1
                        dve.wait_ge(act_hh, 16 * e + jj + 1)
                        dve.tensor_tensor(hL[c][:, f - 1, :], hF[jj % 2][:, 0:w], hH[c][:, f - 1, :].bitcast(F32), ALU.subtract)\
                           .then_inc(dve_hl, 1)
                    if c == 0 and f < FT and not last:
                        low(i + par, 1 - par, f)

            def weigh(e, par, t, first):
                if t == 0 and not (isinstance(e, int) and e < 2):
                    dve.wait_ge(expert_added, e - 1)
                dve.wait_ge(pe_out, CT * e + t + 1)
                dve.tensor_scalar(ysc[par][:, t, :], Yb[(par + t) % 2][:, 0:D], rows[par][:, t, bass.ds(D + e, 1)], None, ALU.mult)\
                   .then_inc(dve_ysc, 1)

            def expert(i, par, last, first):
                e = 2 * i + par
                steps(i, par, 0, last, first)
                if isinstance(e, int) and e == 0:
                    rows_low(0, 0, 2)
                    rows_low(0, 0, 3)
                if not last:
                    for k in range(FT, PIECES):
                        low(i + par, 1 - par, k)
                weigh(e, par, 0, first)
                weigh(e, par, 1, first)
                if not last:
                    rows_low(e + 1, 1 - par, 0)
                    rows_low(e + 1, 1 - par, 1)
                weigh(e, par, 2, first)
                if not last:
                    rows_low(e + 1, 1 - par, 2)
                    rows_low(e + 1, 1 - par, 3)
                with dve.If(more_rows(flags, e)):
                    steps(i, par, 1, last, first)
                    for t in range(CT0, CT):
                        weigh(e, par, t, first)
                with dve.Else():
                    dve.wait_ge(dve_h, 16 * e + FT).then_inc(dve_h, FT)
                    dve.wait_ge(dve_hl, 16 * e + FT).then_inc(dve_hl, FT)
                    dve.wait_ge(dve_ysc, CT * e + CT0).then_inc(dve_ysc, CT - CT0)

            expert(0, 0, False, True)
            expert(0, 1, False, False)
            with dve.Fori(1, E // 2 - 1) as i:
                expert(i, 0, False, False)
                expert(i, 1, False, False)
            expert(E // 2 - 1, 0, False, False)
            expert(E // 2 - 1, 1, True, False)

        @block.tensor
        def _(pe):
            def input_columns(n, first, second):
                if first or second:
                    pe.wait_ge(dve_xn1, SB * n + SB)
                else:
                    pe.wait_ge(pool_xn1, n - 1)
                if not first:
                    pe.wait_ge(act_vf, n)
                for c in range(DC):
                    for j in range(SB):
                        ins = nc.tensor.transpose(Xp[:, (c * SB + j) * T:(c * SB + j + 1) * T], xn1[:, j, c * P:(c + 1) * P], ident32[:, :])
                ins.then_inc(pe_xT, 1)

            def queries(n, bank):
                pe.wait_ge(act_xT, n + 1)
                if bank is Xp:
                    pe.wait_ge(act_k32, DC * (n + 1))
                for t in range(DC):
                    for c in range(DC):
                        ins = nc.tensor.matmul(bank[:, t * SB * T:(t + 1) * SB * T], wq[:, c, t * P:(t + 1) * P], xT[:, c, :],
                                               start=(c == 0), stop=(c == DC - 1))
                ins.then_inc(pe_q, 1)

            def keys(n, par, bank, use):
                pe.wait_ge(ld_ctx[par], 16 * use)
                if bank is Xp:
                    pe.wait_ge(act_xT, n + 1)
                for t in range(DC):
                    for c in range(DC):
                        ins = nc.tensor.matmul(bank[:, t * SB * T:(t + 1) * SB * T], wk[:, c, t * P:(t + 1) * P], cT[par][:, c, :],
                                               start=(c == 0), stop=(c == DC - 1))
                ins.then_inc(pe_k, 1)

            def values(n, par, bank):
                for b in range(SB):
                    for c in range(DC):
                        ins = nc.tensor.matmul(bank[:, b * D:(b + 1) * D], cT[par][:, c, b * T:(b + 1) * T], wv[:, c, :],
                                               start=(c == 0), stop=(c == DC - 1))
                ins.then_inc(pe_v, 1)

            def x2_columns(m, mpar, bank):
                if isinstance(m, int) and m == NSB - 1:
                    pe.wait_ge(dve_xr, SB)
                else:
                    pe.wait_ge(pool_xr, SB * m + SB)
                for c in range(DC):
                    for j in range(SB):
                        ins = nc.tensor.transpose(bank[:, (c * SB + j) * T:(c * SB + j + 1) * T], xr[mpar][:, j, c * P:(c + 1) * P], ident32[:, :])
                ins.then_inc(pe_x2T, 1)

            def logits(m, bank):
                pe.wait_ge(act_x2T, m + 1)
                for j in range(SB):
                    for c in range(DC):
                        ins = nc.tensor.matmul(bank[:, j * E:(j + 1) * E], xnT[:, c, j * T:(j + 1) * T], wr[:, c, :],
                                               start=(c == 0), stop=(c == DC - 1))
                ins.then_inc(pe_lg, 1)

            def ranks(m, bank):
                pe.wait_ge(dve_mem, m + 1)
                rk = bank[:, 0:SB * E].rearrange("p (j e) -> p j e", e=E)
                nc.tensor.matmul(rk, before[:, :], member[:, :, :], start=True, stop=False)
                for j in range(1, SB):
                    nc.tensor.matmul(rk[:, j:SB, :], onesb[:, :], member[:, 0:SB - j, :], start=False, stop=False)
                nc.tensor.matmul(rk, onesb[:, :], seen[:, :].unsqueeze(1).to_broadcast([P, SB, E]), start=False, stop=True)\
                    .then_inc(pe_rk, 1)

            def scores(G, g, n, par, early):
                b, hq = g // GPS, g % GPS
                if g == 0:
                    pe.wait_ge(pool_ql, n + 1)
                if g < 2:
                    pe.wait_ge(ld_km[g], KM * (n + 1))
                if not early:
                    pe.wait_ge(act_exp, G - 1)
                nc.tensor.matmul(S[g % 2][:, :], identb[:, :], causal[:, :, :], start=True, stop=False)
                for sq, sk in ((0, 0), (0, 1), (1, 0)):
                    ins = nc.tensor.matmul(S[g % 2][:, :], q2[par][:, sq, hq // 2, b * T:(b + 1) * T],
                                           kM[par][:, sk, GH * hq:GH * hq + GH, b * T:(b + 1) * T],
                                           start=False, stop=(sq == 1))
                ins.then_inc(pe_s, 1)

            def prob_columns(G, g, early):
                pe.wait_ge(act_exp, G + 1)
                if isinstance(G, int) and G == 0:
                    pe.wait_ge(dve_bo, 1)
                if not early:
                    pe.wait_ge(dve_lo, G - 1)
                for h in range(GH):
                    ins = nc.tensor.transpose(Tb[g % 2][:, h * T:(h + 1) * T], p32[g % 2][:, h, :], ident32[:, :])
                ins.then_inc(pe_t, 1)

            def weigh_values(G, g, n, par, early):
                b, hq, k = g // GPS, g % GPS, g // 2
                if g == 0:
                    pe.wait_ge(pool_v3, n + 1)
                if g % 2 == 0 and not early:
                    pe.wait_ge(dve_on, 2 * SB * n + k - 1)
                pe.wait_ge(dve_lo, G + 1)
                for h in range(GH):
                    o = ((g % 2) * GH + h) * VW
                    for s in range(2):
                        ins = nc.tensor.matmul(O[k % 2][:, o:o + VW], pT[g % 2][:, s, h, :], V3[par][:, b, GH * hq + h, :],
                                               start=(s == 0), stop=(s == 1))
                ins.then_inc(pe_pv, 1)

            def output_columns(i, bank):
                pe.wait_ge(dve_on, 2 * i + 2)
                for c in range(DC):
                    ins = nc.tensor.transpose(bank[:, c * T:(c + 1) * T], oN[:, c * P:(c + 1) * P], ident32[:, :])
                ins.then_inc(pe_oT, 1)

            def project_out(i, bank):
                pe.wait_ge(act_oT, i + 1)
                for c in range(DC):
                    ins = nc.tensor.matmul(bank[:, 0:D], oT[:, c, :], wo[:, c, :], start=(c == 0), stop=(c == DC - 1))
                ins.then_inc(pe_y, 1)

            def body(n, par, prev1, prev2, prev3, cur, nxt, use):
                for g in range(NG):
                    G = NG * n + g
                    if cur:
                        scores(G, g, n, par, not prev1 and g < 2)
                    if g == 7 and prev2:
                        pe.wait_ge(dve_x2, SB * n)
                        ranks(n - 2, Xo)
                    if (cur and g >= 2) or (prev1 and g < 2):
                        prob_columns(G - 2, g % 2, not prev1 and g < 4)
                    if nxt:
                        if g == 2:
                            keys(n + 1, 1 - par, Xp, use)
                        elif g == 4:
                            queries(n + 1, Xp)
                        elif g == 6:
                            pe.wait_ge(act_q32, DC * (n + 2))
                            values(n + 1, 1 - par, Xp)
                    if g == 1 and prev1:
                        project_out(SB * (n - 1), Xo)
                    elif g == 2 and prev2:
                        pe.wait_ge(dve_x2, SB * (n - 1) + 1)
                        x2_columns(n - 2, par, Xo)
                    elif g == 3 and prev2:
                        logits(n - 2, Xo)
                    elif g == 4 and prev1:
                        if prev2:
                            pe.wait_ge(dve_lg, n - 1)
                        else:
                            pe.wait_ge(dve_x2, SB * (n - 1) + 1)
                        output_columns(SB * (n - 1) + 1, Xo)
                    elif g == 5 and prev1:
                        project_out(SB * (n - 1) + 1, Xo)
                    if g == 0 and nxt:
                        input_columns(n + 1, False, not prev1)
                    if cur and g >= 3:
                        weigh_values(G - 3, g - 3, n, par, not prev1 and g < 7)
                    elif prev1 and g < 3:
                        weigh_values(G - 3, NG + g - 3, n - 1, 1 - par, False)
                    if g == 0 and prev1:
                        if prev3:
                            pe.wait_ge(dve_rk, 6 * (n - 3) + 2)
                        elif prev2:
                            pe.wait_ge(dve_x2, SB * (n - 1))
                        else:
                            pe.wait_ge(act_vf, 1)
                        output_columns(SB * (n - 1), Xo)

            pe.wait_ge(ident_ok, 1)
            pe.wait_ge(ld_wk, 16)
            keys(0, 0, K0, 1)
            input_columns(0, True, False)
            pe.wait_ge(ld_wv, 16)
            values(0, 0, Xo)
            pe.wait_ge(ld_wq, 16)
            queries(0, Q0)
            pe.wait_ge(ld_wo, 16)
            pe.wait_ge(ld_b, 16)
            for c in range(DC):
                ins = nc.tensor.matmul(Tb[0][:, 0:D], bqkv[:, 2, c:c + 1].to_broadcast([P, P]), wo[:, c, :], start=(c == 0), stop=(c == DC - 1))
            ins.then_inc(pe_bo, 1)
            pe.wait_ge(const_ok, CONSTS)
            body(0, 0, False, False, False, True, True, 1)
            pe.wait_ge(ld_wr, 16)
            body(1, 1, True, False, False, True, True, 2)
            body(2, 0, True, True, False, True, True, 2)
            body(3, 1, True, True, True, True, True, 3)
            with pe.Fori(2, NSB // 2 - 1) as i:
                body(2 * i, 0, True, True, True, True, True, i + 1)
                body(2 * i + 1, 1, True, True, True, True, True, i + 2)
            body(NSB - 2, 0, True, True, True, True, True, NSB // 2)
            body(NSB - 1, 1, True, True, True, True, False, None)

            first, second = SEQS - 2, SEQS - 1
            G = NG * NSB
            prob_columns(G - 2, 0, False)
            pe.wait_ge(act_vf, NSB)
            output_columns(first, Xp)
            weigh_values(G - 3, NG - 3, NSB - 1, 1, False)
            prob_columns(G - 1, 1, False)
            project_out(first, Xp)
            weigh_values(G - 2, NG - 2, NSB - 1, 1, False)
            pe.wait_ge(dve_rk, 6 * (NSB - 3) + 2)
            x2_columns(NSB - 2, 0, Xo)
            weigh_values(G - 1, NG - 1, NSB - 1, 1, False)
            logits(NSB - 2, Xo)
            pe.wait_ge(dve_x2, first + 1)
            output_columns(second, Xp)
            project_out(second, Xp)
            pe.wait_ge(dve_x2, second + 1)
            x2_columns(NSB - 1, 1, Xp)
            pe.wait_ge(dve_lg, NSB - 1)
            ranks(NSB - 2, Xo)
            logits(NSB - 1, Xp)
            pe.wait_ge(dve_lg, NSB)
            ranks(NSB - 1, Xp)

            pe.wait_ge(dve_idx, NSB)
            nc.tensor.matmul(Xo[:, 0:E], onesb[:, :], seen[:, :], start=True, stop=True).then_inc(pe_cnt, 1)

            def rows_columns(e, par, use, a):
                if a == 0:
                    pe.wait_ge(ld_rows[par], 16 * use)
                c, d = a // 2, a % 2
                o, w = CHUNKS[c]
                if isinstance(e, int) and e == 0 and a < 2:
                    pe.wait_ge(dve_cnt, 1)
                else:
                    pe.wait_ge(dve_bl, 4 * e + a - 1)
                for t in range(w // P):
                    ins = nc.tensor.transpose(Xc[a % 2][:, t * P:(t + 1) * P], rows[par][:, o // P + t, d * P:(d + 1) * P], ident32[:, :])
                ins.then_inc(pe_bT, 1)

            def three(out_ap, parts, start, stop):
                (ah, al), (bh, bl) = parts
                nc.tensor.matmul(out_ap, ah, bh, start=start, stop=False)
                nc.tensor.matmul(out_ap, ah, bl, start=False, stop=False)
                return nc.tensor.matmul(out_ap, al, bh, start=False, stop=stop)

            for a in range(2):
                rows_columns(0, 0, 1, a)

            pe.wait_ge(flag_ok, 1)
            flags = pe.value_load(flag[0:1, 0:1], min_val=0, max_val=2 ** E - 1)

            def up(i, par, c, first):
                e = 2 * i + par
                o, w = CHUNKS[c]
                for f in range(FT):
                    j = c * FT + f
                    if f == 0:
                        pe.wait_ge(dve_bl, 4 * e + 2 * c + 2)
                    if not first or j >= 2:
                        pe.wait_ge(dve_h, 16 * e + j - 1)
                    for half, dst in ((0, Gb), (1, Ub)):
                        fo = half * FF + f * P
                        for d in range(DC):
                            ins = three(dst[j % 2][:, 0:w],
                                        ((Wh[par][:, d, fo:fo + P], Wl[par][:, d, fo:fo + P]),
                                         (bXh[par][:, d, o:o + w], bXl[par][:, d, o:o + w])), d == 0, d == DC - 1)
                    ins.then_inc(pe_gu, 1)

            def down(e, par, c, t, parts):
                o = t * P - CHUNKS[c][0]
                for f in parts:
                    if t in (0, CT0):
                        pe.wait_ge(dve_hl, 16 * e + FT * c + f + 1)
                    ins = three(Yb[(par + t) % 2][:, 0:D],
                                ((hH[c][:, f, o:o + P], hL[c][:, f, o:o + P]),
                                 (Wh[par][:, DC, f * D:(f + 1) * D], Wl[par][:, DC, f * D:(f + 1) * D])), f == 0, f == FT - 1)
                if FT - 1 in parts:
                    ins.then_inc(pe_out, 1)

            def output_bank(e, t, first):
                if not first or t >= 2:
                    pe.wait_ge(dve_ysc, CT * e + t - 1)

            def expert(i, par, last, first):
                e = 2 * i + par
                pe.wait_ge(dve_wl, PIECES * e + 4 * DC)
                up(i, par, 0, first)
                if isinstance(e, int) and e == 0:
                    pe.wait_ge(ld_rows_rest, 16)
                    rows_columns(0, 0, 1, 2)
                    rows_columns(0, 0, 1, 3)
                pe.wait_ge(dve_wl, PIECES * e + PIECES)
                for t in range(2):
                    output_bank(e, t, first)
                    down(e, par, 0, t, range(FT - 1))
                for t in range(2):
                    down(e, par, 0, t, range(FT - 1, FT))
                if not last:
                    rows_columns(e + 1, 1 - par, i + 1 + par, 0)
                    rows_columns(e + 1, 1 - par, i + 1 + par, 1)
                output_bank(e, 2, first)
                down(e, par, 0, 2, range(FT))
                if not last:
                    rows_columns(e + 1, 1 - par, i + 1 + par, 2)
                    rows_columns(e + 1, 1 - par, i + 1 + par, 3)
                with pe.If(more_rows(flags, e)):
                    up(i, par, 1, first)
                    for t in range(CT0, CT):
                        output_bank(e, t, first)
                        down(e, par, 1, t, range(FT))
                with pe.Else():
                    pe.wait_ge(pe_gu, 16 * e + FT).then_inc(pe_gu, FT)
                    pe.wait_ge(pe_out, CT * e + CT0).then_inc(pe_out, CT - CT0)

            expert(0, 0, False, True)
            expert(0, 1, False, False)
            with pe.Fori(1, E // 2 - 1) as i:
                expert(i, 0, False, False)
                expert(i, 1, False, False)
            expert(E // 2 - 1, 0, False, False)
            expert(E // 2 - 1, 1, True, False)


def kernel(**inputs):
    import numpy as _np
    import concourse.bacc as _bacc
    from concourse import mybir as _mybir
    from concourse.bass_utils import run_bass_kernel_spmd as _run

    a = {k: _np.asarray(v) for k, v in inputs.items()}
    flat = a["x"].reshape(TOKENS, D)
    ops = {
        "x": flat,
        "ctxT": a["ctx_1024"].reshape(TOKENS, D).T,
        "gates": _np.concatenate([a["g_xattn"], a["g_ffn"]]),
        "biases": _np.stack([a[f"L0_xattn_b{n}"].reshape(DC, P).T for n in "qkv"], axis=1),
        "wqT": a["L0_xattn_wq"].T, "wkT": a["L0_xattn_wk"].T, "wvT": a["L0_xattn_wv"].T,
        "woT": a["L0_xattn_wo"].T, "bo": a["L0_xattn_bo"],
        "gamma": a["L0_ffn_ln_gamma"], "beta": a["L0_ffn_ln_beta"],
        "wrT": a["L0_ffn_Wr"].T,
        "w12T": a["L0_ffn_W12"].transpose(0, 2, 1),
        "w3T": a["L0_ffn_W3"].transpose(0, 2, 1),
    }
    nc = _bacc.Bacc("TRN2", target_bir_lowering=False, num_devices=1)
    arrays, args = {}, []
    for name, v in ops.items():
        v = _np.ascontiguousarray(v)
        arrays[f"in_{name}"] = v
        args.append(nc.dram_tensor(f"in_{name}", v.shape, _mybir.dt.from_np(v.dtype), kind="ExternalInput").ap())
    args.append(nc.dram_tensor("out_tokens", (TOKENS + P, D), _mybir.dt.float32, kind="ExternalOutput").ap())
    gated_block(nc, *args)
    r = _run(nc, [arrays], core_ids=[0])
    return r.results[0]["out_tokens"][:TOKENS].reshape(SEQS, T, D)
```
